# Optimizing a Trainium2 kernel written in Bass

```python
import numpy as np
import jax
import jax.numpy as jnp

def _softmax(x, axis=-1):
    return jax.nn.softmax(x, axis=axis)

def _gelu(x):
    return jax.nn.gelu(x, approximate=True)

def _silu(x):
    return jax.nn.silu(x)

def _sigmoid(x):
    return jax.nn.sigmoid(x)

def _layernorm(x, axis=-1, eps=1e-05):
    m = jnp.mean(x, axis=axis, keepdims=True)
    v = jnp.var(x, axis=axis, keepdims=True)
    return (x - m) / jnp.sqrt(v + eps)

def _scatter_add(tgt, idx, src, axis=0):
    return tgt.at[idx].add(src)

def _segment_sum(src, seg, n):
    return jax.ops.segment_sum(src, seg, n)
kernel_name = 'mk_cond_seq_d4_seqx_r4_77bd22'

def setup_inputs(seed: int=0):
    np.random.seed(seed)
    _w = jnp.asarray

    def _rec_inputs():
        import jax
        import jax.numpy as jnp
        _rk = jax.random.key(seed)
        x = -0.0003482 + 1 * jax.random.normal(jax.random.fold_in(_rk, 1), (32, 256, 288), jnp.float32)
        _lenS = 256 - jax.random.randint(jax.random.fold_in(_rk, 7), (32,), 0, max(1, 256 // 4) + 1, jnp.int32)
        _lenS2 = 256 - jax.random.randint(jax.random.fold_in(_rk, 8), (32,), 0, max(1, 256 // 4) + 1, jnp.int32)
        cond_1152 = 0.00257642 + 1.0011 * jax.random.normal(jax.random.fold_in(_rk, 11), (32, 288), jnp.float32)
        return (x, cond_1152)
    x, cond_1152 = _rec_inputs()

    def _L0_cond_setup():
        import jax, jax.numpy as jnp
        import numpy as np
        H = 288
        NH = 16
        HD = H // NH
        MLP = int(H * 4.0)
        EPS = 1e-06

        def _ln(z, scale=None):
            m = jnp.mean(z, axis=-1, keepdims=True)
            v = jnp.mean(jnp.square(z - m), axis=-1, keepdims=True)
            y = (z - m) * jax.lax.rsqrt(v + EPS)
            if scale is not None:
                y = y * scale
            return y
        key = jax.random.key(seed)
        ks = jax.random.split(key, 16)
        B, N = (16, 256)
        x = jax.random.normal(ks[0], (B, N, H), dtype=jnp.float32)
        c = jax.random.normal(ks[1], (B, H), dtype=jnp.float32)

        def xav(k, fan_in, fan_out):
            lim = np.sqrt(6.0 / (fan_in + fan_out))
            return jax.random.uniform(k, (fan_in, fan_out), jnp.float32, -lim, lim)
        w_mod = 0.02 * jax.random.normal(ks[2], (H, 6 * H), dtype=jnp.float32)
        b_mod = 0.02 * jax.random.normal(ks[3], (6 * H,), dtype=jnp.float32)
        w_qkv = xav(ks[4], H, 3 * H)
        b_qkv = jnp.zeros((3 * H,), jnp.float32)
        g_q = jnp.ones((HD,), jnp.float32)
        g_k = jnp.ones((HD,), jnp.float32)
        w_proj = xav(ks[5], H, H)
        b_proj = jnp.zeros((H,), jnp.float32)
        w1 = xav(ks[6], H, MLP)
        b1 = jnp.zeros((MLP,), jnp.float32)
        w2 = xav(ks[7], MLP, H)
        b2 = jnp.zeros((H,), jnp.float32)
        return dict(x=x, c=c, w_mod=w_mod, b_mod=b_mod, w_qkv=w_qkv, b_qkv=b_qkv, g_q=g_q, g_k=g_k, w_proj=w_proj, b_proj=b_proj, w1=w1, b1=b1, w2=w2, b2=b2)
    _L0_cond_all = _L0_cond_setup()
    _L0_cond_in = {k: v for k, v in _L0_cond_all.items() if k in ('w_mod', 'b_mod', 'w_qkv', 'b_qkv', 'g_q', 'g_k', 'w_proj', 'b_proj', 'w1', 'b1', 'w2', 'b2')}
    del _L0_cond_all

    def _L1_cond_setup():
        import math
        import jax, jax.numpy as jnp
        import numpy as np
        B, T, D = (8, 256, 288)
        H = 16
        E = 4
        EPS = 1e-06

        def _layer_norm(x):
            mu = jnp.mean(x, axis=-1, keepdims=True)
            var = jnp.mean(jnp.square(x - mu), axis=-1, keepdims=True)
            return (x - mu) * jax.lax.rsqrt(var + EPS)

        def _modulate(x, shift, scale):
            return x * (1.0 + scale) + shift

        def _attention(y, qkv_w, qkv_b, out_w, out_b):
            b, t, d = y.shape
            hd = d // H
            qkv = y @ qkv_w + qkv_b
            q, k, v = jnp.split(qkv, 3, axis=-1)
            q = q.reshape(b, t, H, hd).transpose(0, 2, 1, 3)
            k = k.reshape(b, t, H, hd).transpose(0, 2, 1, 3)
            v = v.reshape(b, t, H, hd).transpose(0, 2, 1, 3)
            scores = jnp.einsum('bhqd,bhkd->bhqk', q, k) / math.sqrt(hd)
            attn = jax.nn.softmax(scores, axis=-1)
            out = jnp.einsum('bhqk,bhkd->bhqd', attn, v)
            out = out.transpose(0, 2, 1, 3).reshape(b, t, d)
            return out @ out_w + out_b
        key = jax.random.key(seed)
        ks = jax.random.split(key, 12)
        std = 0.02
        return {'x': jax.random.normal(ks[0], (B, T, D), dtype=jnp.float32), 'c': jax.random.normal(ks[1], (B, D), dtype=jnp.float32), 'qkv_w': jax.random.normal(ks[2], (D, 3 * D), dtype=jnp.float32) * std, 'qkv_b': jnp.zeros((3 * D,), dtype=jnp.float32), 'out_w': jax.random.normal(ks[3], (D, D), dtype=jnp.float32) * std, 'out_b': jnp.zeros((D,), dtype=jnp.float32), 'w1': jax.random.normal(ks[4], (D, E * D), dtype=jnp.float32) * std, 'b1': jnp.zeros((E * D,), dtype=jnp.float32), 'w2': jax.random.normal(ks[5], (E * D, D), dtype=jnp.float32) * std, 'b2': jnp.zeros((D,), dtype=jnp.float32), 'ada_w': jax.random.normal(ks[6], (D, 6 * D), dtype=jnp.float32) * std, 'ada_b': jnp.zeros((6 * D,), dtype=jnp.float32)}
    _L1_cond_all = _L1_cond_setup()
    _L1_cond_in = {k: v for k, v in _L1_cond_all.items() if k in ('qkv_w', 'qkv_b', 'out_w', 'out_b', 'w1', 'b1', 'w2', 'b2', 'ada_w', 'ada_b')}
    del _L1_cond_all

    def _L2_cond_setup():
        import jax, jax.numpy as jnp
        import numpy as np
        HID = 288
        HEADS = 16
        HD = HID // HEADS
        MLP = int(HID * 4.0)

        def _ln(x, eps, gamma=None, beta=None):
            mu = jnp.mean(x, axis=-1, keepdims=True)
            var = jnp.mean(jnp.square(x - mu), axis=-1, keepdims=True)
            y = (x - mu) / jnp.sqrt(var + eps)
            if gamma is not None:
                y = y * gamma + beta
            return y
        key = jax.random.key(seed)
        ks = jax.random.split(key, 12)
        B, N, C = (8, 256, HID)
        s = lambda k, *sh: jax.random.normal(k, sh, dtype=jnp.float32) * 0.02
        return {'x': jax.random.normal(ks[0], (B, N, C), dtype=jnp.float32), 'c': jax.random.normal(ks[1], (B, C), dtype=jnp.float32), 'w_qkv': s(ks[2], C, 3 * C), 'b_qkv': jnp.zeros((3 * C,), jnp.float32), 'w_proj': s(ks[3], C, C), 'b_proj': jnp.zeros((C,), jnp.float32), 'qn_g': jnp.ones((HD,), jnp.float32), 'qn_b': jnp.zeros((HD,), jnp.float32), 'kn_g': jnp.ones((HD,), jnp.float32), 'kn_b': jnp.zeros((HD,), jnp.float32), 'w1': s(ks[4], C, MLP), 'b1': jnp.zeros((MLP,), jnp.float32), 'w2': s(ks[5], MLP, C), 'b2': jnp.zeros((C,), jnp.float32), 'w_ada': s(ks[6], C, 6 * C), 'b_ada': jnp.zeros((6 * C,), jnp.float32)}
    _L2_cond_all = _L2_cond_setup()
    _L2_cond_in = {k: v for k, v in _L2_cond_all.items() if k in ('w_qkv', 'b_qkv', 'w_proj', 'b_proj', 'qn_g', 'qn_b', 'kn_g', 'kn_b', 'w1', 'b1', 'w2', 'b2', 'w_ada', 'b_ada')}
    del _L2_cond_all

    def _L3_cond_setup():
        import jax, jax.numpy as jnp
        import numpy as np
        from jax.scipy.linalg import expm
        N, D, COND_DIM = (288, 64, 288)
        B, T = (16, 256)

        def _rotation(cond, W, b):
            v = jax.nn.silu(cond) @ W.T + b
            iu, ju = jnp.triu_indices(D, k=1)
            A = jnp.zeros((cond.shape[0], D, D), dtype=v.dtype)
            A = A.at[:, iu, ju].set(v).at[:, ju, iu].set(-v)
            return expm(A)
        key = jax.random.key(seed)
        k1, k2, k3, k4, k5 = jax.random.split(key, 5)
        x = jax.random.normal(k1, (B, T, N), dtype=jnp.float32)
        cond = jax.random.normal(k2, (B, COND_DIM), dtype=jnp.float32)
        P = jax.random.normal(k3, (N, D), dtype=jnp.float32)
        n_skew = D * (D - 1) // 2
        bound = 1.0 / np.sqrt(COND_DIM)
        W = jax.random.uniform(k4, (n_skew, COND_DIM), minval=-bound, maxval=bound, dtype=jnp.float32)
        b = jax.random.uniform(k5, (n_skew,), minval=-bound, maxval=bound, dtype=jnp.float32)
        return {'x': x, 'cond': cond, 'P': P, 'W': W, 'b': b}
    _L3_cond_all = _L3_cond_setup()
    _L3_cond_in = {k: v for k, v in _L3_cond_all.items() if k in ('P', 'W', 'b')}
    del _L3_cond_all
    return {'x': x, 'cond_1152': cond_1152, 'L0_cond_w_mod': _L0_cond_in['w_mod'], 'L0_cond_b_mod': _L0_cond_in['b_mod'], 'L0_cond_w_qkv': _L0_cond_in['w_qkv'], 'L0_cond_b_qkv': _L0_cond_in['b_qkv'], 'L0_cond_g_q': _L0_cond_in['g_q'], 'L0_cond_g_k': _L0_cond_in['g_k'], 'L0_cond_w_proj': _L0_cond_in['w_proj'], 'L0_cond_b_proj': _L0_cond_in['b_proj'], 'L0_cond_w1': _L0_cond_in['w1'], 'L0_cond_b1': _L0_cond_in['b1'], 'L0_cond_w2': _L0_cond_in['w2'], 'L0_cond_b2': _L0_cond_in['b2'], 'L1_cond_qkv_w': _L1_cond_in['qkv_w'], 'L1_cond_qkv_b': _L1_cond_in['qkv_b'], 'L1_cond_out_w': _L1_cond_in['out_w'], 'L1_cond_out_b': _L1_cond_in['out_b'], 'L1_cond_w1': _L1_cond_in['w1'], 'L1_cond_b1': _L1_cond_in['b1'], 'L1_cond_w2': _L1_cond_in['w2'], 'L1_cond_b2': _L1_cond_in['b2'], 'L1_cond_ada_w': _L1_cond_in['ada_w'], 'L1_cond_ada_b': _L1_cond_in['ada_b'], 'L2_cond_w_qkv': _L2_cond_in['w_qkv'], 'L2_cond_b_qkv': _L2_cond_in['b_qkv'], 'L2_cond_w_proj': _L2_cond_in['w_proj'], 'L2_cond_b_proj': _L2_cond_in['b_proj'], 'L2_cond_qn_g': _L2_cond_in['qn_g'], 'L2_cond_qn_b': _L2_cond_in['qn_b'], 'L2_cond_kn_g': _L2_cond_in['kn_g'], 'L2_cond_kn_b': _L2_cond_in['kn_b'], 'L2_cond_w1': _L2_cond_in['w1'], 'L2_cond_b1': _L2_cond_in['b1'], 'L2_cond_w2': _L2_cond_in['w2'], 'L2_cond_b2': _L2_cond_in['b2'], 'L2_cond_w_ada': _L2_cond_in['w_ada'], 'L2_cond_b_ada': _L2_cond_in['b_ada'], 'L3_cond_P': _L3_cond_in['P'], 'L3_cond_W': _L3_cond_in['W'], 'L3_cond_b': _L3_cond_in['b']}

def reference(x, cond_1152, L0_cond_w_mod, L0_cond_b_mod, L0_cond_w_qkv, L0_cond_b_qkv, L0_cond_g_q, L0_cond_g_k, L0_cond_w_proj, L0_cond_b_proj, L0_cond_w1, L0_cond_b1, L0_cond_w2, L0_cond_b2, L1_cond_qkv_w, L1_cond_qkv_b, L1_cond_out_w, L1_cond_out_b, L1_cond_w1, L1_cond_b1, L1_cond_w2, L1_cond_b2, L1_cond_ada_w, L1_cond_ada_b, L2_cond_w_qkv, L2_cond_b_qkv, L2_cond_w_proj, L2_cond_b_proj, L2_cond_qn_g, L2_cond_qn_b, L2_cond_kn_g, L2_cond_kn_b, L2_cond_w1, L2_cond_b1, L2_cond_w2, L2_cond_b2, L2_cond_w_ada, L2_cond_b_ada, L3_cond_P, L3_cond_W, L3_cond_b):
    import jax
    import jax.numpy as jnp

    def _L0_cond_ref(x, c, w_mod, b_mod, w_qkv, b_qkv, g_q, g_k, w_proj, b_proj, w1, b1, w2, b2):
        import jax, jax.numpy as jnp
        import numpy as np
        H = 288
        NH = 16
        HD = H // NH
        MLP = int(H * 4.0)
        EPS = 1e-06

        def _ln(z, scale=None):
            m = jnp.mean(z, axis=-1, keepdims=True)
            v = jnp.mean(jnp.square(z - m), axis=-1, keepdims=True)
            y = (z - m) * jax.lax.rsqrt(v + EPS)
            if scale is not None:
                y = y * scale
            return y
        B, N, _ = x.shape
        mod = jax.nn.swish(c) @ w_mod + b_mod
        sh_msa, sc_msa, g_msa, sh_mlp, sc_mlp, g_mlp = jnp.split(mod, 6, axis=1)
        xn = _ln(x) * (1 + sc_msa[:, None, :]) + sh_msa[:, None, :]
        qkv = xn @ w_qkv + b_qkv
        qkv = qkv.reshape(B, N, 3, NH, HD).transpose(2, 0, 3, 1, 4)
        q, k, v = (qkv[0], qkv[1], qkv[2])
        q = _ln(q, g_q)
        k = _ln(k, g_k)
        attn = jax.nn.softmax(jnp.einsum('bhqd,bhkd->bhqk', q, k) * HD ** (-0.5), axis=-1)
        o = jnp.einsum('bhqk,bhkd->bhqd', attn, v)
        o = o.transpose(0, 2, 1, 3).reshape(B, N, H) @ w_proj + b_proj
        x = x + g_msa[:, None, :] * o
        xn2 = _ln(x) * (1 + sc_mlp[:, None, :]) + sh_mlp[:, None, :]
        h = jax.nn.gelu(xn2 @ w1 + b1, approximate=True)
        x = x + g_mlp[:, None, :] * (h @ w2 + b2)
        return x

    def _L1_cond_ref(x, c, qkv_w, qkv_b, out_w, out_b, w1, b1, w2, b2, ada_w, ada_b):
        import math
        import jax, jax.numpy as jnp
        import numpy as np
        B, T, D = (8, 256, 288)
        H = 16
        E = 4
        EPS = 1e-06

        def _layer_norm(x):
            mu = jnp.mean(x, axis=-1, keepdims=True)
            var = jnp.mean(jnp.square(x - mu), axis=-1, keepdims=True)
            return (x - mu) * jax.lax.rsqrt(var + EPS)

        def _modulate(x, shift, scale):
            return x * (1.0 + scale) + shift

        def _attention(y, qkv_w, qkv_b, out_w, out_b):
            b, t, d = y.shape
            hd = d // H
            qkv = y @ qkv_w + qkv_b
            q, k, v = jnp.split(qkv, 3, axis=-1)
            q = q.reshape(b, t, H, hd).transpose(0, 2, 1, 3)
            k = k.reshape(b, t, H, hd).transpose(0, 2, 1, 3)
            v = v.reshape(b, t, H, hd).transpose(0, 2, 1, 3)
            scores = jnp.einsum('bhqd,bhkd->bhqk', q, k) / math.sqrt(hd)
            attn = jax.nn.softmax(scores, axis=-1)
            out = jnp.einsum('bhqk,bhkd->bhqd', attn, v)
            out = out.transpose(0, 2, 1, 3).reshape(b, t, d)
            return out @ out_w + out_b
        mods = (jax.nn.silu(c) @ ada_w + ada_b)[:, None, :]
        m0, m1, m2, m3, m4, m5 = jnp.split(mods, 6, axis=-1)
        y = _modulate(_layer_norm(x), m0, m1)
        x = x + m2 * _attention(y, qkv_w, qkv_b, out_w, out_b)
        y = _modulate(_layer_norm(x), m3, m4)
        y = jax.nn.gelu(y @ w1 + b1, approximate=True)
        x = x + m5 * (y @ w2 + b2)
        return x

    def _L2_cond_ref(x, c, w_qkv, b_qkv, w_proj, b_proj, qn_g, qn_b, kn_g, kn_b, w1, b1, w2, b2, w_ada, b_ada):
        import jax, jax.numpy as jnp
        import numpy as np
        HID = 288
        HEADS = 16
        HD = HID // HEADS
        MLP = int(HID * 4.0)

        def _ln(x, eps, gamma=None, beta=None):
            mu = jnp.mean(x, axis=-1, keepdims=True)
            var = jnp.mean(jnp.square(x - mu), axis=-1, keepdims=True)
            y = (x - mu) / jnp.sqrt(var + eps)
            if gamma is not None:
                y = y * gamma + beta
            return y
        B, N, C = x.shape
        H, hd = (HEADS, HD)
        scale = hd ** (-0.5)
        mod = jax.nn.silu(c) @ w_ada + b_ada
        sh_msa, sc_msa, g_msa, sh_mlp, sc_mlp, g_mlp = jnp.split(mod, 6, axis=1)
        xn = _ln(x, 1e-06)
        xn = xn * (1 + sc_msa[:, None, :]) + sh_msa[:, None, :]
        qkv = (xn @ w_qkv + b_qkv).reshape(B, N, 3, H, hd)
        q, k, v = (qkv[:, :, 0], qkv[:, :, 1], qkv[:, :, 2])
        q = _ln(q, 1e-05, qn_g, qn_b)
        k = _ln(k, 1e-05, kn_g, kn_b)
        attn = jnp.einsum('bqhd,bkhd->bhqk', q, k) * scale
        attn = jax.nn.softmax(attn, axis=-1)
        o = jnp.einsum('bhqk,bkhd->bqhd', attn, v).reshape(B, N, C)
        o = o @ w_proj + b_proj
        x = x + g_msa[:, None, :] * o
        xn2 = _ln(x, 1e-06)
        xn2 = xn2 * (1 + sc_mlp[:, None, :]) + sh_mlp[:, None, :]
        h = jax.nn.gelu(xn2 @ w1 + b1, approximate=False)
        m = h @ w2 + b2
        x = x + g_mlp[:, None, :] * m
        return x

    def _L3_cond_ref(x, cond, P, W, b):
        import jax, jax.numpy as jnp
        import numpy as np
        from jax.scipy.linalg import expm
        N, D, COND_DIM = (288, 64, 288)
        B, T = (16, 256)

        def _rotation(cond, W, b):
            v = jax.nn.silu(cond) @ W.T + b
            iu, ju = jnp.triu_indices(D, k=1)
            A = jnp.zeros((cond.shape[0], D, D), dtype=v.dtype)
            A = A.at[:, iu, ju].set(v).at[:, ju, iu].set(-v)
            return expm(A)
        U, _ = jnp.linalg.qr(P)
        R = _rotation(cond, W, b)
        z = jnp.einsum('btn,nd->btd', x, U)
        z_rot = jnp.einsum('btd,bde->bte', z, R)
        x_rot = x + jnp.einsum('btd,nd->btn', z_rot - z, U)
        return x_rot
    x = _L0_cond_ref(x, cond_1152, L0_cond_w_mod, L0_cond_b_mod, L0_cond_w_qkv, L0_cond_b_qkv, L0_cond_g_q, L0_cond_g_k, L0_cond_w_proj, L0_cond_b_proj, L0_cond_w1, L0_cond_b1, L0_cond_w2, L0_cond_b2)
    x = _L1_cond_ref(x, cond_1152, L1_cond_qkv_w, L1_cond_qkv_b, L1_cond_out_w, L1_cond_out_b, L1_cond_w1, L1_cond_b1, L1_cond_w2, L1_cond_b2, L1_cond_ada_w, L1_cond_ada_b)
    x = _L2_cond_ref(x, cond_1152, L2_cond_w_qkv, L2_cond_b_qkv, L2_cond_w_proj, L2_cond_b_proj, L2_cond_qn_g, L2_cond_qn_b, L2_cond_kn_g, L2_cond_kn_b, L2_cond_w1, L2_cond_b1, L2_cond_w2, L2_cond_b2, L2_cond_w_ada, L2_cond_b_ada)
    x = _L3_cond_ref(x, cond_1152, L3_cond_P, L3_cond_W, L3_cond_b)
    return x

_drawn_inputs = setup_inputs


def setup_inputs(seed=0):
    import zlib

    import numpy as np

    out = dict(_drawn_inputs(seed))
    spreads = {'L0_cond_b_qkv': (0.0, 0.374),
     'L0_cond_g_q': (1.0, 0.6),
     'L0_cond_g_k': (1.0, 0.6),
     'L0_cond_b_proj': (0.0, 0.384),
     'L0_cond_b1': (0.0, 0.51),
     'L0_cond_b2': (0.0, 0.423),
     'L1_cond_qkv_b': (0.0, 0.8),
     'L1_cond_out_b': (0.0, 0.391),
     'L1_cond_b1': (0.0, 0.8),
     'L1_cond_b2': (0.0, 0.368),
     'L1_cond_ada_b': (0.0, 0.415),
     'L2_cond_b_qkv': (0.0, 0.8),
     'L2_cond_b_proj': (0.0, 0.339),
     'L2_cond_qn_g': (1.0, 0.6),
     'L2_cond_qn_b': (0.0, 0.8),
     'L2_cond_kn_g': (1.0, 0.6),
     'L2_cond_kn_b': (0.0, 0.8),
     'L2_cond_b1': (0.0, 0.8),
     'L2_cond_b2': (0.0, 0.36),
     'L2_cond_b_ada': (0.0, 0.382)}
    factors = {'L0_cond_b_mod': 5.125,
     'L1_cond_qkv_w': 8.0,
     'L1_cond_out_w': 6.121,
     'L2_cond_w_qkv': 8.0,
     'L2_cond_w_proj': 5.322}
    for name, (base, spread) in spreads.items():
        noise = np.random.default_rng([zlib.crc32(name.encode()), seed]).standard_normal(out[name].shape)
        drawn = base * np.exp(spread * noise) if base else spread * noise
        out[name] = jnp.asarray(drawn.astype(out[name].dtype))
    for name, factor in factors.items():
        out[name] = (out[name] * factor).astype(out[name].dtype)
    return out
```

```python
from contextlib import ExitStack

import numpy as np

import concourse.bass as bass
from concourse import mybir

F32 = mybir.dt.float32
F32R = mybir.dt.float32r
I32 = mybir.dt.int32
ALU = mybir.AluOpType
ACT = mybir.ActivationFunctionType
AX = mybir.AxisListType

B, T, D = 32, 256, 288
H, HD = 16, 18
F = 4 * D
LAYERS = 3
P = 128
NT = T // P
KC, KP = 3, 96
FM = F // P
PAIRS = H // 2
SLOT = 64
ROT = 64
SQUARINGS, TAYLOR = 9, 6
NEWTON_MAGIC = 0x5F3759DF
QK_EPS = (1e-6, None, 1e-5)

PER_RUN = dict(
    a_x=16, a_g=16, a_st=1, a_ve=1, a_rs=1, a_xn=2, a_xT=2, a_xf=3, a_xh=1, a_xl=1, a_qkv=6, a_qkvd=6,
    a_c=1, a_sq=1, a_nrm=1, a_qs=1, a_kh=1, a_kl=1, a_T=8, a_qT=4, a_kA=4, a_kB=4, a_S=16, a_mx=8,
    a_nm=1, a_T2=4, a_q2a=2, a_q2d=2, a_ex=8, a_pv=8, a_o=2, a_oT=2, a_on=2, a_nT=2, a_oh=2, a_ol=2,
    a_pr=2, a_gb=1, a_xa=1, a_x1=2,
    m_g=16, m_st=1, m_ve=1, m_rs=1, m_xn=2, m_gb=1, m_xb=1, m_xT=2, m_xf=3, m_xh=1, m_xl=1, m_h=5,
    m_hf=5, m_hh=5, m_hl=5, m_y=2, m_x2=2, m_out=16, m_mod=1, a_mod=1,
    r_e=16, r_T=2, r_x=2, r_z=1, r_zs=1, r_y=1, r_ys=1, r_o=2, r_x3=2,
)


def upto(name, run, k):
    return run * PER_RUN[name] + k


def build(nc, t):
    with ExitStack() as ctx:
        def sb(name, shape, dt=F32, at=ctx):
            return at.enter_context(nc.sbuf_tensor(name, shape, dt))

        def ps(name, shape):
            return ctx.enter_context(nc.psum_tensor(name, shape, F32))

        def sem(name):
            return ctx.enter_context(nc.semaphore(name))

        s = {name: sem(name) for name in PER_RUN}

        def wait(eng, name, run, k):
            value = upto(name, run, k)
            if not (isinstance(value, int) and value <= 0):
                eng.wait_ge(s[name], value)

        S = ps("S", [P, 4, 512])
        ABANK = [ps("A0", [P, 512]), ps("A1", [P, 512])]
        MBANK = [ps("M0", [P, 512]), ps("M1", [P, 512])]

        ident = sb("ident", [P, P])
        modT = sb("modT", [KP, LAYERS, 12, B])
        U = sb("U", [KP, KC, ROT])
        UT = sb("UT", [ROT, D])
        mhalf = sb("mhalf", [P, 2])

        gates = nc.dram_tensor("gates", (LAYERS, B, 2 * D), F32, kind="Internal").ap()
        expm = nc.dram_tensor("expm", (B, ROT, ROT), F32, kind="Internal").ap()
        mid = [nc.dram_tensor(f"mid{i}", (B, T, D), F32, kind="Internal").ap() for i in range(2)]

        preamble(nc, t, sem, S, ABANK, MBANK, ident, modT, U, UT, mhalf, gates, expm)

        wqkv = [sb(f"wqkv_{h}", [KP, KC, 3 * D], F32R) for h in ("hi", "lo")]
        wo = [sb(f"wo_{h}", [KP, KC, D], F32R) for h in ("hi", "lo")]
        w1 = [sb(f"w1_{h}", [KP, KC, F], F32R) for h in ("hi", "lo")]
        w2 = [sb(f"w2_{h}", [P, FM, D], F32R) for h in ("hi", "lo")]
        bqkv = sb("bqkv", [P, 3 * D])
        gam = sb("gam", [P, 2 * HD])
        bet = sb("bet", [P, 2 * HD])
        bo = sb("bo", [P, D])
        b2 = sb("b2", [P, D])
        b1T = sb("b1T", [P, FM])
        xld = sb("xld", [P, NT, D])
        xa = sb("xa", [P, NT, D])
        xn = sb("xn", [P, NT, D])
        gA = sb("gA", [P, D])
        gbA = sb("gbA", [P, D])
        amod = sb("amod", [KP, 6])
        oraw = sb("oraw", [P, 4, T])
        xf = oraw[0:KP, 0:3, :]
        xh = sb("xh", [KP, KC, T], F32R)
        xl = sb("xl", [KP, KC, T], F32R)
        qs = sb("qs", [P, NT, H, SLOT], F32R)
        ks = sb("ks", [P, NT, H, SLOT], F32R)
        V = sb("V", [P, NT, H, 32])
        qT = sb("qT", [P, PAIRS, T], F32R)
        kz = [sb(f"kz{a}", [P, PAIRS, T], F32R) for a in range(2)]
        pT = sb("pT", [P, 3, 2, 512])
        flat = pT[:, :, :, :].rearrange("p s a c -> p (s a c)")
        qk = flat[:, 0:NT * 2 * D].rearrange("p (t c) -> p t c", t=NT)
        sq = flat[:, NT * 2 * D:2 * NT * 2 * D]
        wst = flat[:, 0:2 * F].rearrange("p (r c) -> p r c", r=2)
        mx = sb("mx", [P, PAIRS, 2, NT])
        nmx = sb("nmx", [P, PAIRS, 2, NT])
        stA = sb("stA", [P, NT, 6])
        mvA = sb("mvA", [P, NT, 2])
        rsA = sb("rsA", [P, NT])
        veA = sb("veA", [P, NT])
        sm = sb("sm", [P, 64])
        nv = sb("nv", [P, 64])
        na = sb("na", [P, 64])
        ny = sb("ny", [P, 64])
        rden = sb("rden", [P, NT, H])
        x1 = sb("x1", [P, NT, D])
        xb = sb("xb", [P, NT, D])
        xo = sb("xo", [P, NT, D])
        gM = sb("gM", [P, D])
        gbM = sb("gbM", [P, D])
        mmod = sb("mmod", [KP, 6])
        hf = sb("hf", [P, 2, 512])
        xf2 = hf[0:KP, :, :].rearrange("p r c -> p (r c)")[:, 0:KC * T].rearrange("p (c n) -> p c n", c=KC)
        xh2 = sb("xh2", [KP, KC, T], F32R)
        xl2 = sb("xl2", [KP, KC, T], F32R)
        hh = sb("hh", [P, FM, T], F32R)
        hl = sb("hl", [P, FM, T], F32R)
        stM = sb("stM", [P, NT, 6])
        mvM = sb("mvM", [P, NT, 2])
        rsM = sb("rsM", [P, NT])
        veM = sb("veM", [P, NT])
        eb = sb("eb", [ROT, ROT])
        zT = sb("zT", [ROT, T])
        yT = sb("yT", [ROT, T])

        w_in = [sem("w_in0"), sem("w_in1")]
        w_hi = sem("w_hi")
        w_lo = sem("w_lo")
        p_in = sem("p_in")
        set_done = sem("set_done")
        dve_step = sem("dve_step")

        def chunks(layer):
            w = t[layer]
            out = [(w["wqkv"].rearrange("(k p) n -> p k n", p=KP)[:, k, :], KP, 3 * D,
                    [x[:, k, :] for x in wqkv]) for k in range(KC)]
            out += [(w["wo"].rearrange("(k p) n -> p k n", p=KP)[:, k, :], KP, D,
                     [x[:, k, :] for x in wo]) for k in range(KC)]
            out += [(w["w1"].rearrange("(k p) n -> p k n", p=KP)[:, k, :], KP, F,
                     [x[:, k, :] for x in w1]) for k in range(KC)]
            out += [(w["w2"].rearrange("(k p) n -> p k n", p=P)[:, 3 * k:3 * k + 3, :], P, 3 * D,
                     [x[:, 3 * k:3 * k + 3, :].rearrange("p k n -> p (k n)") for x in w2]) for k in range(FM // 3)]
            return out

        NCH = 4 * KC
        NPAR = [7, 5, 7]
        PAR_SUM = [0, 7, 12, 19]

        def constant_wait(eng):
            eng.nop(nofuse=True)

        steps = [0]

        for layer in range(LAYERS):
            first, last = layer * B, layer * B + B
            src = t["x"] if layer == 0 else mid[layer - 1]
            dst = t["out"] if layer == LAYERS - 1 else mid[layer]
            start = first + (1 if layer == 1 else 2)
            rot = layer == LAYERS - 1
            eps = QK_EPS[layer]
            w = t[layer]

            def qk_run(n):
                return n - B if layer == 2 else n

            def wait_normed(eng, n):
                if eps is None:
                    wait(eng, "a_qkvd", n, 6)
                else:
                    wait(eng, "a_nrm", qk_run(n), 1)

            with ExitStack() as lc:
                block = lc.enter_context(nc.Block())

                @block.sync
                def _(sp):
                    for c, (ap, rows, cols, _) in enumerate(chunks(layer)):
                        n = layer * NCH + c
                        if c >= 2:
                            sp.wait_ge(w_lo, n - 1)
                        to = wst[0:rows, c % 2, 0:cols]
                        if len(ap.shape) == 3:
                            to = to.rearrange("p (k n) -> p k n", k=ap.shape[1])
                        sp.dma_start(to, ap).then_inc(w_in[c % 2], 16)

                    def load_x(n):
                        wait(sp, "a_xn", n, 0)
                        wait(sp, "a_xa", n, 0)
                        sp.dma_start(xld[:, :, :], src[n - first].rearrange("(t p) d -> p t d", p=P)).then_inc(s["a_x"], 16)

                    def load_gA(n):
                        wait(sp, "a_x1", n, 0)
                        sp.dma_start(gA[:, :], gates[layer, n - first, 0:D].partition_broadcast(P)).then_inc(s["a_g"], 16)

                    def load_gM(n):
                        wait(sp, "m_x2", n, 0)
                        sp.dma_start(gM[:, :], gates[layer, n - first, D:2 * D].partition_broadcast(P)).then_inc(s["m_g"], 16)
                        if rot:
                            wait(sp, "r_y", n - first, 0)
                            sp.dma_start(eb[:, :], expm[n - first]).then_inc(s["r_e"], 16)

                    def store(n):
                        if rot:
                            wait(sp, "r_x3", n - first, 2)
                        else:
                            wait(sp, "m_x2", n, 2)
                        sp.dma_start(dst[n - first].rearrange("(t p) d -> p t d", p=P), xo[:, :, :]).then_inc(s["m_out"], 16)

                    def slot(n):
                        load_x(n)
                        load_gM(n - 1)
                        load_gA(n)
                        store(n - 1)

                    load_x(first)
                    load_gA(first)
                    if start > first + 1:
                        slot(first + 1)
                    with sp.Fori(start, last) as n:
                        slot(n)
                    load_gM(last - 1)
                    store(last - 1)
                    sp.wait_ge(s["m_out"], upto("m_out", last, 0))

                @block.gpsimd
                def _(pool):
                    if layer == 0:
                        pool.memset(qs[:, :, :, :].bitcast(F32), 0.0).then_inc(set_done, 1)
                        pool.memset(ks[:, :, :, :].bitcast(F32), 0.0).then_inc(set_done, 1)
                        pool.memset(V[:, :, :, :], 0.0).then_inc(set_done, 1)
                        for a in range(2):
                            pool.memset(kz[a][:, :, :].bitcast(F32), 0.0).then_inc(set_done, 1)
                        pool.wait_ge(set_done, 5)
                        pool.memset(ks[:, :, :, 0:2].bitcast(F32), 1.0).then_inc(set_done, 1)
                        pool.memset(V[:, :, :, 0:1], 1.0).then_inc(set_done, 1)
                    for to, ap in ((bqkv[:, :], w["bqkv"].partition_broadcast(P)), (bo[:, :], w["bo"].partition_broadcast(P)),
                                   (b2[:, :], w["b2"].partition_broadcast(P)), (b1T[:, :], w["b1T"])):
                        pool.dma_start(to, ap).then_inc(p_in, 16)
                    n_par = 4
                    if eps is not None:
                        pool.dma_start(gam[:, 0:HD], w["gq"].partition_broadcast(P)).then_inc(p_in, 16)
                        pool.dma_start(gam[:, HD:2 * HD], w["gk"].partition_broadcast(P)).then_inc(p_in, 16)
                        n_par += 2
                    if rot:
                        pool.dma_start(bet[:, 0:HD], w["bq"].partition_broadcast(P)).then_inc(p_in, 16)
                        pool.dma_start(bet[:, HD:2 * HD], w["bk"].partition_broadcast(P)).then_inc(p_in, 16)
                        n_par += 2
                    par = [6, 10, 18][layer]
                    assert par == [0, 6, 10][layer] + n_par
                    pool.wait_ge(p_in, 16 * par)

                    def A_mod(n):
                        wait(pool, "a_xf", n, 0)
                        pool.tensor_copy(amod[:, :], modT[:, layer, 0:6, bass.ds(n - first, 1)].rearrange("p c b -> p (c b)")).then_inc(s["a_mod"], 1)

                    def M_mod(n):
                        wait(pool, "m_xf", n, 0)
                        pool.tensor_copy(mmod[:, :], modT[:, layer, 6:12, bass.ds(n - first, 1)].rearrange("p c b -> p (c b)")).then_inc(s["m_mod"], 1)

                    def A_rstd(n):
                        wait(pool, "a_st", n, 1)
                        wait(pool, "a_xn", n, 0)
                        constant_wait(pool)
                        pool.tensor_scalar(veA[:, :], mvA[:, :, 1], 1.0, 1e-6, ALU.mult, ALU.add).then_inc(s["a_ve"], 1)
                        wait(pool, "a_ve", n, 1)
                        pool.tensor_tensor(rsA[:, :], veA[:, :], mhalf[:, :], ALU.pow).then_inc(s["a_rs"], 1)

                    def M_rstd(n):
                        wait(pool, "m_st", n, 1)
                        wait(pool, "m_xn", n, 0)
                        constant_wait(pool)
                        pool.tensor_scalar(veM[:, :], mvM[:, :, 1], 1.0, 1e-6, ALU.mult, ALU.add).then_inc(s["m_ve"], 1)
                        wait(pool, "m_ve", n, 1)
                        pool.tensor_tensor(rsM[:, :], veM[:, :], mhalf[:, :], ALU.pow).then_inc(s["m_rs"], 1)

                    def A_xh(n):
                        wait(pool, "a_xf", n, 3)
                        wait(pool, "a_pr", n, 0)
                        constant_wait(pool)
                        pool.tensor_scalar(xh[:, :, :], xf, 1.0, 0.0, ALU.mult, ALU.add).then_inc(s["a_xh"], 1)

                    def M_xh(n):
                        wait(pool, "m_xf", n, 3)
                        wait(pool, "m_h", n, 0)
                        constant_wait(pool)
                        pool.tensor_scalar(xh2[:, :, :], xf2, 1.0, 0.0, ALU.mult, ALU.add).then_inc(s["m_xh"], 1)

                    def A_residual(n):
                        wait(pool, "a_g", n, 16)
                        wait(pool, "a_x", n, 16)
                        wait(pool, "a_x1", n, 0)
                        pool.tensor_tensor(gbA[:, :], gA[:, :], bo[:, :], ALU.mult).then_inc(s["a_gb"], 1)
                        wait(pool, "a_gb", n, 1)
                        pool.tensor_tensor(xa[:, :, :], xld[:, :, :], gbA[:, :].unsqueeze(1).broadcast_to([P, NT, D]), ALU.add).then_inc(s["a_xa"], 1)

                    def M_residual(n):
                        wait(pool, "m_g", n, 16)
                        wait(pool, "m_x2", n, 0)
                        wait(pool, "a_x1", n, 2)
                        pool.tensor_tensor(gbM[:, :], gM[:, :], b2[:, :], ALU.mult).then_inc(s["m_gb"], 1)
                        wait(pool, "m_gb", n, 1)
                        pool.tensor_tensor(xb[:, :, :], x1[:, :, :], gbM[:, :].unsqueeze(1).broadcast_to([P, NT, D]), ALU.add).then_inc(s["m_xb"], 1)

                    def A_klo(n):
                        wait_normed(pool, n)
                        wait(pool, "a_kh", n, 1)
                        for i in range(NT):
                            op = pool.tensor_tensor(
                                ks[:, i, :, 2 + HD:2 + 2 * HD], qk[:, i, D:2 * D].rearrange("p (h d) -> p h d", h=H),
                                ks[:, i, :, 2:2 + HD].bitcast(F32), ALU.subtract)
                        op.then_inc(s["a_kl"], 1)

                    def M_hh(n, f):
                        wait(pool, "m_hf", n, f + 1)
                        wait(pool, "m_y", n, 0)
                        m = min(2, FM - 2 * f)
                        constant_wait(pool)
                        pool.tensor_scalar(hh[:, 2 * f:2 * f + m, :].rearrange("p m c -> p (m c)"), hf[:, f % 2, 0:m * T],
                                           1.0, 0.0, ALU.mult, ALU.add).then_inc(s["m_hh"], 1)

                    def slot(a, m):
                        if a is not None:
                            A_mod(a)
                            A_rstd(a)
                        if m is not None:
                            M_mod(m)
                            M_rstd(m)
                        if a is not None:
                            A_xh(a)
                        if m is not None:
                            M_xh(m)
                            M_residual(m)
                            for f in range(3):
                                M_hh(m, f)
                        if m is not None:
                            M_hh(m, 3)
                            M_hh(m, 4)
                        if a is not None:
                            A_klo(a)
                            A_residual(a)

                    slot(first, None)
                    if start > first + 1:
                        slot(first + 1, first)
                    with pool.Fori(start, last) as n:
                        slot(n, n - 1)
                    slot(None, last - 1)

                @block.scalar
                def _(act):
                    for c, (_, rows, cols, to) in enumerate(chunks(layer)):
                        act.wait_ge(w_in[c % 2], 16 * (layer * NCH // 2 + c // 2 + 1))
                        act.activation(to[0], wst[0:rows, c % 2, 0:cols], ACT.Identity).then_inc(w_hi, 1)
                    act.wait_ge(p_in, 16 * [6, 10, 18][layer])

                    def A_xf(n):
                        wait(act, "a_mod", n, 1)
                        wait(act, "a_oT", n, 0)
                        for c in range(KC):
                            if c != 1:
                                wait(act, "a_xT", n, c // 2 + 1)
                            act.activation(xf[:, c, :], ABANK[c // 2][0:KP, (c % 2) * T:(c % 2 + 1) * T], ACT.Identity,
                                           bias=amod[:, c:c + 1], scale=amod[:, 3 + c:4 + c]).then_inc(s["a_xf"], 1)

                    def M_xf(n):
                        wait(act, "m_mod", n, 1)
                        wait(act, "m_hl", n, 0)
                        for c in range(KC):
                            if c != 1:
                                wait(act, "m_xT", n, c // 2 + 1)
                            act.activation(xf2[:, c, :], MBANK[c // 2][0:KP, (c % 2) * T:(c % 2 + 1) * T], ACT.Identity,
                                           bias=mmod[:, c:c + 1], scale=mmod[:, 3 + c:4 + c]).then_inc(s["m_xf"], 1)

                    def M_gelu(n, f):
                        wait(act, "m_h", n, f + 1)
                        if f == 0:
                            wait(act, "m_xl", n, 1)
                        if f >= 2:
                            wait(act, "m_hl", n, f - 1)
                        for i in range(min(2, FM - 2 * f)):
                            op = act.activation(hf[:, f % 2, i * T:(i + 1) * T], MBANK[f % 2][:, i * T:(i + 1) * T],
                                                ACT.Gelu if rot else ACT.Gelu_apprx_tanh, bias=b1T[:, 2 * f + i:2 * f + i + 1])
                        op.then_inc(s["m_hf"], 1)

                    def A_square(n):
                        wait(act, "a_c", qk_run(n), 1)
                        act.activation(sq, qk.rearrange("p t c -> p (t c)"), ACT.Square).then_inc(s["a_sq"], 1)

                    def A_khi(n):
                        wait_normed(act, n)
                        wait(act, "a_T", n, 0)
                        for i in range(NT):
                            kv = qk[:, i, D:2 * D].rearrange("p (h d) -> p h d", h=H)
                            act.activation(ks[:, i, :, 2:2 + HD], kv, ACT.Identity)
                            op = act.activation(ks[:, i, :, 2 + 2 * HD:2 + 3 * HD], kv, ACT.Identity)
                        op.then_inc(s["a_kh"], 1)

                    def A_turned(n, f):
                        if f == 0:
                            wait(act, "a_S", n, 0)
                        wait(act, "a_T", n, 2 * f + 1)
                        act.activation(qT[:, 2 * f:2 * f + 2, :].rearrange("p m c -> p (m c)"), ABANK[0][:, :], ACT.Identity).then_inc(s["a_qT"], 1)
                        wait(act, "a_T", n, 2 * f + 2)
                        act.activation(kz[0][0:SLOT, 2 * f:2 * f + 2, :].rearrange("p m c -> p (m c)"), ABANK[1][0:SLOT, :],
                                       ACT.Identity).then_inc(s["a_kA"], 1)

                    def A_turned2(n, f):
                        wait(act, "a_T2", n, f + 1)
                        act.activation(qT[:, 2 * f:2 * f + 2, :].rearrange("p m c -> p (m c)"), ABANK[f % 2][:, :], ACT.Identity).then_inc(s["a_q2a"], 1)

                    def A_exp(n, p):
                        wait(act, "a_S", n, PAIRS + p + 1)
                        if p >= 3:
                            wait(act, "a_pv", n, p - 2)
                        r = 2 * (p % 2)
                        act.activation(pT[:, p % 3, :, :], S[:, r:r + 2, :], ACT.Exp, scale=float(HD) ** -0.5).then_inc(s["a_ex"], 1)

                    def A_ohi(n):
                        wait(act, "a_nT", n, 1)
                        act.activation(xh[:, 0:2, :].rearrange("p m c -> p (m c)"), ABANK[0][0:KP, :], ACT.Identity).then_inc(s["a_oh"], 1)
                        wait(act, "a_nT", n, 2)
                        act.activation(xh[:, 2, :], ABANK[1][0:KP, 0:T], ACT.Identity).then_inc(s["a_oh"], 1)

                    def R_x(n):
                        b = n - first
                        wait(act, "r_T", b, 1)
                        act.activation(xf2[:, 0:2, :].rearrange("p m c -> p (m c)"), MBANK[1][0:KP, :], ACT.Identity).then_inc(s["r_x"], 1)
                        wait(act, "r_T", b, 2)
                        act.activation(xf2[:, 2, :], MBANK[0][0:KP, 0:T], ACT.Identity).then_inc(s["r_x"], 1)

                    def R_z(n):
                        wait(act, "r_z", n - first, 1)
                        act.activation(zT[:, :], MBANK[1][0:ROT, 0:T], ACT.Identity).then_inc(s["r_zs"], 1)

                    def R_y(n):
                        wait(act, "r_y", n - first, 1)
                        act.activation(yT[:, :], MBANK[0][0:ROT, 0:T], ACT.Identity).then_inc(s["r_ys"], 1)

                    def slot(a, m):
                        if a is not None:
                            A_xf(a)
                        if m is not None:
                            M_xf(m)
                            M_gelu(m, 0)
                        if a is not None and eps is not None:
                            A_square(a)
                        if m is not None:
                            for f in range(1, 5):
                                M_gelu(m, f)
                        if a is not None:
                            A_khi(a)
                            for f in range(4):
                                A_turned(a, f)
                            A_turned2(a, 0)
                            A_turned2(a, 2)
                            A_exp(a, 0)
                            A_exp(a, 1)
                        if m is not None and rot:
                            R_x(m)
                        if a is not None:
                            A_exp(a, 2)
                            A_exp(a, 3)
                        if m is not None and rot:
                            R_z(m)
                        if a is not None:
                            A_exp(a, 4)
                            A_exp(a, 5)
                        if m is not None and rot:
                            R_y(m)
                        if a is not None:
                            A_exp(a, 6)
                            A_exp(a, 7)
                            A_ohi(a)

                    slot(first, None)
                    if start > first + 1:
                        slot(first + 1, first)
                    with act.Fori(start, last) as n:
                        slot(n, n - 1)
                    slot(None, last - 1)

                @block.vector
                def _(dve):
                    for c, (_, rows, cols, to) in enumerate(chunks(layer)):
                        dve.wait_ge(w_hi, layer * NCH + c + 1)
                        dve.tensor_tensor(to[1], wst[0:rows, c % 2, 0:cols], to[0].bitcast(F32), ALU.subtract).then_inc(w_lo, 1)
                    if layer == 0:
                        dve.wait_ge(set_done, 7)
                    dve.wait_ge(p_in, 16 * [6, 10, 18][layer])

                    STEPS_A = 8 + (16 if eps is not None else 0) + (1 if rot else 0)
                    STEPS_M = 3
                    base = steps[0]
                    state = {}

                    def own(op):
                        op.then_inc(dve_step, 1)
                        state["k"] += 1
                        dve.wait_ge(dve_step, state["from"] + state["k"])

                    def A_stats(n):
                        wait(dve, "a_x", n, 16)
                        wait(dve, "a_rs", n, 0)
                        for i in range(NT):
                            op = dve.bn_stats(stA[:, i, :], xld[:, i, :])
                        own(op)
                        constant_wait(dve)
                        for i in range(NT):
                            op = dve.bn_aggr(mvA[:, i, :], stA[:, i, :])
                        op.then_inc(s["a_st"], 1)

                    def M_stats(n):
                        wait(dve, "a_x1", n, 2)
                        wait(dve, "m_rs", n, 0)
                        for i in range(NT):
                            op = dve.bn_stats(stM[:, i, :], x1[:, i, :])
                        own(op)
                        constant_wait(dve)
                        for i in range(NT):
                            op = dve.bn_aggr(mvM[:, i, :], stM[:, i, :])
                        op.then_inc(s["m_st"], 1)

                    def A_norm(n):
                        wait(dve, "a_rs", n, 1)
                        wait(dve, "a_st", n, 1)
                        wait(dve, "a_nT", n, 0)
                        for i in range(NT):
                            dve.tensor_scalar(xn[:, i, :], xld[:, i, :], mvA[:, i, 0:1], rsA[:, i:i + 1],
                                              ALU.subtract, ALU.mult).then_inc(s["a_xn"], 1)

                    def M_norm(n):
                        wait(dve, "m_rs", n, 1)
                        wait(dve, "m_st", n, 1)
                        wait(dve, "m_out", n, 0)
                        for i in range(NT):
                            dve.tensor_scalar(xo[:, i, :], x1[:, i, :], mvM[:, i, 0:1], rsM[:, i:i + 1],
                                              ALU.subtract, ALU.mult).then_inc(s["m_xn"], 1)

                    def A_xl(n):
                        wait(dve, "a_xh", n, 1)
                        wait(dve, "a_pr", n, 0)
                        dve.tensor_tensor(xl[:, :, :], xf, xh[:, :, :].bitcast(F32), ALU.subtract).then_inc(s["a_xl"], 1)

                    def M_xl(n):
                        wait(dve, "m_xh", n, 1)
                        wait(dve, "m_h", n, 0)
                        dve.tensor_tensor(xl2[:, :, :], xf2, xh2[:, :, :].bitcast(F32), ALU.subtract).then_inc(s["m_xl"], 1)

                    def A_qkv(n):
                        wait(dve, "a_pv", n, 0)
                        for f in range(6):
                            wait(dve, "a_qkv", n, f + 1)
                            i, part = (f // 2, f % 2) if f < 4 else (f - 4, 2)
                            to = qk[:, i, part * D:(part + 1) * D] if part < 2 else V[:, i, :, 1:1 + HD]
                            a, b = ABANK[f % 2][:, 0:D], bqkv[:, part * D:(part + 1) * D]
                            if part == 2:
                                a, b = (z.rearrange("p (h d) -> p h d", h=H) for z in (a, b))
                            dve.tensor_tensor(to, a, b, ALU.add).then_inc(s["a_qkvd"], 1)
                        wait(dve, "a_qkvd", n, 6)

                    heads = qk.rearrange("p t c -> p (t c)").rearrange("p (g d) -> p g d", d=HD)

                    def A_center(n):
                        own(dve.tensor_reduce(sm[:, :], heads, AX.X, ALU.add))
                        own(dve.tensor_scalar(sm[:, :], sm[:, :], -1.0 / HD, None, ALU.mult))
                        dve.tensor_tensor(heads, heads, sm[:, :].unsqueeze(2).broadcast_to([P, 64, HD]), ALU.add).then_inc(s["a_c"], 1)

                    def A_heads_rstd(n):
                        wait(dve, "a_sq", qk_run(n), 1)
                        own(dve.tensor_reduce(nv[:, :], sq.rearrange("p (g d) -> p g d", d=HD), AX.X, ALU.add))
                        own(dve.tensor_scalar(nv[:, :], nv[:, :], 1.0 / HD, eps, ALU.mult, ALU.add))
                        own(dve.tensor_scalar(ny[:, :].bitcast(I32), nv[:, :].bitcast(I32), 1, None, ALU.logical_shift_right))
                        own(dve.tensor_scalar(ny[:, :].bitcast(I32), ny[:, :].bitcast(I32), -1.0, float(NEWTON_MAGIC), ALU.mult, ALU.add))
                        for _ in range(3):
                            own(dve.scalar_tensor_tensor(out=na[:, :], in0=ny[:, :], scalar=-0.5, in1=ny[:, :], op0=ALU.mult, op1=ALU.mult))
                            own(dve.tensor_tensor(na[:, :], na[:, :], nv[:, :], ALU.mult))
                            own(dve.scalar_tensor_tensor(out=ny[:, :], in0=na[:, :], scalar=1.5, in1=ny[:, :], op0=ALU.add, op1=ALU.mult))

                    def A_heads_norm(n):
                        wait(dve, "a_c", qk_run(n), 1)
                        own(dve.tensor_tensor(heads, heads, ny[:, :].unsqueeze(2).broadcast_to([P, 64, HD]), ALU.mult))
                        for table, op in ((gam, ALU.mult),) + (((bet, ALU.add),) if rot else ()):
                            for i in range(2):
                                part = qk[:, :, i * D:(i + 1) * D].rearrange("p t (h d) -> p t h d", h=H)
                                for j in range(NT):
                                    step = dve.tensor_tensor(
                                        part[:, j], part[:, j], table[:, i * HD:(i + 1) * HD].unsqueeze(1).broadcast_to([P, H, HD]), op)
                            if table is (bet if rot else gam):
                                step.then_inc(s["a_nrm"], 1)
                                wait(dve, "a_nrm", qk_run(n), 1)
                            else:
                                own(step)

                    def A_qs(n):
                        wait(dve, "a_T2", n, 0)
                        own(dve.memset(qs[:, :, :, 0:2].bitcast(F32), 0.0))
                        for i in range(NT):
                            qv = qk[:, i, 0:D].rearrange("p (h d) -> p h d", h=H)
                            dve.tensor_copy(qs[:, i, :, 2:2 + HD], qv)
                            op = dve.tensor_copy(qs[:, i, :, 2 + HD:2 + 2 * HD], qv)
                        own(op)
                        for i in range(NT):
                            qv = qk[:, i, 0:D].rearrange("p (h d) -> p h d", h=H)
                            op = dve.tensor_tensor(qs[:, i, :, 2 + 2 * HD:2 + 3 * HD], qv, qs[:, i, :, 2:2 + HD].bitcast(F32), ALU.subtract)
                        op.then_inc(s["a_qs"], 1)

                    def M_hl(n, f):
                        wait(dve, "m_hh", n, f + 1)
                        m = min(2, FM - 2 * f)
                        dve.tensor_tensor(hl[:, 2 * f:2 * f + m, :].rearrange("p m c -> p (m c)"), hf[:, f % 2, 0:m * T],
                                          hh[:, 2 * f:2 * f + m, :].rearrange("p m c -> p (m c)").bitcast(F32),
                                          ALU.subtract).then_inc(s["m_hl"], 1)

                    def A_kB(n, f):
                        if f == 0:
                            wait(dve, "a_S", n, 0)
                        wait(dve, "a_T", n, 2 * f + 2)
                        dve.tensor_copy(kz[1][SLOT:P, 2 * f:2 * f + 2, :].rearrange("p m c -> p (m c)"), ABANK[1][SLOT:P, :]).then_inc(s["a_kB"], 1)

                    def A_max(n, p):
                        wait(dve, "a_S", n, p + 1)
                        if p == 0:
                            wait(dve, "a_nm", n, 0)
                        r = 2 * (p % 2)
                        dve.tensor_reduce(mx[:, p, :, :], S[:, r:r + 2, :].rearrange("p a (t k) -> p a t k", t=NT),
                                          AX.X, ALU.max).then_inc(s["a_mx"], 1)

                    def A_negmax(n):
                        wait(dve, "a_mx", n, PAIRS)
                        own(dve.tensor_scalar(nmx[:, :, :, :], mx[:, :, :, :], -1.0, None, ALU.mult))
                        wait(dve, "a_T", n, 8)
                        view = nmx[:, :, :, :].rearrange("p q a t -> p t (q a)")
                        own(dve.tensor_copy(qs[:, :, :, 0], view))
                        dve.tensor_tensor(qs[:, :, :, 1], view, qs[:, :, :, 0].bitcast(F32), ALU.subtract).then_inc(s["a_nm"], 1)

                    def A_turned2(n, f):
                        wait(dve, "a_T2", n, f + 1)
                        dve.tensor_copy(qT[:, 2 * f:2 * f + 2, :].rearrange("p m c -> p (m c)"), ABANK[f % 2][:, :]).then_inc(s["a_q2d"], 1)

                    def A_oraw(n, i):
                        wait(dve, "a_pv", n, 4 * i + 4)
                        dve.tensor_copy(oraw[:, 2 * i:2 * i + 2, :].rearrange("p m c -> p (m c)"), ABANK[i][:, :]).then_inc(s["a_o"], 1)

                    def A_out(n):
                        for i in range(NT):
                            wait(dve, "a_oT", n, i + 1)
                            v = ABANK[i][:, :].rearrange("p (h d) -> p h d", h=H)
                            own(dve.reciprocal(rden[:, i, :], v[:, :, 0]))
                            dve.tensor_tensor(xn[:, i, :].rearrange("p (h d) -> p h d", h=H), v[:, :, 1:1 + HD],
                                              rden[:, i, :].unsqueeze(2).broadcast_to([P, H, HD]), ALU.mult).then_inc(s["a_on"], 1)

                    def A_olo(n):
                        wait(dve, "a_oh", n, 1)
                        dve.tensor_tensor(xl[:, 0:2, :].rearrange("p m c -> p (m c)"), ABANK[0][0:KP, :],
                                          xh[:, 0:2, :].rearrange("p m c -> p (m c)").bitcast(F32), ALU.subtract).then_inc(s["a_ol"], 1)
                        wait(dve, "a_oh", n, 2)
                        dve.tensor_tensor(xl[:, 2, :], ABANK[1][0:KP, 0:T], xh[:, 2, :].bitcast(F32), ALU.subtract).then_inc(s["a_ol"], 1)

                    def A_x1(n):
                        wait(dve, "a_xa", n, 1)
                        wait(dve, "m_xb", n, 0)
                        wait(dve, "m_xn", n, 0)
                        for i in range(NT):
                            wait(dve, "a_pr", n, i + 1)
                            step = dve.tensor_tensor(x1[:, i, :], ABANK[i][:, 0:D], gA[:, :], ALU.mult)
                        own(step)
                        for i in range(NT):
                            dve.tensor_tensor(x1[:, i, :], x1[:, i, :], xa[:, i, :], ALU.add).then_inc(s["a_x1"], 1)

                    def M_x2(n, i):
                        if i == 0:
                            wait(dve, "m_xb", n, 1)
                            wait(dve, "m_xT", n, 2)
                        wait(dve, "m_y", n, i + 1)
                        own(dve.tensor_tensor(xo[:, i, :], MBANK[1 - i][:, 0:D], gM[:, :], ALU.mult))
                        dve.tensor_tensor(xo[:, i, :], xo[:, i, :], xb[:, i, :], ALU.add).then_inc(s["m_x2"], 1)

                    def R_x3(n):
                        wait(dve, "m_x2", n, 2)
                        wait(dve, "r_T", n - first, 2)
                        for i in range(NT):
                            wait(dve, "r_o", n - first, i + 1)
                            dve.tensor_tensor(xo[:, i, :], MBANK[1 - i][:, 0:D], xo[:, i, :], ALU.add).then_inc(s["r_x3"], 1)

                    def slot(a, m):
                        if a is not None:
                            runs_a, runs_m = a - first, (a - first - 1 if m is not None else 0)
                        else:
                            runs_a, runs_m = B, B - 1
                        state["from"] = base + runs_a * STEPS_A + runs_m * STEPS_M
                        state["k"] = 0
                        if a is not None:
                            A_stats(a)
                        if m is not None:
                            M_stats(m)
                        if a is not None:
                            A_norm(a)
                        if m is not None:
                            M_norm(m)
                        if a is not None:
                            A_xl(a)
                        if m is not None:
                            M_xl(m)
                        if a is not None:
                            A_qkv(a)
                            if eps is not None:
                                A_center(a)
                        if m is not None:
                            M_hl(m, 0)
                            M_hl(m, 1)
                        if a is not None and eps is not None:
                            A_heads_rstd(a)
                        if m is not None:
                            M_hl(m, 2)
                        if a is not None and eps is not None:
                            A_heads_norm(a)
                        if m is not None:
                            M_hl(m, 3)
                        if a is not None:
                            A_qs(a)
                        if m is not None:
                            M_hl(m, 4)
                        if a is not None:
                            A_kB(a, 0)
                            for f in range(4):
                                if f < 3:
                                    A_kB(a, f + 1)
                                A_max(a, 2 * f)
                                A_max(a, 2 * f + 1)
                                if f == 1 and m is not None:
                                    M_x2(m, 0)
                            A_negmax(a)
                        elif m is not None:
                            M_x2(m, 0)
                        if m is not None:
                            M_x2(m, 1)
                        if a is not None:
                            A_turned2(a, 1)
                            A_turned2(a, 3)
                            A_oraw(a, 0)
                        if m is not None and rot:
                            R_x3(m)
                        if a is not None:
                            A_oraw(a, 1)
                            A_out(a)
                            A_olo(a)
                            A_x1(a)
                        made = (STEPS_A if a is not None else 0) + (STEPS_M if m is not None else 0)
                        assert state["k"] == made

                    slot(first, None)
                    if start > first + 1:
                        slot(first + 1, first)
                    with dve.Fori(start, last) as n:
                        slot(n, n - 1)
                    slot(None, last - 1)
                    steps[0] = base + B * (STEPS_A + STEPS_M)

                @block.tensor
                def _(pe):
                    pe.wait_ge(w_lo, NCH * (layer + 1))
                    if layer == 0:
                        pe.wait_ge(set_done, 7)

                    def three(out, xs, ws, n_k, lhs, rhs):
                        terms = [(xs[0], ws[0]), (xs[0], ws[1]), (xs[1], ws[0])]
                        for j, (x, wt) in enumerate(terms):
                            for k in range(n_k):
                                op = pe.matmul(out, lhs(x, k), rhs(wt, k), start=(j == 0 and k == 0), stop=(j == 2 and k == n_k - 1))
                        return op

                    def turn3(x, banks, done, run):
                        for c in range(KC):
                            for i in range(NT):
                                op = pe.transpose(banks[c // 2][0:KP, (c % 2) * T + i * P:(c % 2) * T + (i + 1) * P],
                                                  x[:, i, c * KP:(c + 1) * KP], ident[:, :])
                            if c:
                                op.then_inc(s[done], 1)

                    def A_turn(n):
                        wait(pe, "a_xn", n, 2)
                        wait(pe, "a_x1", n, 0)
                        turn3(xn, ABANK, "a_xT", n)

                    def A_qkv(n):
                        wait(pe, "a_xl", n, 1)
                        for f in range(6):
                            i, part = (f // 2, f % 2) if f < 4 else (f - 4, 2)
                            if f < 2:
                                wait(pe, "a_xf", n, 2 + f)
                            else:
                                wait(pe, "a_qkvd", n, f - 1)
                            three(ABANK[f % 2][:, 0:D], (xh, xl), wqkv, KC,
                                  lambda x, k: x[:, k, i * P:(i + 1) * P],
                                  lambda wt, k: wt[:, k, part * D:(part + 1) * D]).then_inc(s["a_qkv"], 1)

                    def A_turn_qk(n, f):
                        if f == 0:
                            wait(pe, "a_qs", n, 1)
                            wait(pe, "a_kh", n, 1)
                            wait(pe, "a_kl", n, 1)
                            wait(pe, "a_qkvd", n, 6)
                        else:
                            wait(pe, "a_qT", n, f)
                        for p in range(2):
                            for i in range(NT):
                                op = pe.transpose(ABANK[0][:, p * T + i * P:p * T + (i + 1) * P],
                                                  qs[:, i, 4 * f + 2 * p:4 * f + 2 * p + 2, :].rearrange("p h d -> p (h d)").bitcast(F32), ident[:, :])
                        op.then_inc(s["a_T"], 1)
                        if f:
                            wait(pe, "a_kA", n, f)
                            wait(pe, "a_kB", n, f)
                        for p in range(2):
                            for i in range(NT):
                                op = pe.transpose(ABANK[1][:, p * T + i * P:p * T + (i + 1) * P],
                                                  ks[:, i, 4 * f + 2 * p:4 * f + 2 * p + 2, :].rearrange("p h d -> p (h d)").bitcast(F32), ident[:, :])
                        op.then_inc(s["a_T"], 1)

                    def A_scores(n, p):
                        if p % 2 == 0:
                            wait(pe, "a_qT", n, p // 2 + 1)
                            wait(pe, "a_kA", n, p // 2 + 1)
                            wait(pe, "a_kB", n, p // 2 + 1)
                        if p < 2:
                            wait(pe, "a_ex", n, 0)
                        else:
                            wait(pe, "a_mx", n, p - 1)
                        for a in range(2):
                            for i in range(NT):
                                op = pe.matmul(S[:, 2 * (p % 2) + a, i * T:(i + 1) * T], qT[:, p, i * P:(i + 1) * P], kz[a][:, p, :],
                                               start=True, stop=True)
                        op.then_inc(s["a_S"], 1)

                    def A_turn_q2(n, f):
                        if f == 0:
                            wait(pe, "a_nm", n, 1)
                            wait(pe, "a_qT", n, 4)
                        if f == 1:
                            wait(pe, "a_kA", n, 4)
                            wait(pe, "a_kB", n, 4)
                        if f == 2:
                            wait(pe, "a_q2a", n, 1)
                        if f == 3:
                            wait(pe, "a_q2d", n, 1)
                        for p in range(2):
                            for i in range(NT):
                                op = pe.transpose(ABANK[f % 2][:, p * T + i * P:p * T + (i + 1) * P],
                                                  qs[:, i, 4 * f + 2 * p:4 * f + 2 * p + 2, :].rearrange("p h d -> p (h d)").bitcast(F32), ident[:, :])
                        op.then_inc(s["a_T2"], 1)

                    def A_scoresT(n, p):
                        if p % 2 == 0:
                            wait(pe, "a_q2a" if p % 4 == 0 else "a_q2d", n, p // 4 + 1)
                        if p < 2:
                            wait(pe, "a_mx", n, PAIRS - 1 + p)
                        else:
                            wait(pe, "a_ex", n, p - 1)
                        for a in range(2):
                            for i in range(NT):
                                op = pe.matmul(S[:, 2 * (p % 2) + a, i * T:(i + 1) * T], kz[a][:, p, i * P:(i + 1) * P], qT[:, p, :],
                                               start=True, stop=True)
                        op.then_inc(s["a_S"], 1)

                    def A_pv(n, p):
                        wait(pe, "a_ex", n, p + 1)
                        if p == 0:
                            wait(pe, "a_q2a", n, 2)
                            wait(pe, "a_q2d", n, 2)
                        j = p // 2
                        for i in range(NT):
                            for a in range(2):
                                g = 2 * (p % 2) + a
                                op = pe.matmul(ABANK[j // 2][32 * g:32 * g + 32, (j % 2) * T:(j % 2 + 1) * T], V[:, i, 2 * p + a, :],
                                               pT[:, p % 3, a, i * T:(i + 1) * T], start=(i == 0), stop=(i == NT - 1),
                                               tile_position=(0, 32 * g))
                        op.then_inc(s["a_pv"], 1)

                    def A_turn_o(n):
                        for i in range(NT):
                            wait(pe, "a_o", n, 2)
                            for j in range(4):
                                op = pe.transpose(ABANK[i][:, j * P:(j + 1) * P], oraw[:, j, i * P:(i + 1) * P], ident[:, :])
                            op.then_inc(s["a_oT"], 1)

                    def A_turn_n(n):
                        wait(pe, "a_on", n, 2)
                        turn3(xn, ABANK, "a_nT", n)

                    def A_proj(n):
                        wait(pe, "a_ol", n, 2)
                        for i in range(NT):
                            three(ABANK[i][:, 0:D], (xh, xl), wo, KC, lambda x, k: x[:, k, i * P:(i + 1) * P],
                                  lambda wt, k: wt[:, k, :]).then_inc(s["a_pr"], 1)

                    def M_turn(n):
                        wait(pe, "m_xn", n, 2)
                        if rot:
                            wait(pe, "r_x3", n - first, 0)
                            if isinstance(n, int) and n == first:
                                wait(pe, "m_x2", n, 0)
                        else:
                            wait(pe, "m_x2", n, 0)
                        turn3(xo, MBANK, "m_xT", n)

                    def M_up(n, f):
                        if f == 0:
                            wait(pe, "m_xl", n, 1)
                            wait(pe, "m_xf", n, 2)
                        elif f == 1:
                            wait(pe, "m_xf", n, 3)
                        else:
                            wait(pe, "m_hf", n, f - 1)
                        for i in range(min(2, FM - 2 * f)):
                            m = 2 * f + i
                            terms = [(w1[0], xh2), (w1[1], xh2), (w1[0], xl2)]
                            for j, (wt, x) in enumerate(terms):
                                for k in range(KC):
                                    op = pe.matmul(MBANK[f % 2][:, i * T:(i + 1) * T], wt[:, k, m * P:(m + 1) * P], x[:, k, :],
                                                   start=(j == 0 and k == 0), stop=(j == 2 and k == KC - 1))
                        op.then_inc(s["m_h"], 1)

                    def M_down(n, i):
                        if i == 0:
                            wait(pe, "m_hl", n, 5)
                            wait(pe, "m_hf", n, 4)
                        else:
                            wait(pe, "m_hf", n, 5)
                        three(MBANK[1 - i][:, 0:D], (hh, hl), w2, FM, lambda x, k: x[:, k, i * P:(i + 1) * P],
                              lambda wt, k: wt[:, k, :]).then_inc(s["m_y"], 1)

                    def R_turn(n):
                        wait(pe, "m_x2", n, 2)
                        turn3(xo, MBANK[::-1], "r_T", n)

                    def R_z(n):
                        wait(pe, "r_x", n - first, 2)
                        for k in range(KC):
                            op = pe.matmul(MBANK[1][0:ROT, 0:T], U[:, k, :], xf2[:, k, :], start=(k == 0), stop=(k == KC - 1))
                        op.then_inc(s["r_z"], 1)

                    def R_y(n):
                        wait(pe, "r_zs", n - first, 1)
                        wait(pe, "r_e", n - first, 16)
                        constant_wait(pe)
                        pe.matmul(MBANK[0][0:ROT, 0:T], eb[:, :], zT[:, :], start=True, stop=True).then_inc(s["r_y"], 1)

                    def R_out(n):
                        wait(pe, "r_ys", n - first, 1)
                        for i in range(NT):
                            pe.matmul(MBANK[1 - i][:, 0:D], yT[:, i * P:(i + 1) * P], UT[:, :], start=True, stop=True).then_inc(s["r_o"], 1)

                    def slot(a, m):
                        if a is not None:
                            A_turn(a)
                        if m is not None:
                            M_turn(m)
                        if a is not None:
                            A_qkv(a)
                        if m is not None:
                            for f in range(5):
                                M_up(m, f)
                            M_down(m, 0)
                        if a is not None:
                            A_turn_qk(a, 0)
                            for f in range(4):
                                if f < 3:
                                    A_turn_qk(a, f + 1)
                                A_scores(a, 2 * f)
                                A_scores(a, 2 * f + 1)
                        if m is not None:
                            M_down(m, 1)
                        if a is not None:
                            for f in range(4):
                                A_turn_q2(a, f)
                            A_scoresT(a, 0)
                            A_scoresT(a, 1)
                        if m is not None and rot:
                            R_turn(m)
                        if a is not None:
                            for p in range(2, PAIRS):
                                A_pv(a, p - 2)
                                A_scoresT(a, p)
                                if m is not None and rot and p == 3:
                                    R_z(m)
                                if m is not None and rot and p == 5:
                                    R_y(m)
                                if m is not None and rot and p == 7:
                                    R_out(m)
                            A_pv(a, PAIRS - 2)
                            A_pv(a, PAIRS - 1)
                            A_turn_o(a)
                            A_turn_n(a)
                            A_proj(a)
                        elif rot:
                            R_z(m)
                            R_y(m)
                            R_out(m)

                    slot(first, None)
                    if start > first + 1:
                        slot(first + 1, first)
                    with pe.Fori(start, last) as n:
                        slot(n, n - 1)
                    slot(None, last - 1)


def preamble(nc, t, sem, S, ABANK, MBANK, ident, modT, U, UT, mhalf, gates, expm):
    HB = B // 2
    with ExitStack() as ctx:
        def sb(name, shape, dt=F32):
            return ctx.enter_context(nc.sbuf_tensor(name, shape, dt))

        cT = sb("cT", [KP, KC, B])
        sT = sb("sT", [KP, KC, B])
        wmod = sb("wmod", [KP, KC, 6 * D])
        bmodT = sb("bmodT", [KP, LAYERS, 12])
        bgate = sb("bgate", [B, LAYERS, 2 * D])
        grow = sb("grow", [B, 2 * D])
        WJ = 16
        wr = sb("wr", [KP, KC, 2, WJ, ROT])
        bfull = sb("bfull", [P, ROT])
        sign = sb("sign", [P, ROT])
        Bm = sb("Bm", [P, HB, ROT])
        Nm = sb("Nm", [P, HB, ROT])
        Em = sb("Em", [P, HB, ROT])
        Fm = sb("Fm", [P, HB, ROT])
        Bk = sb("Bk", [P, HB, ROT])
        Nk = sb("Nk", [P, HB, ROT])
        blockones = sb("blockones", [P, P])
        house_row = sb("house_row", [P, P])
        eye2 = sb("eye2", [P, ROT])
        after = sb("after", [P, ROT])
        mask = sb("mask", [P, ROT + D])
        house = sb("house", [P, 1])
        G = sb("G", [P, D])
        mk = sb("mk", [P, D])
        vs = sb("vs", [P, D])
        junk = sb("junk", [P, D])
        junk2 = sb("junk2", [P, D])
        dot = sb("dot", [P, 1])
        n2 = sb("n2", [P, 1])
        rt = sb("rt", [P, 1])
        sg = sb("sg", [P, ROT])
        q = [sb(f"q{i}", [P, 1]) for i in range(8)]

        load = sem("load")
        wm_in = sem("wm_in")
        wr_in = [sem("wr_in0"), sem("wr_in1")]
        silu = sem("silu")
        const = sem("const")
        mod_mm = sem("mod_mm")
        mod_out = sem("mod_out")
        gate_out = sem("gate_out")
        a_mm = sem("a_mm")
        a_done = sem("a_done")
        e_mm = sem("e_mm")
        e_up = sem("e_up")
        e_k = sem("e_k")
        e_out = sem("e_out")
        g_mk = sem("g_mk")
        g_vb = sem("g_vb")
        g_n2 = sem("g_n2")
        g_rt = sem("g_rt")
        g_step = sem("g_step")
        u_mm = sem("u_mm")
        u_n2 = sem("u_n2")
        u_rt = sem("u_rt")

        CONSTS = 23
        A4 = [S[:, i, :] for i in range(4)]
        NJ = ROT // WJ

        block = ctx.enter_context(nc.Block())

        @block.sync
        def _(sp):
            for to, ap in ((cT[:, :, :], t["cT"]), (bmodT[:, :, :], t["bmodT"]), (bfull[0:ROT, :], t["bfull"]),
                           (bfull[ROT:P, :], t["bfull"]), (G[0:ROT, :], t["PT"]), (G[ROT:P, :], t["PT"])):
                sp.dma_start(to, ap).then_inc(load, 16)
            for i in range(LAYERS):
                sp.dma_start(bgate[:, i, :], t["bgate"][i].partition_broadcast(B)).then_inc(load, 16)
            for i in range(LAYERS):
                if i:
                    sp.wait_ge(mod_mm, 2 * i)
                sp.dma_start(wmod[:, :, :], t[i]["wmod"].rearrange("(k p) n -> p k n", p=KP)).then_inc(wm_in, 16)
            for c in range(NJ):
                if c >= 2:
                    sp.wait_ge(a_mm, c - 1)
                sp.dma_start(wr[:, :, c % 2, :, :], t["wrot"].rearrange("(k p) j i -> p k j i", p=KP)[:, :, c * WJ:(c + 1) * WJ, :]).then_inc(wr_in[c % 2], 16)
            sp.wait_ge(e_up, 2 * (TAYLOR + SQUARINGS))
            for h in range(2):
                sp.dma_start(expm[h * HB:(h + 1) * HB].rearrange("b d e -> d b e"), Em[h * ROT:(h + 1) * ROT, :, :]).then_inc(e_out, 16)
            sp.wait_ge(gate_out, 16 * LAYERS)
            sp.wait_ge(e_out, 32)

        @block.gpsimd
        def _(pool):
            made = [0]

            def own(op):
                op.then_inc(const, 1)
                made[0] += 1
                pool.wait_ge(const, made[0])

            def keep(tile, rows, op, value, step=1, tilestep=-1):
                view = tile[rows[0]:rows[1], :]
                own(pool.affine_select(out=view, in_=view, compare_op=op, fill=value, base=0,
                                       pattern=[[tilestep, view.shape[1]]], channel_multiplier=step))

            for tile, value in ((ident, 0.0), (blockones, 0.0), (house_row, 0.0), (eye2, 0.0), (after, -1.0), (mask, 1.0),
                                (mhalf, -0.5), (house, 0.0), (sign, 1.0)):
                own(pool.memset(tile[:, :], value))
            keep(ident, (0, P), ALU.not_equal, 1.0)
            own(pool.memset(blockones[0:ROT, 0:ROT], 1.0))
            own(pool.memset(blockones[ROT:P, ROT:P], 1.0))
            own(pool.memset(house_row[ROT:ROT + 1, :], 1.0))
            own(pool.memset(mask[ROT:P, 0:ROT], 0.0))
            own(pool.memset(house[ROT:P, :], 1.0))
            for rows in ((0, ROT), (ROT, P)):
                keep(eye2, rows, ALU.not_equal, 1.0)
                keep(after, rows, ALU.is_gt, 0.0)
                keep(sign, rows, ALU.is_gt, -1.0, step=-1, tilestep=1)
                keep(sign, rows, ALU.not_equal, 0.0)
            assert made[0] == CONSTS
            with pool.Fori(0, ROT) as j:
                pool.wait_ge(g_n2, j + 1)
                pool.tensor_tensor(rt[:, :], n2[:, :], mhalf[:, 0:1], ALU.pow).then_inc(g_rt, 1)
            pool.wait_ge(u_n2, 1)
            pool.tensor_tensor(rt[:, :], n2[:, :], mhalf[:, 0:1], ALU.pow).then_inc(u_rt, 1)

        @block.scalar
        def _(act):
            act.wait_ge(load, 16 * 9)
            act.activation(sT[:, :, :], cT[:, :, :], ACT.Silu).then_inc(silu, 1)
            for i in range(LAYERS):
                act.wait_ge(mod_out, 3 * i + 3)
                act.dma_start(gates[i], grow[:, :]).then_inc(gate_out, 16)
            for k in range(TAYLOR, 0, -1):
                i = TAYLOR - k
                if i == 0:
                    act.wait_ge(a_done, 3 * NJ)
                else:
                    act.wait_ge(e_up, 2 * i)
                act.mul(Bk[:, :, :], Bm[:, :, :], 1.0 / k).then_inc(e_k, 1)
                act.mul(Nk[:, :, :], Bm[:, :, :], -1.0 / k).then_inc(e_k, 1)
            with act.Fori(0, ROT) as j:
                act.wait_ge(g_step, j * 14 + 2)
                act.activation(junk2[:, :], vs[:, :], ACT.Square, accum_out=n2[:, :]).then_inc(g_n2, 1)
            act.wait_ge(g_step, 14 * ROT)
            act.activation(junk2[:, :], G[:, :], ACT.Square, accum_out=n2[:, :]).then_inc(u_n2, 1)

        @block.vector
        def _(dve):
            dve.wait_ge(const, CONSTS)
            dve.wait_ge(load, 16 * 9)
            for i in range(LAYERS):
                dve.wait_ge(mod_mm, 2 * i + 1)
                v = modT[:, i, :, :]
                dve.tensor_tensor(v, MBANK[0][0:KP, 0:12 * B].rearrange("p (c b) -> p c b", b=B),
                                  bmodT[:, i, :].unsqueeze(2).broadcast_to([KP, 12, B]), ALU.add).then_inc(mod_out, 1)
                dve.wait_ge(mod_out, 3 * i + 1)
                for c in (3, 9):
                    op = dve.tensor_scalar(v[:, c:c + 3, :], v[:, c:c + 3, :], 1.0, None, ALU.add)
                op.then_inc(mod_out, 1)
                dve.wait_ge(mod_mm, 2 * i + 2)
                if i:
                    dve.wait_ge(gate_out, 16 * i)
                for g in range(2):
                    op = dve.tensor_tensor(grow[:, g * D:(g + 1) * D], ABANK[g][0:B, 0:D], bgate[:, i, g * D:(g + 1) * D], ALU.add)
                op.then_inc(mod_out, 1)
            for c in range(NJ):
                dve.wait_ge(a_mm, c + 1)
                for h in range(2):
                    to = Bm[h * ROT:(h + 1) * ROT, :, c * WJ:(c + 1) * WJ]
                    at = A4[c % 4][h * ROT:(h + 1) * ROT, :].rearrange("p (j b) -> p b j", b=B)[:, h * HB:(h + 1) * HB, :]
                    op = dve.tensor_tensor(to, at, bfull[h * ROT:(h + 1) * ROT, c * WJ:(c + 1) * WJ].unsqueeze(1).broadcast_to([ROT, HB, WJ]), ALU.add)
                op.then_inc(a_done, 1)
                dve.wait_ge(a_done, 3 * c + 1)
                part = Bm[:, :, c * WJ:(c + 1) * WJ]
                dve.tensor_tensor(part, part, sign[:, c * WJ:(c + 1) * WJ].unsqueeze(1).broadcast_to([P, HB, WJ]), ALU.mult).then_inc(a_done, 1)
                dve.wait_ge(a_done, 3 * c + 2)
                dve.tensor_scalar(part, part, 2.0 ** -SQUARINGS, None, ALU.mult).then_inc(a_done, 1)
            dve.wait_ge(a_done, 3 * NJ)
            dve.tensor_scalar(Nm[:, :, :], Bm[:, :, :], -1.0, None, ALU.mult).then_inc(a_done, 1)
            dve.wait_ge(e_k, 2)
            dve.tensor_copy(Em[:, :, :], Bk[:, :, :]).then_inc(e_up, 1)
            dve.tensor_copy(Fm[:, :, :], Nk[:, :, :]).then_inc(e_up, 1)
            S2 = S[:, :, :].rearrange("p (x y) c -> p x (y c)", x=2)

            def flat(x):
                return x[:, :, :].rearrange("p b e -> p (b e)")

            for k in range(TAYLOR - 1, 0, -1):
                i = TAYLOR - k
                dve.wait_ge(e_k, 2 * i + 2)
                dve.wait_ge(e_mm, i)
                for x, part, m in ((Em, 0, Bk), (Fm, 1, Nk)):
                    dve.scalar_tensor_tensor(out=flat(x), in0=S2[:, part, :], scalar=1.0 / k, in1=flat(m),
                                             op0=ALU.mult, op1=ALU.add).then_inc(e_up, 1)
            with dve.Fori(0, SQUARINGS) as i:
                dve.wait_ge(e_mm, i + TAYLOR)
                dve.wait_ge(e_up, 2 * i + 2 * TAYLOR)
                for x, part in ((Em, 0), (Fm, 1)):
                    dve.scalar_tensor_tensor(out=flat(x), in0=flat(x), scalar=2.0, in1=S2[:, part, :],
                                             op0=ALU.mult, op1=ALU.add).then_inc(e_up, 1)

            vb = ABANK[0]
            with dve.Fori(0, ROT) as j:
                count = [0]

                def own(op):
                    op.then_inc(g_step, 1)
                    count[0] += 1
                    dve.wait_ge(g_step, j * 14 + count[0])

                def col(tile):
                    return tile[:, bass.ds(j, 1)]

                own(dve.scalar_tensor_tensor(out=mk[:, :], in0=G[:, :], scalar=col(eye2), in1=mask[:, bass.ds(ROT - j, D)],
                                             op0=ALU.mult, op1=ALU.mult))
                dve.wait_ge(g_vb, j + 1)
                own(dve.tensor_copy(vs[:, :], vb[:, 0:D]))
                own(dve.tensor_tensor(junk[:, :], vs[:, :], G[:, :], ALU.mult))
                own(dve.tensor_reduce(dot[:, :], junk[:, :], AX.X, ALU.add))
                own(dve.tensor_scalar(q[1][:, :], col(vs), 0.0, 2.0, ALU.is_ge, ALU.mult))
                own(dve.tensor_scalar(col(sg), q[1][:, :], -1.0, house[:, :], ALU.add, ALU.mult))
                dve.wait_ge(g_rt, j + 1)
                own(dve.scalar_tensor_tensor(out=q[2][:, :], in0=n2[:, :], scalar=rt[:, :], in1=col(sg), op0=ALU.mult, op1=ALU.mult))
                own(dve.scalar_tensor_tensor(out=q[3][:, :], in0=col(vs), scalar=q[2][:, :], in1=n2[:, :], op0=ALU.mult, op1=ALU.add))
                own(dve.reciprocal(q[4][:, :], q[3][:, :]))
                own(dve.scalar_tensor_tensor(out=q[5][:, :], in0=col(G), scalar=q[2][:, :], in1=dot[:, :], op0=ALU.mult, op1=ALU.add))
                own(dve.tensor_scalar(q[6][:, :], q[5][:, :], q[4][:, :], col(after), ALU.mult, ALU.mult))
                own(dve.scalar_tensor_tensor(out=G[:, :], in0=vs[:, :], scalar=q[6][:, :], in1=G[:, :], op0=ALU.mult, op1=ALU.add))
                own(dve.tensor_tensor(q[7][:, :], q[6][:, :], q[2][:, :], ALU.mult))
                own(dve.tensor_tensor(col(G), col(G), q[7][:, :], ALU.add))
            assert count[0] == 14
            dve.wait_ge(u_mm, 1)
            end = 14 * ROT
            dve.tensor_tensor(junk[0:ROT, 0:ROT], ABANK[1][0:ROT, 0:ROT], eye2[0:ROT, :], ALU.mult).then_inc(g_step, 1)
            dve.wait_ge(g_step, end + 1)
            dve.tensor_reduce(dot[0:ROT, :], junk[0:ROT, 0:ROT], AX.X, ALU.add).then_inc(g_step, 1)
            dve.wait_ge(u_rt, 1)
            dve.wait_ge(g_step, end + 2)
            dve.scalar_tensor_tensor(out=q[0][0:ROT, :], in0=dot[0:ROT, :], scalar=-1.0, in1=rt[0:ROT, :], op0=ALU.mult, op1=ALU.mult).then_inc(g_step, 1)
            dve.wait_ge(g_step, end + 3)
            dve.tensor_scalar(UT[:, :], G[0:ROT, :], q[0][0:ROT, :], None, ALU.mult).then_inc(g_step, 1)
            dve.wait_ge(u_mm, 2)
            dve.tensor_copy(U[:, :, :], ABANK[0][0:KP, 0:KC * ROT].rearrange("p (k e) -> p k e", k=KC)).then_inc(g_step, 1)

        @block.tensor
        def _(pe):
            pe.wait_ge(silu, 1)
            for i in range(LAYERS):
                pe.wait_ge(wm_in, 16 * (i + 1))
                if i:
                    pe.wait_ge(mod_out, 3 * i)
                for c, part in enumerate((0, 1, 3, 4)):
                    for e in range(KC):
                        for k in range(KC):
                            op = pe.matmul(MBANK[0][0:KP, (3 * c + e) * B:(3 * c + e + 1) * B],
                                           wmod[:, k, part * D + e * KP:part * D + (e + 1) * KP], sT[:, k, :],
                                           start=(k == 0), stop=(k == KC - 1))
                op.then_inc(mod_mm, 1)
                for g, part in enumerate((2, 5)):
                    for k in range(KC):
                        op = pe.matmul(ABANK[g][0:B, 0:D], sT[:, k, :], wmod[:, k, part * D:(part + 1) * D], start=(k == 0), stop=(k == KC - 1))
                op.then_inc(mod_mm, 1)
            for c in range(NJ):
                pe.wait_ge(wr_in[c % 2], 16 * (c // 2 + 1))
                for j in range(WJ):
                    for h in range(2):
                        for k in range(KC):
                            op = pe.matmul(A4[c % 4][h * ROT:(h + 1) * ROT, j * B:(j + 1) * B], wr[:, k, c % 2, j, :], sT[:, k, :],
                                           start=(k == 0), stop=(k == KC - 1))
                op.then_inc(a_mm, 1)
            pe.wait_ge(a_done, 3 * NJ + 1)

            def products(left_e, left_f):
                for x, part, lhs in ((Em, 0, left_e), (Fm, 2, left_f)):
                    for b in range(HB):
                        for h in range(2):
                            rows = slice(h * ROT, (h + 1) * ROT)
                            bank = part + b * ROT // 512
                            at = b * ROT % 512
                            op = pe.matmul(S[rows, bank, at:at + ROT], lhs[rows, b, :], x[rows, b, :], start=True, stop=True)
                return op

            for k in range(TAYLOR - 1, 0, -1):
                pe.wait_ge(e_up, 2 * (TAYLOR - k))
                products(Nm, Bm).then_inc(e_mm, 1)
            with pe.Fori(0, SQUARINGS) as i:
                pe.wait_ge(e_up, 2 * i + 2 * TAYLOR)
                pe.nop(nofuse=True)
                products(Fm, Em).then_inc(e_mm, 1)
            with pe.Fori(0, ROT) as j:
                pe.wait_ge(g_step, j * 14 + 1)
                pe.matmul(ABANK[0][:, 0:D], blockones[:, :], mk[:, :], start=True, stop=True).then_inc(g_vb, 1)
            pe.wait_ge(g_step, 14 * ROT)
            pe.matmul(ABANK[1][:, 0:ROT], house_row[:, :], sg[:, :], start=True, stop=True).then_inc(u_mm, 1)
            pe.wait_ge(g_step, 14 * ROT + 4)
            for k in range(KC):
                op = pe.transpose(ABANK[0][0:KP, k * ROT:(k + 1) * ROT], UT[:, k * KP:(k + 1) * KP], ident[0:ROT, 0:ROT])
            op.then_inc(u_mm, 1)


_LAYER = [
    dict(wmod="w_mod", bmod="b_mod", wqkv="w_qkv", bqkv="b_qkv", gq="g_q", gk="g_k", wo="w_proj", bo="b_proj", w1="w1", b1="b1", w2="w2", b2="b2"),
    dict(wmod="ada_w", bmod="ada_b", wqkv="qkv_w", bqkv="qkv_b", wo="out_w", bo="out_b", w1="w1", b1="b1", w2="w2", b2="b2"),
    dict(wmod="w_ada", bmod="b_ada", wqkv="w_qkv", bqkv="b_qkv", gq="qn_g", bq="qn_b", gk="kn_g", bk="kn_b", wo="w_proj", bo="b_proj", w1="w1", b1="b1", w2="w2", b2="b2"),
]


def kernel(**inputs):
    import concourse.bacc as _bacc
    from concourse.bass_utils import run_bass_kernel_spmd as _run

    nc = _bacc.Bacc("TRN2", target_bir_lowering=False, num_devices=1)
    arrays = {}

    def give(name, a):
        a = np.ascontiguousarray(a)
        name = f"in_{name}_dram"
        arrays[name] = a
        return nc.dram_tensor(name, a.shape, mybir.dt.from_np(a.dtype), kind="ExternalInput").ap()

    t = {"x": give("x", inputs["x"])}
    c = np.asarray(inputs["cond_1152"])
    t["cT"] = give("cT", c.T.reshape(KC, KP, B).transpose(1, 0, 2))
    bm, bg = [], []
    for i, names in enumerate(_LAYER):
        p = f"L{i}_cond_"
        t[i] = {}
        for k, name in names.items():
            a = np.asarray(inputs[p + name])
            if k == "b1":
                t[i]["b1T"] = give(f"L{i}_b1T", a.reshape(FM, P).T)
            elif k == "bmod":
                parts = a.reshape(6, KC, KP)
                bm.append(parts[[0, 1, 3, 4]].reshape(12, KP).T)
                bg.append(parts[[2, 5]].reshape(2 * D))
            else:
                t[i][k] = give(f"L{i}_{k}", a)
    t["bmodT"] = give("bmodT", np.stack(bm, 1))
    t["bgate"] = give("bgate", np.stack(bg))
    t["PT"] = give("PT", np.asarray(inputs["L3_cond_P"]).T)
    iu, ju = np.triu_indices(ROT, k=1)
    at = np.zeros((ROT, ROT), np.int64)
    at[iu, ju] = at[ju, iu] = np.arange(iu.size)
    W = np.asarray(inputs["L3_cond_W"])
    t["wrot"] = give("wrot", W[at.T.ravel()].reshape(ROT, ROT, D).transpose(2, 0, 1))
    t["bfull"] = give("bfull", np.asarray(inputs["L3_cond_b"])[at])
    t["out"] = nc.dram_tensor("out_0_dram", (B, T, D), F32, kind="ExternalOutput").ap()
    build(nc, t)
    r = _run(nc, [arrays], core_ids=[0])
    return r.results[0]["out_0_dram"]
```

```python
from contextlib import ExitStack

import numpy as np

import concourse.bass as bass
from concourse import mybir

F32 = mybir.dt.float32
F32R = mybir.dt.float32r
I32 = mybir.dt.int32
ALU = mybir.AluOpType
ACT = mybir.ActivationFunctionType
AX = mybir.AxisListType

B, T, D = 32, 256, 288
H, HD = 16, 18
F = 4 * D
LAYERS = 3
P = 128
NT = T // P
KC, KP = 3, 96
FM = F // P
PAIRS = H // 2
SLOT = 64
ROT = 64
SQUARINGS, TAYLOR = 9, 6
NEWTON_MAGIC = 0x5F3759DF
QK_EPS = (1e-6, None, 1e-5)

PER_RUN = dict(
    a_x=16, a_g=16, a_st=1, a_ve=1, a_rs=1, a_xn=2, a_xT=2, a_xf=3, a_xh=1, a_xl=1, a_qkv=6, a_qkvd=6,
    a_sq=1, a_nrm=1, a_qs=1, a_qh=1, a_kh=2, a_kl=1, a_T=8, a_qT=4, a_kA=4, a_kB=4, a_S=16, a_mx=8,
    a_nm=1, a_T2=4, a_q2a=2, a_q2d=2, a_ex=8, a_pv=8, a_o=2, a_oT=2, a_on=2, a_nT=2, a_oh=2, a_ol=2,
    a_pr=2, a_prd=2, a_gb=1, a_xa=1, a_x1=2, a_warm=2,
    m_g=16, m_bn=2, m_st=1, m_ve=1, m_rs=1, m_xn=2, m_gb=1, m_xb=1, m_xT=2, m_xf=3, m_xh=3, m_xl=1, m_h=5,
    m_hf=5, m_hh=5, m_hl=5, m_y=2, m_x2=2, m_out=16, m_mod=1, a_mod=1,
    r_e=16, r_T=2, r_x=2, r_z=1, r_zs=1, r_y=1, r_ys=1, r_o=2, r_x3=2,
)


def upto(name, run, k):
    return run * PER_RUN[name] + k


def build(nc, t):
    with ExitStack() as ctx:
        def sb(name, shape, dt=F32, at=ctx):
            return at.enter_context(nc.sbuf_tensor(name, shape, dt))

        def ps(name, shape):
            return ctx.enter_context(nc.psum_tensor(name, shape, F32))

        def sem(name):
            return ctx.enter_context(nc.semaphore(name))

        s = {name: sem(name) for name in PER_RUN}

        def wait(eng, name, run, k):
            value = upto(name, run, k)
            if not (isinstance(value, int) and value <= 0):
                eng.wait_ge(s[name], value)

        S = ps("S", [P, 4, 512])
        ABANK = [ps("A0", [P, 512]), ps("A1", [P, 512])]
        MBANK = [ps("M0", [P, 512]), ps("M1", [P, 512])]

        ident = sb("ident", [P, P])
        modT = sb("modT", [KP, LAYERS, 12, B])
        U = sb("U", [KP, KC, ROT])
        UT = sb("UT", [ROT, D])
        mhalf = sb("mhalf", [P, 2])

        gates = nc.dram_tensor("gates", (LAYERS, B, 2 * D), F32, kind="Internal").ap()
        expm = nc.dram_tensor("expm", (B, ROT, ROT), F32, kind="Internal").ap()
        mid = [nc.dram_tensor(f"mid{i}", (B, T, D), F32, kind="Internal").ap() for i in range(2)]

        preamble(nc, t, sem, S, ABANK, MBANK, ident, modT, U, UT, mhalf, gates, expm)

        wqkv = [sb(f"wqkv_{h}", [KP, KC, 3 * D], F32R) for h in ("hi", "lo")]
        wo = [sb(f"wo_{h}", [KP, KC, D], F32R) for h in ("hi", "lo")]
        w1 = [sb(f"w1_{h}", [KP, KC, F], F32R) for h in ("hi", "lo")]
        w2 = [sb(f"w2_{h}", [P, FM, D], F32R) for h in ("hi", "lo")]
        bqkv = sb("bqkv", [P, 3 * D])
        gam = sb("gam", [P, 2 * HD])
        bet = sb("bet", [P, 2 * HD])
        bo = sb("bo", [P, D])
        b2 = sb("b2", [P, D])
        b1T = sb("b1T", [P, FM])
        xld = sb("xld", [P, NT, D])
        xa = sb("xa", [P, NT, D])
        xn = sb("xn", [P, NT, D])
        gA = sb("gA", [P, D])
        gbA = sb("gbA", [P, D])
        amod = sb("amod", [KP, 6])
        oraw = sb("oraw", [P, 4, T])
        xf = oraw[0:KP, 0:3, :]
        xh = sb("xh", [KP, KC, T], F32R)
        xl = sb("xl", [KP, KC, T], F32R)
        qs = sb("qs", [P, NT, H, SLOT], F32R)
        ks = sb("ks", [P, NT, H, SLOT], F32R)
        V = sb("V", [P, NT, H, 32])
        qT = sb("qT", [P, PAIRS, T], F32R)
        oh, ol = (qT[0:KP, KC * i:KC * i + KC, :] for i in range(2))
        kz = [sb(f"kz{a}", [P, PAIRS, T], F32R) for a in range(2)]
        pT = sb("pT", [P, 3, 2, 512])
        flat = pT[:, :, :, :].rearrange("p s a c -> p (s a c)")
        qk = flat[:, 0:NT * 2 * D].rearrange("p (t c) -> p t c", t=NT)
        sq = flat[:, NT * 2 * D:2 * NT * 2 * D]
        on = flat[:, 4 * NT * D:5 * NT * D].rearrange("p (t d) -> p t d", t=NT)
        wst = flat[:, 0:2 * F].rearrange("p (r c) -> p r c", r=2)
        mx = sb("mx", [P, PAIRS, 2, NT])
        nmx = sb("nmx", [P, PAIRS, 2, NT])
        stA = sb("stA", [P, NT, 6])
        mvA = sb("mvA", [P, NT, 2])
        rsA = sb("rsA", [P, NT])
        veA = sb("veA", [P, NT])
        sm = sb("sm", [P, 64])
        nv = sb("nv", [P, 64])
        na = sb("na", [P, 64])
        ny = sb("ny", [P, 64])
        rden = sb("rden", [P, NT, H])
        warm = sb("warm", [P, 2])
        x1 = sb("x1", [P, NT, D])
        xb = sb("xb", [P, NT, D])
        xo = sb("xo", [P, NT, D])
        gM = sb("gM", [P, D])
        gbM = sb("gbM", [P, D])
        mmod = sb("mmod", [KP, 6])
        hf = sb("hf", [P, 2, 512])
        xf2 = hf[0:KP, :, :].rearrange("p r c -> p (r c)")[:, 0:KC * T].rearrange("p (c n) -> p c n", c=KC)
        xh2 = sb("xh2", [KP, KC, T], F32R)
        xl2 = sb("xl2", [KP, KC, T], F32R)
        hh = sb("hh", [P, FM, T], F32R)
        hl = sb("hl", [P, FM, T], F32R)
        stM = sb("stM", [P, NT, 6])
        mvM = sb("mvM", [P, NT, 2])
        rsM = sb("rsM", [P, NT])
        veM = sb("veM", [P, NT])
        eb = sb("eb", [ROT, ROT])
        zT = sb("zT", [ROT, T])
        yT = sb("yT", [ROT, T])

        w_in = [sem("w_in0"), sem("w_in1")]
        w_hi = sem("w_hi")
        w_lo = sem("w_lo")
        p_in = sem("p_in")
        w_mean = sem("w_mean")
        w_step = sem("w_step")
        set_done = sem("set_done")
        dve_step = sem("dve_step")

        def chunks(layer):
            w = t[layer]
            out = [(w["wqkv"].rearrange("(k p) n -> p k n", p=KP)[:, k, :], KP, 3 * D,
                    [x[:, k, :] for x in wqkv]) for k in range(KC)]
            out += [(w["wo"].rearrange("(k p) n -> p k n", p=KP)[:, k, :], KP, D,
                     [x[:, k, :] for x in wo]) for k in range(KC)]
            out += [(w["w1"].rearrange("(k p) n -> p k n", p=KP)[:, k, :], KP, F,
                     [x[:, k, :] for x in w1]) for k in range(KC)]
            out += [(w["w2"].rearrange("(k p) n -> p k n", p=P)[:, 3 * k:3 * k + 3, :], P, 3 * D,
                     [x[:, 3 * k:3 * k + 3, :].rearrange("p k n -> p (k n)") for x in w2]) for k in range(FM // 3)]
            return out

        NCH = 4 * KC

        def constant_wait(eng):
            eng.nop(nofuse=True)

        steps = [0]
        w_steps = [0]
        means = [0]

        for layer in range(LAYERS):
            first, last = layer * B, layer * B + B
            src = t["x"] if layer == 0 else mid[layer - 1]
            dst = t["out"] if layer == LAYERS - 1 else mid[layer]
            start = first + (1 if layer == 1 else 2)
            rot = layer == LAYERS - 1
            eps = QK_EPS[layer]
            w = t[layer]

            def qk_run(n):
                return n - B if layer == 2 else n

            def wait_normed(eng, n):
                if eps is None:
                    wait(eng, "a_qkvd", n, 6)
                else:
                    wait(eng, "a_nrm", qk_run(n), 1)

            def slots(eng, slot):
                slot(None, None, first)
                slot(first, None, first + 1)
                if start > first + 1:
                    slot(first + 1, first, first + 2)
                with eng.Fori(start, last - 1) as n:
                    slot(n, n - 1, n + 1)
                slot(last - 1, last - 2, None)
                slot(None, last - 1, None)

            with ExitStack() as lc:
                block = lc.enter_context(nc.Block())

                @block.sync
                def _(sp):
                    for c, (ap, rows, cols, _) in enumerate(chunks(layer)):
                        n = layer * NCH + c
                        if c >= 2:
                            sp.wait_ge(w_lo, n - 1)
                        to = wst[0:rows, c % 2, 0:cols]
                        if len(ap.shape) == 3:
                            to = to.rearrange("p (k n) -> p k n", k=ap.shape[1])
                        sp.dma_start(to, ap).then_inc(w_in[c % 2], 16)

                    def load_x(n):
                        wait(sp, "a_xn", n, 0)
                        wait(sp, "a_xa", n, 0)
                        sp.dma_start(xld[:, :, :], src[n - first].rearrange("(t p) d -> p t d", p=P)).then_inc(s["a_x"], 16)

                    def load_gA(n):
                        wait(sp, "a_x1", n, 0)
                        sp.dma_start(gA[:, :], gates[layer, n - first, 0:D].partition_broadcast(P)).then_inc(s["a_g"], 16)

                    def load_gM(n):
                        wait(sp, "m_x2", n, 0)
                        sp.dma_start(gM[:, :], gates[layer, n - first, D:2 * D].partition_broadcast(P)).then_inc(s["m_g"], 16)
                        if rot:
                            wait(sp, "r_y", n - first, 0)
                            sp.dma_start(eb[:, :], expm[n - first]).then_inc(s["r_e"], 16)

                    def store(n):
                        if rot:
                            wait(sp, "r_x3", n - first, 2)
                        else:
                            wait(sp, "m_x2", n, 2)
                        sp.dma_start(dst[n - first].rearrange("(t p) d -> p t d", p=P), xo[:, :, :]).then_inc(s["m_out"], 16)

                    def slot(a, m, p):
                        if a is not None:
                            load_gA(a)
                        if m is not None:
                            load_gM(m)
                        if p is not None:
                            load_x(p)
                        if m is not None:
                            store(m)

                    slots(sp, slot)
                    sp.wait_ge(s["m_out"], upto("m_out", last, 0))

                @block.gpsimd
                def _(pool):
                    if layer == 0:
                        pool.memset(qs[:, :, :, :].bitcast(F32), 0.0).then_inc(set_done, 1)
                        pool.memset(ks[:, :, :, :].bitcast(F32), 0.0).then_inc(set_done, 1)
                        pool.memset(V[:, :, :, :], 0.0).then_inc(set_done, 1)
                        for a in range(2):
                            pool.memset(kz[a][:, :, :].bitcast(F32), 0.0).then_inc(set_done, 1)
                        pool.wait_ge(set_done, 5)
                        pool.memset(ks[:, :, :, 0:2].bitcast(F32), 1.0).then_inc(set_done, 1)
                        pool.memset(V[:, :, :, 0:1], 1.0).then_inc(set_done, 1)
                    for to, ap in ((bqkv[:, :], w["bqkv"].partition_broadcast(P)), (bo[:, :], w["bo"].partition_broadcast(P)),
                                   (b2[:, :], w["b2"].partition_broadcast(P)), (b1T[:, :], w["b1T"])):
                        pool.dma_start(to, ap).then_inc(p_in, 16)
                    n_par = 4
                    if eps is not None:
                        pool.dma_start(gam[:, 0:HD], w["gq"].partition_broadcast(P)).then_inc(p_in, 16)
                        pool.dma_start(gam[:, HD:2 * HD], w["gk"].partition_broadcast(P)).then_inc(p_in, 16)
                        n_par += 2
                    if rot:
                        pool.dma_start(bet[:, 0:HD], w["bq"].partition_broadcast(P)).then_inc(p_in, 16)
                        pool.dma_start(bet[:, HD:2 * HD], w["bk"].partition_broadcast(P)).then_inc(p_in, 16)
                        n_par += 2
                    par = [6, 10, 18][layer]
                    assert par == [0, 6, 10][layer] + n_par
                    pool.wait_ge(p_in, 16 * par)

                    def A_mod(n):
                        wait(pool, "a_xf", n, 0)
                        pool.tensor_copy(amod[:, :], modT[:, layer, 0:6, bass.ds(n - first, 1)].rearrange("p c b -> p (c b)")).then_inc(s["a_mod"], 1)

                    def M_mod(n):
                        wait(pool, "m_xf", n, 0)
                        pool.tensor_copy(mmod[:, :], modT[:, layer, 6:12, bass.ds(n - first, 1)].rearrange("p c b -> p (c b)")).then_inc(s["m_mod"], 1)

                    def A_rstd(n):
                        wait(pool, "a_xn", n, 0)
                        wait(pool, "a_st", n, 1)
                        constant_wait(pool)
                        pool.tensor_scalar(veA[:, :], mvA[:, :, 1], 1.0, 1e-6, ALU.mult, ALU.add).then_inc(s["a_ve"], 1)
                        wait(pool, "a_ve", n, 1)
                        pool.tensor_tensor(rsA[:, :], veA[:, :], mhalf[:, :], ALU.pow).then_inc(s["a_rs"], 1)

                    def M_rstd(n):
                        wait(pool, "m_xn", n, 0)
                        wait(pool, "m_st", n, 1)
                        constant_wait(pool)
                        pool.tensor_scalar(veM[:, :], mvM[:, :, 1], 1.0, 1e-6, ALU.mult, ALU.add).then_inc(s["m_ve"], 1)
                        wait(pool, "m_ve", n, 1)
                        pool.tensor_tensor(rsM[:, :], veM[:, :], mhalf[:, :], ALU.pow).then_inc(s["m_rs"], 1)

                    def A_xh(n):
                        wait(pool, "a_qkv", n, 0)
                        wait(pool, "a_xf", n, 3)
                        constant_wait(pool)
                        pool.tensor_scalar(xh[:, :, :], xf, 1.0, 0.0, ALU.mult, ALU.add).then_inc(s["a_xh"], 1)

                    def M_xh(n):
                        wait(pool, "m_h", n, 0)
                        for c in range(KC):
                            wait(pool, "m_xf", n, c + 1)
                            constant_wait(pool)
                            pool.tensor_scalar(xh2[:, c, :], xf2[:, c, :], 1.0, 0.0, ALU.mult, ALU.add).then_inc(s["m_xh"], 1)

                    def A_residual(n):
                        wait(pool, "a_g", n, 16)
                        wait(pool, "a_x", n, 16)
                        wait(pool, "a_x1", n, 0)
                        pool.tensor_tensor(gbA[:, :], gA[:, :], bo[:, :], ALU.mult).then_inc(s["a_gb"], 1)
                        wait(pool, "a_gb", n, 1)
                        pool.tensor_tensor(xa[:, :, :], xld[:, :, :], gbA[:, :].unsqueeze(1).broadcast_to([P, NT, D]), ALU.add).then_inc(s["a_xa"], 1)

                    def M_residual(n):
                        wait(pool, "m_g", n, 16)
                        wait(pool, "m_x2", n, 0)
                        wait(pool, "a_x1", n, 2)
                        pool.tensor_tensor(gbM[:, :], gM[:, :], b2[:, :], ALU.mult).then_inc(s["m_gb"], 1)
                        wait(pool, "m_gb", n, 1)
                        pool.tensor_tensor(xb[:, :, :], x1[:, :, :], gbM[:, :].unsqueeze(1).broadcast_to([P, NT, D]), ALU.add).then_inc(s["m_xb"], 1)

                    def M_hh(n, f):
                        wait(pool, "m_y", n, 0)
                        wait(pool, "m_hf", n, f + 1)
                        m = min(2, FM - 2 * f)
                        constant_wait(pool)
                        pool.tensor_scalar(hh[:, 2 * f:2 * f + m, :].rearrange("p m c -> p (m c)"), hf[:, f % 2, 0:m * T],
                                           1.0, 0.0, ALU.mult, ALU.add).then_inc(s["m_hh"], 1)

                    def slot(a, m, p):
                        if m is not None:
                            M_mod(m)
                            M_rstd(m)
                        if a is not None:
                            A_residual(a)
                        if m is not None:
                            M_xh(m)
                            M_residual(m)
                        if p is not None:
                            A_mod(p)
                        if m is not None:
                            for f in range(5):
                                M_hh(m, f)
                        if p is not None:
                            A_rstd(p)
                            A_xh(p)

                    slots(pool, slot)

                @block.scalar
                def _(act):
                    for c, (_, rows, cols, to) in enumerate(chunks(layer)):
                        act.wait_ge(w_in[c % 2], 16 * (layer * NCH // 2 + c // 2 + 1))
                        if c < KC and eps is not None:
                            act.wait_ge(w_mean, means[0] + c + 1)
                        act.activation(to[0], wst[0:rows, c % 2, 0:cols], ACT.Identity).then_inc(w_hi, 1)
                    act.wait_ge(p_in, 16 * [6, 10, 18][layer])

                    def M_xf(n):
                        wait(act, "m_mod", n, 1)
                        wait(act, "m_hl", n, 0)
                        for c in range(KC):
                            if c != 1:
                                wait(act, "m_xT", n, c // 2 + 1)
                            act.activation(xf2[:, c, :], MBANK[c // 2][0:KP, (c % 2) * T:(c % 2 + 1) * T], ACT.Identity,
                                           bias=mmod[:, c:c + 1], scale=mmod[:, 3 + c:4 + c]).then_inc(s["m_xf"], 1)

                    def M_gelu(n, f):
                        wait(act, "m_h", n, f + 1)
                        if f == 0:
                            wait(act, "m_xl", n, 1)
                        if f >= 2:
                            wait(act, "m_hl", n, f - 1)
                        for i in range(min(2, FM - 2 * f)):
                            op = act.activation(hf[:, f % 2, i * T:(i + 1) * T], MBANK[f % 2][:, i * T:(i + 1) * T],
                                                ACT.Gelu if rot else ACT.Gelu_apprx_tanh, bias=b1T[:, 2 * f + i:2 * f + i + 1])
                        op.then_inc(s["m_hf"], 1)

                    def A_square(n):
                        wait(act, "a_qkvd", n, 4)
                        act.activation(sq, qk.rearrange("p t c -> p (t c)"), ACT.Square).then_inc(s["a_sq"], 1)

                    def A_hi(n):
                        wait(act, "a_T", n, 0)
                        wait_normed(act, n)
                        for i in range(NT):
                            kv = qk[:, i, D:2 * D].rearrange("p (h d) -> p h d", h=H)
                            op = act.activation(ks[:, i, :, 2:2 + HD], kv, ACT.Identity)
                        op.then_inc(s["a_kh"], 1)
                        wait(act, "a_T2", n, 0)
                        for i in range(NT):
                            qv = qk[:, i, 0:D].rearrange("p (h d) -> p h d", h=H)
                            op = act.activation(qs[:, i, :, 2 + HD:2 + 2 * HD], qv, ACT.Identity)
                        op.then_inc(s["a_qh"], 1)
                        for i in range(NT):
                            kv = qk[:, i, D:2 * D].rearrange("p (h d) -> p h d", h=H)
                            op = act.activation(ks[:, i, :, 2 + 2 * HD:2 + 3 * HD], kv, ACT.Identity)
                        op.then_inc(s["a_kh"], 1)

                    def A_turned(n, f):
                        if f == 0:
                            wait(act, "a_S", n, 0)
                            wait(act, "a_pr", n, 0)
                        wait(act, "a_T", n, 2 * f + 1)
                        act.activation(qT[:, 2 * f:2 * f + 2, :].rearrange("p m c -> p (m c)"), ABANK[0][:, :], ACT.Identity).then_inc(s["a_qT"], 1)
                        wait(act, "a_T", n, 2 * f + 2)
                        act.activation(kz[0][0:SLOT, 2 * f:2 * f + 2, :].rearrange("p m c -> p (m c)"), ABANK[1][0:SLOT, :],
                                       ACT.Identity).then_inc(s["a_kA"], 1)
                        act.activation(kz[1][SLOT:P, 2 * f:2 * f + 2, :].rearrange("p m c -> p (m c)"), ABANK[1][SLOT:P, :],
                                       ACT.Identity).then_inc(s["a_kB"], 1)

                    def A_turned2(n, f):
                        wait(act, "a_T2", n, f + 1)
                        act.activation(qT[:, 2 * f:2 * f + 2, :].rearrange("p m c -> p (m c)"), ABANK[f % 2][:, :], ACT.Identity).then_inc(s["a_q2a"], 1)

                    def load_table(n, i, function):
                        wait(act, "a_warm", n, i)
                        act.activation(warm[:, i:i + 1], mhalf[:, 0:1], function).then_inc(s["a_warm"], 1)

                    def A_exp(n, p):
                        if p >= 3:
                            wait(act, "a_pv", n, p - 2)
                        wait(act, "a_S", n, PAIRS + p + 1)
                        r = 2 * (p % 2)
                        act.activation(pT[:, p % 3, :, :], S[:, r:r + 2, :], ACT.Exp, scale=float(HD) ** -0.5).then_inc(s["a_ex"], 1)

                    def A_ohi(n):
                        wait(act, "a_nT", n, 1)
                        act.activation(oh[:, 0:2, :].rearrange("p m c -> p (m c)"), ABANK[0][0:KP, :], ACT.Identity).then_inc(s["a_oh"], 1)
                        wait(act, "a_nT", n, 2)
                        act.activation(oh[:, 2, :], ABANK[1][0:KP, 0:T], ACT.Identity).then_inc(s["a_oh"], 1)

                    def R_x(n):
                        b = n - first
                        wait(act, "r_T", b, 1)
                        act.activation(xf2[:, 0:2, :].rearrange("p m c -> p (m c)"), MBANK[1][0:KP, :], ACT.Identity).then_inc(s["r_x"], 1)
                        wait(act, "r_T", b, 2)
                        act.activation(xf2[:, 2, :], MBANK[0][0:KP, 0:T], ACT.Identity).then_inc(s["r_x"], 1)

                    def R_z(n):
                        wait(act, "r_z", n - first, 1)
                        act.activation(zT[:, :], MBANK[1][0:ROT, 0:T], ACT.Identity).then_inc(s["r_zs"], 1)

                    def R_y(n):
                        wait(act, "r_y", n - first, 1)
                        act.activation(yT[:, :], MBANK[0][0:ROT, 0:T], ACT.Identity).then_inc(s["r_ys"], 1)

                    def slot(a, m, p):
                        if a is not None and eps is not None:
                            A_square(a)
                        if m is not None:
                            M_xf(m)
                        if a is not None and eps is None:
                            A_hi(a)
                        late = a is not None and eps is None
                        if m is not None:
                            for f in range(2 if late else 5 if rot else 4):
                                M_gelu(m, f)
                        if a is not None and eps is not None:
                            A_hi(a)
                        if m is not None and not late and not rot:
                            M_gelu(m, 4)
                        if a is not None:
                            for f in range(4):
                                if m is not None and late and f >= 1:
                                    M_gelu(m, f + 1)
                                A_turned(a, f)
                            load_table(a, 0, ACT.Exp)
                            A_turned2(a, 0)
                            A_turned2(a, 2)
                            for i in range(PAIRS):
                                A_exp(a, i)
                                if m is not None and rot:
                                    if i == 4:
                                        R_x(m)
                                    if i == 6:
                                        R_z(m)
                                    if i == 7:
                                        R_y(m)
                        elif rot and m is not None:
                            R_x(m)
                            R_z(m)
                            R_y(m)
                        if a is not None:
                            load_table(a, 1, ACT.Gelu if rot else ACT.Gelu_apprx_tanh)
                            A_ohi(a)

                    slots(act, slot)

                @block.vector
                def _(dve):
                    def weight_step(op):
                        op.then_inc(w_step, 1)
                        w_steps[0] += 1
                        dve.wait_ge(w_step, w_steps[0])

                    def center(columns, rows):
                        by_head = columns.rearrange("p (h d) -> p h d", d=HD)
                        weight_step(dve.tensor_reduce(sm[0:rows, 0:2 * H], by_head, AX.X, ALU.add))
                        weight_step(dve.tensor_scalar(sm[0:rows, 0:2 * H], sm[0:rows, 0:2 * H], -1.0 / HD, None, ALU.mult))
                        weight_step(dve.tensor_tensor(by_head, by_head, sm[0:rows, 0:2 * H].unsqueeze(2).broadcast_to([rows, 2 * H, HD]), ALU.add))

                    def center_chunk(c):
                        dve.wait_ge(w_in[c % 2], 16 * (layer * NCH // 2 + c // 2 + 1))
                        center(wst[0:KP, c % 2, 0:2 * D], KP)
                        dve.sem_inc(w_mean, 1)

                    if eps is not None:
                        center_chunk(0)
                    for c, (_, rows, cols, to) in enumerate(chunks(layer)):
                        if eps is not None and 1 <= c + 1 < KC:
                            center_chunk(c + 1)
                        dve.wait_ge(w_hi, layer * NCH + c + 1)
                        dve.tensor_tensor(to[1], wst[0:rows, c % 2, 0:cols], to[0].bitcast(F32), ALU.subtract).then_inc(w_lo, 1)
                    if layer == 0:
                        dve.wait_ge(set_done, 7)
                    dve.wait_ge(p_in, 16 * [6, 10, 18][layer])
                    if eps is not None:
                        means[0] += KC
                        center(bqkv[:, 0:2 * D], P)
                        if not rot:
                            weight_step(dve.tensor_tensor(gam[:, 0:HD], gam[:, 0:HD], gam[:, HD:2 * HD], ALU.mult))

                    STEPS_P = 1
                    STEPS_A = 4 + (14 if eps is not None else 0) + (1 if rot else 0)
                    STEPS_M = 2
                    base = steps[0]
                    state = {}

                    def own(op):
                        op.then_inc(dve_step, 1)
                        state["k"] += 1
                        dve.wait_ge(dve_step, state["from"] + state["k"])

                    def A_stats(n):
                        wait(dve, "a_x", n, 16)
                        wait(dve, "a_rs", n, 0)
                        for i in range(NT):
                            op = dve.bn_stats(stA[:, i, :], xld[:, i, :])
                        own(op)
                        constant_wait(dve)
                        for i in range(NT):
                            op = dve.bn_aggr(mvA[:, i, :], stA[:, i, :])
                        op.then_inc(s["a_st"], 1)

                    def M_stats(n):
                        wait(dve, "m_bn", n, 2)
                        wait(dve, "m_rs", n, 0)
                        constant_wait(dve)
                        for i in range(NT):
                            op = dve.bn_aggr(mvM[:, i, :], stM[:, i, :])
                        op.then_inc(s["m_st"], 1)

                    def A_norm(n):
                        wait(dve, "a_st", n, 1)
                        wait(dve, "a_xT", n, 0)
                        wait(dve, "a_rs", n, 1)
                        for i in range(NT):
                            dve.tensor_scalar(xn[:, i, :], xld[:, i, :], mvA[:, i, 0:1], rsA[:, i:i + 1],
                                              ALU.subtract, ALU.mult).then_inc(s["a_xn"], 1)

                    def M_norm(n):
                        wait(dve, "m_st", n, 1)
                        wait(dve, "m_out", n, 0)
                        wait(dve, "m_rs", n, 1)
                        for i in range(NT):
                            dve.tensor_scalar(xo[:, i, :], x1[:, i, :], mvM[:, i, 0:1], rsM[:, i:i + 1],
                                              ALU.subtract, ALU.mult).then_inc(s["m_xn"], 1)

                    def A_xf(n, c):
                        if c == 0:
                            wait(dve, "a_mod", n, 1)
                            wait(dve, "a_oT", n - 1, 0)
                        if c != 1:
                            wait(dve, "a_xT", n, c // 2 + 1)
                        dve.tensor_scalar(xf[:, c, :], MBANK[1][0:KP, (c % 2) * T:(c % 2 + 1) * T], amod[:, 3 + c:4 + c],
                                          amod[:, c:c + 1], ALU.mult, ALU.add).then_inc(s["a_xf"], 1)

                    def A_xl(n):
                        wait(dve, "a_qkv", n, 0)
                        wait(dve, "a_xh", n, 1)
                        dve.tensor_tensor(xl[:, :, :], xf, xh[:, :, :].bitcast(F32), ALU.subtract).then_inc(s["a_xl"], 1)

                    def M_xl(n):
                        wait(dve, "m_h", n, 0)
                        wait(dve, "m_xh", n, 3)
                        dve.tensor_tensor(xl2[:, :, :], xf2, xh2[:, :, :].bitcast(F32), ALU.subtract).then_inc(s["m_xl"], 1)

                    def A_qkv(n, fills):
                        if fills[0] == 0:
                            wait(dve, "a_pv", n, 0)
                        for f in fills:
                            wait(dve, "a_qkv", n, f + 1)
                            i, part = (f // 2, f % 2) if f < 4 else (f - 4, 2)
                            to = qk[:, i, part * D:(part + 1) * D] if part < 2 else V[:, i, :, 1:1 + HD]
                            a, b = S[:, f % 4, 0:D], bqkv[:, part * D:(part + 1) * D]
                            if part == 2:
                                a, b = (z.rearrange("p (h d) -> p h d", h=H) for z in (a, b))
                            dve.tensor_tensor(to, a, b, ALU.add).then_inc(s["a_qkvd"], 1)

                    heads = qk.rearrange("p t c -> p (t c)").rearrange("p (g d) -> p g d", d=HD)

                    def A_heads_sum(n):
                        wait(dve, "a_sq", qk_run(n), 1)
                        own(dve.tensor_reduce(nv[:, :], sq.rearrange("p (g d) -> p g d", d=HD), AX.X, ALU.add))

                    def A_heads_rstd(n):
                        own(dve.tensor_scalar(nv[:, :], nv[:, :], 1.0 / HD, eps, ALU.mult, ALU.add))
                        own(dve.tensor_scalar(ny[:, :].bitcast(I32), nv[:, :].bitcast(I32), 1, None, ALU.logical_shift_right))
                        own(dve.tensor_scalar(ny[:, :].bitcast(I32), ny[:, :].bitcast(I32), -1.0, float(NEWTON_MAGIC), ALU.mult, ALU.add))
                        for _ in range(3):
                            own(dve.scalar_tensor_tensor(out=na[:, :], in0=ny[:, :], scalar=-0.5, in1=ny[:, :], op0=ALU.mult, op1=ALU.mult))
                            own(dve.tensor_tensor(na[:, :], na[:, :], nv[:, :], ALU.mult))
                            own(dve.scalar_tensor_tensor(out=ny[:, :], in0=na[:, :], scalar=1.5, in1=ny[:, :], op0=ALU.add, op1=ALU.mult))

                    def A_heads_norm(n, m):
                        own(dve.tensor_tensor(heads, heads, ny[:, :].unsqueeze(2).broadcast_to([P, 64, HD]), ALU.mult))
                        if m is not None:
                            M_hl(m, 1)
                        for table, op in ((gam, ALU.mult),) + (((bet, ALU.add),) if rot else ()):
                            parts = 2 if rot else 1
                            for j in range(NT):
                                part = qk[:, j, 0:parts * D].rearrange("p (x h d) -> p x h d", h=H, d=HD)
                                step = dve.tensor_tensor(part, part, table[:, 0:parts * HD].rearrange("p (x d) -> p x d", d=HD)
                                                         .unsqueeze(2).broadcast_to([P, parts, H, HD]), op)
                            if table is (bet if rot else gam):
                                step.then_inc(s["a_nrm"], 1)
                                wait(dve, "a_nrm", qk_run(n), 1)
                            else:
                                own(step)
                                if m is not None:
                                    M_hl(m, 2)

                    def A_halves(n):
                        wait(dve, "a_T2", n, 0)
                        wait(dve, "a_qkvd", n, 6)
                        dve.memset(qs[:, :, :, 0:2].bitcast(F32), 0.0)
                        for i in range(NT):
                            qv = qk[:, i, 0:D].rearrange("p (h d) -> p h d", h=H)
                            op = dve.tensor_copy(qs[:, i, :, 2:2 + HD], qv)
                        own(op)
                        for i in range(NT):
                            qv = qk[:, i, 0:D].rearrange("p (h d) -> p h d", h=H)
                            op = dve.tensor_tensor(qs[:, i, :, 2 + 2 * HD:2 + 3 * HD], qv, qs[:, i, :, 2:2 + HD].bitcast(F32), ALU.subtract)
                        op.then_inc(s["a_qs"], 1)
                        wait(dve, "a_kh", n, 1)
                        wait(dve, "a_T", n, 0)
                        for i in range(NT):
                            op = dve.tensor_tensor(
                                ks[:, i, :, 2 + HD:2 + 2 * HD], qk[:, i, D:2 * D].rearrange("p (h d) -> p h d", h=H),
                                ks[:, i, :, 2:2 + HD].bitcast(F32), ALU.subtract)
                        op.then_inc(s["a_kl"], 1)

                    def M_hl(n, f):
                        wait(dve, "m_hh", n, f + 1)
                        m = min(2, FM - 2 * f)
                        dve.tensor_tensor(hl[:, 2 * f:2 * f + m, :].rearrange("p m c -> p (m c)"), hf[:, f % 2, 0:m * T],
                                          hh[:, 2 * f:2 * f + m, :].rearrange("p m c -> p (m c)").bitcast(F32),
                                          ALU.subtract).then_inc(s["m_hl"], 1)

                    def A_max(n, p):
                        wait(dve, "a_S", n, p + 1)
                        if p == 0:
                            wait(dve, "a_nm", n, 0)
                        r = 2 * (p % 2)
                        dve.tensor_reduce(mx[:, p, :, :], S[:, r:r + 2, :].rearrange("p a (t k) -> p a t k", t=NT),
                                          AX.X, ALU.max).then_inc(s["a_mx"], 1)

                    def A_negmax(n):
                        wait(dve, "a_T", n, 8)
                        wait(dve, "a_mx", n, PAIRS)
                        own(dve.tensor_scalar(nmx[:, :, :, :], mx[:, :, :, :], -1.0, None, ALU.mult))
                        view = nmx[:, :, :, :].rearrange("p q a t -> p t (q a)")
                        own(dve.tensor_copy(qs[:, :, :, 0], view))
                        dve.tensor_tensor(qs[:, :, :, 1], view, qs[:, :, :, 0].bitcast(F32), ALU.subtract).then_inc(s["a_nm"], 1)

                    def A_turned2(n, f):
                        wait(dve, "a_T2", n, f + 1)
                        dve.tensor_copy(qT[:, 2 * f:2 * f + 2, :].rearrange("p m c -> p (m c)"), ABANK[f % 2][:, :]).then_inc(s["a_q2d"], 1)

                    def A_oraw(n, p, i):
                        if i == 0 and p is not None:
                            wait(dve, "a_xl", p, 1)
                        wait(dve, "a_pv", n, 4 * i + 4)
                        dve.tensor_copy(oraw[:, 2 * i:2 * i + 2, :].rearrange("p m c -> p (m c)"), ABANK[i][:, :]).then_inc(s["a_o"], 1)

                    def A_out(n):
                        for i in range(NT):
                            wait(dve, "a_oT", n, i + 1)
                            op = dve.reciprocal(rden[:, i, :], ABANK[i][:, :].rearrange("p (h d) -> p h d", h=H)[:, :, 0])
                        own(op)
                        for i in range(NT):
                            v = ABANK[i][:, :].rearrange("p (h d) -> p h d", h=H)
                            dve.tensor_tensor(on[:, i, :].rearrange("p (h d) -> p h d", h=H), v[:, :, 1:1 + HD],
                                              rden[:, i, :].unsqueeze(2).broadcast_to([P, H, HD]), ALU.mult).then_inc(s["a_on"], 1)

                    def A_olo(n):
                        wait(dve, "a_oh", n, 1)
                        dve.tensor_tensor(ol[:, 0:2, :].rearrange("p m c -> p (m c)"), ABANK[0][0:KP, :],
                                          oh[:, 0:2, :].rearrange("p m c -> p (m c)").bitcast(F32), ALU.subtract).then_inc(s["a_ol"], 1)
                        wait(dve, "a_oh", n, 2)
                        dve.tensor_tensor(ol[:, 2, :], ABANK[1][0:KP, 0:T], oh[:, 2, :].bitcast(F32), ALU.subtract).then_inc(s["a_ol"], 1)

                    def A_x1(n):
                        wait(dve, "a_xa", n, 1)
                        wait(dve, "m_xb", n, 0)
                        wait(dve, "m_xn", n, 0)
                        wait(dve, "m_st", n, 0)
                        for i in range(NT):
                            wait(dve, "a_pr", n, i + 1)
                            dve.tensor_tensor(x1[:, i, :], ABANK[i][:, 0:D], gA[:, :], ALU.mult).then_inc(s["a_prd"], 1)
                            wait(dve, "a_prd", n, i + 1)
                            dve.tensor_tensor(x1[:, i, :], x1[:, i, :], xa[:, i, :], ALU.add).then_inc(s["a_x1"], 1)
                            wait(dve, "a_x1", n, i + 1)
                            constant_wait(dve)
                            dve.bn_stats(stM[:, i, :], x1[:, i, :]).then_inc(s["m_bn"], 1)

                    def M_x2(n, i):
                        if i == 0:
                            wait(dve, "m_xb", n, 1)
                            wait(dve, "m_xT", n, 2)
                        wait(dve, "m_y", n, i + 1)
                        own(dve.tensor_tensor(xo[:, i, :], MBANK[1 - i][:, 0:D], gM[:, :], ALU.mult))
                        dve.tensor_tensor(xo[:, i, :], xo[:, i, :], xb[:, i, :], ALU.add).then_inc(s["m_x2"], 1)

                    def R_x3(n):
                        wait(dve, "m_x2", n, 2)
                        wait(dve, "r_T", n - first, 2)
                        for i in range(NT):
                            wait(dve, "r_o", n - first, i + 1)
                            dve.tensor_tensor(xo[:, i, :], MBANK[1 - i][:, 0:D], xo[:, i, :], ALU.add).then_inc(s["r_x3"], 1)

                    def slot(a, m, p):
                        if a is not None:
                            opened, run_a, run_m = a - first + 1, a - first, (a - first - 1 if m is not None else 0)
                        elif m is not None:
                            opened, run_a, run_m = B, B, B - 1
                        else:
                            opened, run_a, run_m = 0, 0, 0
                        state["from"] = base + opened * STEPS_P + run_a * STEPS_A + run_m * STEPS_M
                        state["k"] = 0
                        if m is not None:
                            M_stats(m)
                        if a is not None:
                            A_qkv(a, (2,))
                        if m is not None:
                            M_norm(m)
                        if a is not None:
                            A_qkv(a, (3, 4))
                            if eps is not None:
                                A_heads_sum(a)
                            A_qkv(a, (5,))
                        if m is not None:
                            M_xl(m)
                        if a is not None and eps is None:
                            A_halves(a)
                        if a is not None and eps is not None:
                            A_heads_rstd(a)
                        if m is not None:
                            M_hl(m, 0)
                        if a is not None and eps is not None:
                            A_heads_norm(a, m)
                        if a is not None and eps is not None:
                            A_halves(a)
                        if m is not None:
                            for f in range(1 if a is None or eps is None else 3 if rot else 2,
                                           5 if a is None or eps is not None else 2):
                                M_hl(m, f)
                        if a is not None:
                            for i in range(PAIRS):
                                A_max(a, i)
                                if m is not None and eps is None and i in (0, 2, 4):
                                    M_hl(m, 2 + i // 2)
                            A_negmax(a)
                        if m is not None:
                            M_x2(m, 0)
                        if a is not None:
                            A_turned2(a, 1)
                        if p is not None:
                            A_stats(p)
                        if a is not None:
                            A_turned2(a, 3)
                        if p is not None:
                            A_norm(p)
                        if m is not None and rot:
                            M_x2(m, 1)
                        if p is not None:
                            A_xf(p, 0)
                            A_xf(p, 1)
                            A_xf(p, 2)
                            A_xl(p)
                        if a is not None:
                            A_oraw(a, p, 0)
                            A_oraw(a, p, 1)
                        if m is not None and rot:
                            R_x3(m)
                        if a is not None:
                            A_out(a)
                        if p is not None:
                            A_qkv(p, (0,))
                        if a is not None:
                            A_olo(a)
                        if m is not None and not rot:
                            M_x2(m, 1)
                        if p is not None:
                            A_qkv(p, (1,))
                        if a is not None:
                            A_x1(a)
                        assert state["k"] == STEPS_P * (p is not None) + STEPS_A * (a is not None) + STEPS_M * (m is not None)

                    slots(dve, slot)
                    steps[0] = base + B * (STEPS_P + STEPS_A + STEPS_M)

                @block.tensor
                def _(pe):
                    pe.wait_ge(w_lo, NCH * (layer + 1))
                    if layer == 0:
                        pe.wait_ge(set_done, 7)

                    def three(out, xs, ws, n_k, lhs, rhs):
                        terms = [(xs[0], ws[0]), (xs[0], ws[1]), (xs[1], ws[0])]
                        for j, (x, wt) in enumerate(terms):
                            for k in range(n_k):
                                op = pe.matmul(out, lhs(x, k), rhs(wt, k), start=(j == 0 and k == 0), stop=(j == 2 and k == n_k - 1))
                        return op

                    def turn3(x, banks, done, run):
                        for c in range(KC):
                            for i in range(NT):
                                op = pe.transpose(banks[c // 2][0:KP, (c % 2) * T + i * P:(c % 2) * T + (i + 1) * P],
                                                  x[:, i, c * KP:(c + 1) * KP], ident[:, :])
                            if c:
                                op.then_inc(s[done], 1)

                    def A_turn(n, m, part):
                        if part == 0:
                            wait(pe, "a_xn", n, 2)
                            if m is not None:
                                wait(pe, "m_x2", m, 1)
                        else:
                            wait(pe, "a_xf", n, 2)
                        for c in ((0, 1), (2,))[part]:
                            for i in range(NT):
                                op = pe.transpose(MBANK[1][0:KP, (c % 2) * T + i * P:(c % 2) * T + (i + 1) * P],
                                                  xn[:, i, c * KP:(c + 1) * KP], ident[:, :])
                        op.then_inc(s["a_xT"], 1)

                    def A_qkv(n, fills):
                        if fills[0] == 0:
                            wait(pe, "a_xl", n, 1)
                        for f in fills:
                            i, part = (f // 2, f % 2) if f < 4 else (f - 4, 2)
                            if f == 0:
                                wait(pe, "a_ex", n, -1)
                            elif f == 2:
                                wait(pe, "a_ex", n, 0)
                            elif f >= 4:
                                wait(pe, "a_qkvd", n, f - 3)
                            three(S[:, f % 4, 0:D], (xh, xl), wqkv, KC,
                                  lambda x, k: x[:, k, i * P:(i + 1) * P],
                                  lambda wt, k: wt[:, k, part * D:(part + 1) * D]).then_inc(s["a_qkv"], 1)

                    def A_turn_pairs(bank, x, f):
                        for p in range(2):
                            for i in range(NT):
                                op = pe.transpose(bank[:, p * T + i * P:p * T + (i + 1) * P],
                                                  x[:, i, 4 * f + 2 * p:4 * f + 2 * p + 2, :].rearrange("p h d -> p (h d)").bitcast(F32), ident[:, :])
                        return op

                    def A_turn_q(n, f):
                        if f == 0:
                            wait(pe, "a_prd", n, 0)
                            wait(pe, "a_qh", n, 1)
                            wait(pe, "a_qs", n, 1)
                        else:
                            wait(pe, "a_qT", n, f)
                        A_turn_pairs(ABANK[0], qs, f).then_inc(s["a_T"], 1)

                    def A_turn_k(n, f):
                        if f == 0:
                            wait(pe, "a_kh", n, 2)
                            wait(pe, "a_kl", n, 1)
                        else:
                            wait(pe, "a_kA", n, f)
                            wait(pe, "a_kB", n, f)
                        A_turn_pairs(ABANK[1], ks, f).then_inc(s["a_T"], 1)

                    def A_scores(n, p):
                        if p % 2 == 0:
                            wait(pe, "a_qT", n, p // 2 + 1)
                            wait(pe, "a_kA", n, p // 2 + 1)
                            wait(pe, "a_kB", n, p // 2 + 1)
                        if p < 2:
                            wait(pe, "a_qkvd", n, 6)
                        else:
                            wait(pe, "a_mx", n, p - 1)
                        for a in range(2):
                            for i in range(NT):
                                op = pe.matmul(S[:, 2 * (p % 2) + a, i * T:(i + 1) * T], qT[:, p, i * P:(i + 1) * P], kz[a][:, p, :],
                                               start=True, stop=True)
                        op.then_inc(s["a_S"], 1)

                    def A_turn_q2(n, f):
                        if f == 0:
                            wait(pe, "a_qT", n, 4)
                            wait(pe, "a_nm", n, 1)
                        if f == 1:
                            wait(pe, "a_kA", n, 4)
                            wait(pe, "a_kB", n, 4)
                        if f == 2:
                            wait(pe, "a_q2a", n, 1)
                        if f == 3:
                            wait(pe, "a_q2d", n, 1)
                        A_turn_pairs(ABANK[f % 2], qs, f).then_inc(s["a_T2"], 1)

                    def A_scoresT(n, p):
                        if p % 2 == 0:
                            wait(pe, "a_q2a" if p % 4 == 0 else "a_q2d", n, p // 4 + 1)
                        if p < 2:
                            wait(pe, "a_mx", n, PAIRS - 1 + p)
                        else:
                            wait(pe, "a_ex", n, p - 1)
                        for a in range(2):
                            for i in range(NT):
                                op = pe.matmul(S[:, 2 * (p % 2) + a, i * T:(i + 1) * T], kz[a][:, p, i * P:(i + 1) * P], qT[:, p, :],
                                               start=True, stop=True)
                        op.then_inc(s["a_S"], 1)

                    def A_pv(n, p):
                        if p == 0:
                            wait(pe, "a_q2a", n, 2)
                            wait(pe, "a_q2d", n, 2)
                        wait(pe, "a_ex", n, p + 1)
                        j = p // 2
                        for i in range(NT):
                            for a in range(2):
                                g = 2 * (p % 2) + a
                                op = pe.matmul(ABANK[j // 2][32 * g:32 * g + 32, (j % 2) * T:(j % 2 + 1) * T], V[:, i, 2 * p + a, :],
                                               pT[:, p % 3, a, i * T:(i + 1) * T], start=(i == 0), stop=(i == NT - 1),
                                               tile_position=(0, 32 * g))
                        op.then_inc(s["a_pv"], 1)

                    def A_turn_o(n):
                        for i in range(NT):
                            if i == 0:
                                wait(pe, "a_o", n, 2)
                            for j in range(4):
                                op = pe.transpose(ABANK[i][:, j * P:(j + 1) * P], oraw[:, j, i * P:(i + 1) * P], ident[:, :])
                            op.then_inc(s["a_oT"], 1)

                    def A_turn_n(n):
                        wait(pe, "a_on", n, 2)
                        turn3(on, ABANK, "a_nT", n)

                    def A_proj(n):
                        wait(pe, "a_ol", n, 2)
                        for i in range(NT):
                            three(ABANK[i][:, 0:D], (oh, ol), wo, KC, lambda x, k: x[:, k, i * P:(i + 1) * P],
                                  lambda wt, k: wt[:, k, :]).then_inc(s["a_pr"], 1)

                    def M_turn(n, a):
                        wait(pe, "a_xf", last if a is None else a + 1, 0)
                        if rot:
                            wait(pe, "r_x3", n - first, 0)
                            if isinstance(n, int) and n == first:
                                wait(pe, "m_x2", n, 0)
                        else:
                            wait(pe, "m_x2", n, 0)
                        wait(pe, "m_xn", n, 2)
                        turn3(xo, MBANK, "m_xT", n)

                    def M_up_part(n, m, terms):
                        f, i = divmod(m, 2)
                        for j in terms:
                            wt, x = ((w1[0], xh2), (w1[1], xh2), (w1[0], xl2))[j]
                            if m == 0 and j == 2:
                                wait(pe, "m_xl", n, 1)
                            for k in range(KC):
                                if m == 0 and j == 0:
                                    wait(pe, "m_xh", n, k + 1)
                                op = pe.matmul(MBANK[f % 2][:, i * T:(i + 1) * T], wt[:, k, m * P:(m + 1) * P], x[:, k, :],
                                               start=(j == 0 and k == 0), stop=(j == 2 and k == KC - 1))
                        if j == 2 and (i == 1 or m == FM - 1):
                            op.then_inc(s["m_h"], 1)

                    def M_up_first(n):
                        wait(pe, "m_xf", n, 2)
                        M_up_part(n, 0, (0, 1))
                        wait(pe, "m_xf", n, 3)
                        M_up_part(n, 2, (0, 1))
                        M_up_part(n, 0, (2,))
                        M_up_part(n, 1, (0, 1, 2))
                        M_up_part(n, 2, (2,))
                        M_up_part(n, 3, (0, 1, 2))

                    def M_up(n, f):
                        wait(pe, "m_hf", n, f - 1)
                        for m in range(2 * f, min(2 * f + 2, FM)):
                            M_up_part(n, m, (0, 1, 2))

                    DOWN = [(j, k) for ks_ in (range(6), range(6, FM)) for j in range(2) for k in ks_] + [(2, k) for k in range(FM)]

                    def M_down(n, i, lo, hi):
                        if lo == 0 and i == 0:
                            wait(pe, "m_hf", n, 4)
                        if lo == 0 and i == 1:
                            wait(pe, "m_hf", n, 5)
                        for z in range(lo, hi):
                            j, k = DOWN[z]
                            x, wt = ((hh, w2[0]), (hh, w2[1]), (hl, w2[0]))[j]
                            if i == 0 and j == 0 and k % 2 == 0:
                                wait(pe, "m_hh", n, k // 2 + 1)
                            if i == 0 and z == 2 * FM:
                                wait(pe, "m_hl", n, 5)
                            op = pe.matmul(MBANK[1 - i][:, 0:D], x[:, k, i * P:(i + 1) * P], wt[:, k, :],
                                           start=(z == 0), stop=(z == 3 * FM - 1))
                        if hi == 3 * FM:
                            op.then_inc(s["m_y"], 1)

                    def R_turn(n, p=None):
                        wait(pe, "m_x2", n, 2)
                        if p is not None:
                            wait(pe, "a_xf", p, 3)
                        turn3(xo, MBANK[::-1], "r_T", n)

                    def R_z(n):
                        wait(pe, "r_x", n - first, 2)
                        for k in range(KC):
                            op = pe.matmul(MBANK[1][0:ROT, 0:T], U[:, k, :], xf2[:, k, :], start=(k == 0), stop=(k == KC - 1))
                        op.then_inc(s["r_z"], 1)

                    def R_y(n):
                        wait(pe, "r_zs", n - first, 1)
                        wait(pe, "r_e", n - first, 16)
                        constant_wait(pe)
                        pe.matmul(MBANK[0][0:ROT, 0:T], eb[:, :], zT[:, :], start=True, stop=True).then_inc(s["r_y"], 1)

                    def R_out(n):
                        wait(pe, "r_ys", n - first, 1)
                        for i in range(NT):
                            pe.matmul(MBANK[1 - i][:, 0:D], yT[:, i * P:(i + 1) * P], UT[:, :], start=True, stop=True).then_inc(s["r_o"], 1)

                    def slot(a, m, p):
                        def down(i, lo, hi):
                            if m is not None and hi > lo:
                                M_down(m, i, lo, hi)

                        if a is not None:
                            A_qkv(a, (2, 3, 4))
                        if m is not None:
                            M_turn(m, a)
                        if a is not None:
                            A_qkv(a, (5,))
                        if m is not None:
                            M_up_first(m)
                            if a is None or eps is not None:
                                for f in range(2, 5):
                                    M_up(m, f)
                        if a is None:
                            down(0, 0, 27)
                            down(1, 0, 27)
                            if p is not None:
                                A_turn(p, m, 0)
                                A_turn(p, m, 1)
                                A_qkv(p, (0, 1))
                            if rot and m is not None:
                                R_turn(m)
                                R_z(m)
                                R_y(m)
                                R_out(m)
                            return
                        if eps is not None:
                            here = 18 if rot else 12
                            down(0, 0, here)
                            fills = [lambda f=f: down(0, here + (27 - here) * f // 5, here + (27 - here) * (f + 1) // 5) for f in range(5)]
                            if rot:
                                down(1, 0, 9)
                        elif m is not None:
                            fills = [lambda f=f: M_up(m, f) for f in range(2, 5)] + [lambda: down(0, 0, 12), lambda: down(0, 12, 27)]
                        else:
                            fills = [lambda: None] * 5
                        A_turn_q(a, 0)
                        A_turn_k(a, 0)
                        fills[0]()
                        A_turn_q(a, 1)
                        A_turn_k(a, 1)
                        for f in range(4):
                            A_scores(a, 2 * f)
                            A_scores(a, 2 * f + 1)
                            if f < 2:
                                A_turn_q(a, f + 2)
                                A_turn_k(a, f + 2)
                            fills[f + 1]()
                        places = (17, 20, 24, 27, 27, 27, 27) if rot else (9, 12, 16, 16, 21, 24, 27)
                        down(1, 9 if rot else 0, places[0])
                        A_turn_q2(a, 0)
                        A_turn_q2(a, 1)
                        down(1, places[0], places[1])
                        A_turn_q2(a, 2)
                        A_turn_q2(a, 3)
                        A_scoresT(a, 0)
                        A_scoresT(a, 1)
                        down(1, places[1], places[2])
                        for i in range(2, PAIRS):
                            A_scoresT(a, i)
                            A_pv(a, i - 2)
                            if i == 2:
                                down(1, places[2], places[3])
                            if p is not None and i == 3:
                                A_turn(p, m, 0)
                            if p is not None and i == 4:
                                A_turn(p, m, 1)
                            if m is not None and rot:
                                if i == 5:
                                    R_turn(m, p)
                                if i == 6:
                                    R_z(m)
                                if i == 7:
                                    R_y(m)
                        A_pv(a, PAIRS - 2)
                        A_pv(a, PAIRS - 1)
                        down(1, places[3], places[4])
                        if rot and m is not None:
                            R_out(m)
                        A_turn_o(a)
                        if p is not None:
                            A_qkv(p, (0,))
                        down(1, places[4], places[5])
                        A_turn_n(a)
                        if p is not None:
                            A_qkv(p, (1,))
                        down(1, places[5], places[6])
                        A_proj(a)

                    slots(pe, slot)


def preamble(nc, t, sem, S, ABANK, MBANK, ident, modT, U, UT, mhalf, gates, expm):
    HB = B // 2
    with ExitStack() as ctx:
        def sb(name, shape, dt=F32):
            return ctx.enter_context(nc.sbuf_tensor(name, shape, dt))

        cT = sb("cT", [KP, KC, B])
        sT = sb("sT", [KP, KC, B])
        wmod = sb("wmod", [KP, KC, 6 * D])
        bmodT = sb("bmodT", [KP, LAYERS, 12])
        bgate = sb("bgate", [B, LAYERS, 2 * D])
        grow = sb("grow", [B, 2 * D])
        WJ = 16
        wr = sb("wr", [KP, KC, 2, WJ, ROT])
        bfull = sb("bfull", [P, ROT])
        sign = sb("sign", [P, ROT])
        Bm = sb("Bm", [P, HB, ROT])
        Nm = sb("Nm", [P, HB, ROT])
        Em = sb("Em", [P, HB, ROT])
        Fm = sb("Fm", [P, HB, ROT])
        Bk = sb("Bk", [P, HB, ROT])
        Nk = sb("Nk", [P, HB, ROT])
        blockones = sb("blockones", [P, P])
        house_row = sb("house_row", [P, P])
        eye2 = sb("eye2", [P, ROT])
        after = sb("after", [P, ROT])
        mask = sb("mask", [P, ROT + D])
        house = sb("house", [P, 1])
        G = sb("G", [P, D])
        mk = sb("mk", [P, D])
        vs = sb("vs", [P, D])
        junk = sb("junk", [P, D])
        junk2 = sb("junk2", [P, D])
        dot = sb("dot", [P, 1])
        n2 = sb("n2", [P, 1])
        rt = sb("rt", [P, 1])
        sg = sb("sg", [P, ROT])
        q = [sb(f"q{i}", [P, 1]) for i in range(8)]

        load = sem("load")
        wm_in = sem("wm_in")
        wr_in = [sem("wr_in0"), sem("wr_in1")]
        silu = sem("silu")
        const = sem("const")
        mod_mm = sem("mod_mm")
        mod_out = sem("mod_out")
        gate_out = sem("gate_out")
        a_mm = sem("a_mm")
        a_done = sem("a_done")
        e_mm = sem("e_mm")
        e_up = sem("e_up")
        e_k = sem("e_k")
        e_out = sem("e_out")
        g_mk = sem("g_mk")
        g_vb = sem("g_vb")
        g_n2 = sem("g_n2")
        g_rt = sem("g_rt")
        g_step = sem("g_step")
        u_mm = sem("u_mm")
        u_n2 = sem("u_n2")
        u_rt = sem("u_rt")

        CONSTS = 23
        Q_MOD, Q_A, Q_TAYLOR, Q_SQUARE = 4, 4, (2, 2, 2, 2, 1), 3
        TAYLOR_FROM = LAYERS * Q_MOD + ROT // 16 * Q_A
        SQUARE_FROM = TAYLOR_FROM + sum(Q_TAYLOR)
        assert len(Q_TAYLOR) == TAYLOR - 1 and SQUARE_FROM + SQUARINGS * Q_SQUARE == ROT

        def steps_between(start, count):
            return range(start, start + count)

        A4 = [S[:, i, :] for i in range(4)]
        NJ = ROT // WJ

        block = ctx.enter_context(nc.Block())

        @block.sync
        def _(sp):
            for to, ap in ((cT[:, :, :], t["cT"]), (bmodT[:, :, :], t["bmodT"]), (bfull[0:ROT, :], t["bfull"]),
                           (bfull[ROT:P, :], t["bfull"]), (G[0:ROT, :], t["PT"]), (G[ROT:P, :], t["PT"])):
                sp.dma_start(to, ap).then_inc(load, 16)
            for i in range(LAYERS):
                sp.dma_start(bgate[:, i, :], t["bgate"][i].partition_broadcast(B)).then_inc(load, 16)
            for i in range(LAYERS):
                if i:
                    sp.wait_ge(mod_mm, 2 * i)
                sp.dma_start(wmod[:, :, :], t[i]["wmod"].rearrange("(k p) n -> p k n", p=KP)).then_inc(wm_in, 16)
            for c in range(NJ):
                if c >= 2:
                    sp.wait_ge(a_mm, c - 1)
                sp.dma_start(wr[:, :, c % 2, :, :], t["wrot"].rearrange("(k p) j i -> p k j i", p=KP)[:, :, c * WJ:(c + 1) * WJ, :]).then_inc(wr_in[c % 2], 16)
            sp.wait_ge(e_up, 2 * (TAYLOR + SQUARINGS))
            for h in range(2):
                sp.dma_start(expm[h * HB:(h + 1) * HB].rearrange("b d e -> d b e"), Em[h * ROT:(h + 1) * ROT, :, :]).then_inc(e_out, 16)
            sp.wait_ge(gate_out, 16 * LAYERS)
            sp.wait_ge(e_out, 32)

        @block.gpsimd
        def _(pool):
            made = [0]

            def own(op):
                op.then_inc(const, 1)
                made[0] += 1
                pool.wait_ge(const, made[0])

            def keep(tile, rows, op, value, step=1, tilestep=-1):
                view = tile[rows[0]:rows[1], :]
                own(pool.affine_select(out=view, in_=view, compare_op=op, fill=value, base=0,
                                       pattern=[[tilestep, view.shape[1]]], channel_multiplier=step))

            for tile, value in ((ident, 0.0), (blockones, 0.0), (house_row, 0.0), (eye2, 0.0), (after, -1.0), (mask, 1.0),
                                (mhalf, -0.5), (house, 0.0), (sign, 1.0)):
                own(pool.memset(tile[:, :], value))
            keep(ident, (0, P), ALU.not_equal, 1.0)
            own(pool.memset(blockones[0:ROT, 0:ROT], 1.0))
            own(pool.memset(blockones[ROT:P, ROT:P], 1.0))
            own(pool.memset(house_row[ROT:ROT + 1, :], 1.0))
            own(pool.memset(mask[ROT:P, 0:ROT], 0.0))
            own(pool.memset(house[ROT:P, :], 1.0))
            for rows in ((0, ROT), (ROT, P)):
                keep(eye2, rows, ALU.not_equal, 1.0)
                keep(after, rows, ALU.is_gt, 0.0)
                keep(sign, rows, ALU.is_gt, -1.0, step=-1, tilestep=1)
                keep(sign, rows, ALU.not_equal, 0.0)
            assert made[0] == CONSTS
            with pool.Fori(0, ROT) as j:
                pool.wait_ge(g_n2, j + 1)
                pool.tensor_tensor(rt[:, :], n2[:, :], mhalf[:, 0:1], ALU.pow).then_inc(g_rt, 1)
            pool.wait_ge(u_n2, 1)
            pool.tensor_tensor(rt[:, :], n2[:, :], mhalf[:, 0:1], ALU.pow).then_inc(u_rt, 1)

        @block.scalar
        def _(act):
            act.wait_ge(load, 16 * 9)
            act.activation(sT[:, :, :], cT[:, :, :], ACT.Silu).then_inc(silu, 1)

            def length2(j):
                act.wait_ge(g_step, j * 14 + 2)
                act.activation(junk2[:, :], vs[:, :], ACT.Square, accum_out=n2[:, :]).then_inc(g_n2, 1)

            for i in range(LAYERS):
                for j in steps_between(i * Q_MOD, Q_MOD):
                    length2(j)
                act.wait_ge(mod_out, 3 * i + 3)
                act.dma_start(gates[i], grow[:, :]).then_inc(gate_out, 16)
            for j in steps_between(LAYERS * Q_MOD, NJ * Q_A):
                length2(j)
            for k in range(TAYLOR, 0, -1):
                i = TAYLOR - k
                if i == 0:
                    act.wait_ge(a_done, 3 * NJ)
                else:
                    act.wait_ge(e_up, 2 * i)
                act.mul(Bk[:, :, :], Bm[:, :, :], 1.0 / k).then_inc(e_k, 1)
                act.mul(Nk[:, :, :], Bm[:, :, :], -1.0 / k).then_inc(e_k, 1)
                if i < len(Q_TAYLOR):
                    for j in steps_between(TAYLOR_FROM + sum(Q_TAYLOR[:i]), Q_TAYLOR[i]):
                        length2(j)
            with act.Fori(0, SQUARINGS * Q_SQUARE) as j:
                length2(j + SQUARE_FROM)
            act.wait_ge(g_step, 14 * ROT)
            act.activation(junk2[:, :], G[:, :], ACT.Square, accum_out=n2[:, :]).then_inc(u_n2, 1)

        @block.vector
        def _(dve):
            dve.wait_ge(const, CONSTS)
            dve.wait_ge(load, 16 * 9)

            vb = MBANK[1]

            def basis_step(j):
                count = [0]

                def own(op):
                    op.then_inc(g_step, 1)
                    count[0] += 1
                    dve.wait_ge(g_step, j * 14 + count[0])

                def col(tile):
                    return tile[:, bass.ds(j, 1)]

                own(dve.scalar_tensor_tensor(out=mk[:, :], in0=G[:, :], scalar=col(eye2), in1=mask[:, bass.ds(ROT - j, D)],
                                             op0=ALU.mult, op1=ALU.mult))
                dve.wait_ge(g_vb, j + 1)
                own(dve.tensor_copy(vs[:, :], vb[:, 0:D]))
                own(dve.tensor_tensor(junk[:, :], vs[:, :], G[:, :], ALU.mult))
                own(dve.tensor_reduce(dot[:, :], junk[:, :], AX.X, ALU.add))
                own(dve.tensor_scalar(q[1][:, :], col(vs), 0.0, 2.0, ALU.is_ge, ALU.mult))
                own(dve.tensor_scalar(col(sg), q[1][:, :], -1.0, house[:, :], ALU.add, ALU.mult))
                dve.wait_ge(g_rt, j + 1)
                own(dve.scalar_tensor_tensor(out=q[2][:, :], in0=n2[:, :], scalar=rt[:, :], in1=col(sg), op0=ALU.mult, op1=ALU.mult))
                own(dve.scalar_tensor_tensor(out=q[3][:, :], in0=col(vs), scalar=q[2][:, :], in1=n2[:, :], op0=ALU.mult, op1=ALU.add))
                own(dve.reciprocal(q[4][:, :], q[3][:, :]))
                own(dve.scalar_tensor_tensor(out=q[5][:, :], in0=col(G), scalar=q[2][:, :], in1=dot[:, :], op0=ALU.mult, op1=ALU.add))
                own(dve.tensor_scalar(q[6][:, :], q[5][:, :], q[4][:, :], col(after), ALU.mult, ALU.mult))
                own(dve.scalar_tensor_tensor(out=G[:, :], in0=vs[:, :], scalar=q[6][:, :], in1=G[:, :], op0=ALU.mult, op1=ALU.add))
                own(dve.tensor_tensor(q[7][:, :], q[6][:, :], q[2][:, :], ALU.mult))
                own(dve.tensor_tensor(col(G), col(G), q[7][:, :], ALU.add))
                assert count[0] == 14

            for i in range(LAYERS):
                for j in steps_between(i * Q_MOD, Q_MOD):
                    basis_step(j)
                dve.wait_ge(mod_mm, 2 * i + 1)
                v = modT[:, i, :, :]
                dve.tensor_tensor(v, MBANK[0][0:KP, 0:12 * B].rearrange("p (c b) -> p c b", b=B),
                                  bmodT[:, i, :].unsqueeze(2).broadcast_to([KP, 12, B]), ALU.add).then_inc(mod_out, 1)
                dve.wait_ge(mod_out, 3 * i + 1)
                for c in (3, 9):
                    op = dve.tensor_scalar(v[:, c:c + 3, :], v[:, c:c + 3, :], 1.0, None, ALU.add)
                op.then_inc(mod_out, 1)
                dve.wait_ge(mod_mm, 2 * i + 2)
                if i:
                    dve.wait_ge(gate_out, 16 * i)
                for g in range(2):
                    op = dve.tensor_tensor(grow[:, g * D:(g + 1) * D], ABANK[g][0:B, 0:D], bgate[:, i, g * D:(g + 1) * D], ALU.add)
                op.then_inc(mod_out, 1)
            for c in range(NJ):
                for j in steps_between(LAYERS * Q_MOD + c * Q_A, Q_A):
                    basis_step(j)
                dve.wait_ge(a_mm, c + 1)
                for h in range(2):
                    to = Bm[h * ROT:(h + 1) * ROT, :, c * WJ:(c + 1) * WJ]
                    at = A4[c % 4][h * ROT:(h + 1) * ROT, :].rearrange("p (j b) -> p b j", b=B)[:, h * HB:(h + 1) * HB, :]
                    op = dve.tensor_tensor(to, at, bfull[h * ROT:(h + 1) * ROT, c * WJ:(c + 1) * WJ].unsqueeze(1).broadcast_to([ROT, HB, WJ]), ALU.add)
                op.then_inc(a_done, 1)
                dve.wait_ge(a_done, 3 * c + 1)
                part = Bm[:, :, c * WJ:(c + 1) * WJ]
                dve.tensor_tensor(part, part, sign[:, c * WJ:(c + 1) * WJ].unsqueeze(1).broadcast_to([P, HB, WJ]), ALU.mult).then_inc(a_done, 1)
                dve.wait_ge(a_done, 3 * c + 2)
                dve.tensor_scalar(part, part, 2.0 ** -SQUARINGS, None, ALU.mult).then_inc(a_done, 1)
            dve.wait_ge(a_done, 3 * NJ)
            dve.tensor_scalar(Nm[:, :, :], Bm[:, :, :], -1.0, None, ALU.mult).then_inc(a_done, 1)
            dve.wait_ge(e_k, 2)
            dve.tensor_copy(Em[:, :, :], Bk[:, :, :]).then_inc(e_up, 1)
            dve.tensor_copy(Fm[:, :, :], Nk[:, :, :]).then_inc(e_up, 1)
            S2 = S[:, :, :].rearrange("p (x y) c -> p x (y c)", x=2)

            def flat(x):
                return x[:, :, :].rearrange("p b e -> p (b e)")

            for k in range(TAYLOR - 1, 0, -1):
                i = TAYLOR - k
                for j in steps_between(TAYLOR_FROM + sum(Q_TAYLOR[:i - 1]), Q_TAYLOR[i - 1]):
                    basis_step(j)
                dve.wait_ge(e_k, 2 * i + 2)
                dve.wait_ge(e_mm, i)
                for x, part, m in ((Em, 0, Bk), (Fm, 1, Nk)):
                    dve.scalar_tensor_tensor(out=flat(x), in0=S2[:, part, :], scalar=1.0 / k, in1=flat(m),
                                             op0=ALU.mult, op1=ALU.add).then_inc(e_up, 1)
            with dve.Fori(0, SQUARINGS) as i:
                for j in range(Q_SQUARE):
                    basis_step(i * Q_SQUARE + (SQUARE_FROM + j))
                dve.wait_ge(e_mm, i + TAYLOR)
                dve.wait_ge(e_up, 2 * i + 2 * TAYLOR)
                for x, part in ((Em, 0), (Fm, 1)):
                    dve.scalar_tensor_tensor(out=flat(x), in0=flat(x), scalar=2.0, in1=S2[:, part, :],
                                             op0=ALU.mult, op1=ALU.add).then_inc(e_up, 1)

            dve.wait_ge(u_mm, 1)
            end = 14 * ROT
            dve.tensor_tensor(junk[0:ROT, 0:ROT], ABANK[1][0:ROT, 0:ROT], eye2[0:ROT, :], ALU.mult).then_inc(g_step, 1)
            dve.wait_ge(g_step, end + 1)
            dve.tensor_reduce(dot[0:ROT, :], junk[0:ROT, 0:ROT], AX.X, ALU.add).then_inc(g_step, 1)
            dve.wait_ge(u_rt, 1)
            dve.wait_ge(g_step, end + 2)
            dve.scalar_tensor_tensor(out=q[0][0:ROT, :], in0=dot[0:ROT, :], scalar=-1.0, in1=rt[0:ROT, :], op0=ALU.mult, op1=ALU.mult).then_inc(g_step, 1)
            dve.wait_ge(g_step, end + 3)
            dve.tensor_scalar(UT[:, :], G[0:ROT, :], q[0][0:ROT, :], None, ALU.mult).then_inc(g_step, 1)
            dve.wait_ge(u_mm, 2)
            dve.tensor_copy(U[:, :, :], ABANK[0][0:KP, 0:KC * ROT].rearrange("p (k e) -> p k e", k=KC)).then_inc(g_step, 1)

        @block.tensor
        def _(pe):
            def spread(j):
                pe.wait_ge(g_step, j * 14 + 1)
                pe.matmul(MBANK[1][:, 0:D], blockones[:, :], mk[:, :], start=True, stop=True).then_inc(g_vb, 1)

            pe.wait_ge(silu, 1)
            for i in range(LAYERS):
                for j in steps_between(i * Q_MOD, Q_MOD):
                    spread(j)
                pe.wait_ge(wm_in, 16 * (i + 1))
                if i:
                    pe.wait_ge(mod_out, 3 * i)
                for c, part in enumerate((0, 1, 3, 4)):
                    for e in range(KC):
                        for k in range(KC):
                            op = pe.matmul(MBANK[0][0:KP, (3 * c + e) * B:(3 * c + e + 1) * B],
                                           wmod[:, k, part * D + e * KP:part * D + (e + 1) * KP], sT[:, k, :],
                                           start=(k == 0), stop=(k == KC - 1))
                op.then_inc(mod_mm, 1)
                for g, part in enumerate((2, 5)):
                    for k in range(KC):
                        op = pe.matmul(ABANK[g][0:B, 0:D], sT[:, k, :], wmod[:, k, part * D:(part + 1) * D], start=(k == 0), stop=(k == KC - 1))
                op.then_inc(mod_mm, 1)
            for c in range(NJ):
                pe.wait_ge(wr_in[c % 2], 16 * (c // 2 + 1))
                for j in range(WJ):
                    if j % (WJ // Q_A) == 0:
                        spread(LAYERS * Q_MOD + c * Q_A + j // (WJ // Q_A))
                    for h in range(2):
                        for k in range(KC):
                            op = pe.matmul(A4[c % 4][h * ROT:(h + 1) * ROT, j * B:(j + 1) * B], wr[:, k, c % 2, j, :], sT[:, k, :],
                                           start=(k == 0), stop=(k == KC - 1))
                op.then_inc(a_mm, 1)
            pe.wait_ge(a_done, 3 * NJ + 1)

            def products(left_e, left_f, columns):
                work = [(x, part, lhs, b) for x, part, lhs in ((Em, 0, left_e), (Fm, 2, left_f)) for b in range(HB)]
                for at, (x, part, lhs, b) in enumerate(work):
                    for c, j in enumerate(columns):
                        if at == c * len(work) // len(columns):
                            spread(j)
                    for h in range(2):
                        rows = slice(h * ROT, (h + 1) * ROT)
                        bank = part + b * ROT // 512
                        to = b * ROT % 512
                        op = pe.matmul(S[rows, bank, to:to + ROT], lhs[rows, b, :], x[rows, b, :], start=True, stop=True)
                return op

            for k in range(TAYLOR - 1, 0, -1):
                i = TAYLOR - k
                pe.wait_ge(e_up, 2 * i)
                products(Nm, Bm, steps_between(TAYLOR_FROM + sum(Q_TAYLOR[:i - 1]), Q_TAYLOR[i - 1])).then_inc(e_mm, 1)
            with pe.Fori(0, SQUARINGS) as i:
                pe.wait_ge(e_up, 2 * i + 2 * TAYLOR)
                pe.nop(nofuse=True)
                products(Fm, Em, [i * Q_SQUARE + (SQUARE_FROM + j) for j in range(Q_SQUARE)]).then_inc(e_mm, 1)
            pe.wait_ge(g_step, 14 * ROT)
            pe.matmul(ABANK[1][:, 0:ROT], house_row[:, :], sg[:, :], start=True, stop=True).then_inc(u_mm, 1)
            pe.wait_ge(g_step, 14 * ROT + 4)
            for k in range(KC):
                op = pe.transpose(ABANK[0][0:KP, k * ROT:(k + 1) * ROT], UT[:, k * KP:(k + 1) * KP], ident[0:ROT, 0:ROT])
            op.then_inc(u_mm, 1)


_LAYER = [
    dict(wmod="w_mod", bmod="b_mod", wqkv="w_qkv", bqkv="b_qkv", gq="g_q", gk="g_k", wo="w_proj", bo="b_proj", w1="w1", b1="b1", w2="w2", b2="b2"),
    dict(wmod="ada_w", bmod="ada_b", wqkv="qkv_w", bqkv="qkv_b", wo="out_w", bo="out_b", w1="w1", b1="b1", w2="w2", b2="b2"),
    dict(wmod="w_ada", bmod="b_ada", wqkv="w_qkv", bqkv="b_qkv", gq="qn_g", bq="qn_b", gk="kn_g", bk="kn_b", wo="w_proj", bo="b_proj", w1="w1", b1="b1", w2="w2", b2="b2"),
]


def kernel(**inputs):
    import concourse.bacc as _bacc
    from concourse.bass_utils import run_bass_kernel_spmd as _run

    nc = _bacc.Bacc("TRN2", target_bir_lowering=False, num_devices=1)
    arrays = {}

    def give(name, a):
        a = np.ascontiguousarray(a)
        name = f"in_{name}_dram"
        arrays[name] = a
        return nc.dram_tensor(name, a.shape, mybir.dt.from_np(a.dtype), kind="ExternalInput").ap()

    t = {"x": give("x", inputs["x"])}
    c = np.asarray(inputs["cond_1152"])
    t["cT"] = give("cT", c.T.reshape(KC, KP, B).transpose(1, 0, 2))
    bm, bg = [], []
    for i, names in enumerate(_LAYER):
        p = f"L{i}_cond_"
        t[i] = {}
        for k, name in names.items():
            a = np.asarray(inputs[p + name])
            if k == "b1":
                t[i]["b1T"] = give(f"L{i}_b1T", a.reshape(FM, P).T)
            elif k == "bmod":
                parts = a.reshape(6, KC, KP)
                bm.append(parts[[0, 1, 3, 4]].reshape(12, KP).T)
                bg.append(parts[[2, 5]].reshape(2 * D))
            else:
                t[i][k] = give(f"L{i}_{k}", a)
    t["bmodT"] = give("bmodT", np.stack(bm, 1))
    t["bgate"] = give("bgate", np.stack(bg))
    t["PT"] = give("PT", np.asarray(inputs["L3_cond_P"]).T)
    iu, ju = np.triu_indices(ROT, k=1)
    at = np.zeros((ROT, ROT), np.int64)
    at[iu, ju] = at[ju, iu] = np.arange(iu.size)
    W = np.asarray(inputs["L3_cond_W"])
    t["wrot"] = give("wrot", W[at.T.ravel()].reshape(ROT, ROT, D).transpose(2, 0, 1))
    t["bfull"] = give("bfull", np.asarray(inputs["L3_cond_b"])[at])
    t["out"] = nc.dram_tensor("out_0_dram", (B, T, D), F32, kind="ExternalOutput").ap()
    build(nc, t)
    r = _run(nc, [arrays], core_ids=[0])
    return r.results[0]["out_0_dram"]
```

```python
from contextlib import ExitStack

import numpy as np

import concourse.bass as bass
from concourse import mybir

F32 = mybir.dt.float32
F32R = mybir.dt.float32r
I32 = mybir.dt.int32
ALU = mybir.AluOpType
ACT = mybir.ActivationFunctionType
AX = mybir.AxisListType

B, T, D = 32, 256, 288
H, HD = 16, 18
F = 4 * D
LAYERS = 3
P = 128
NT = T // P
KC, KP = 3, 96
FM = F // P
PAIRS = H // 2
SLOT = 64
ROT = 64
SQUARINGS, TAYLOR = 9, 6
NEWTON_MAGIC = 0x5F3759DF
QK_EPS = (1e-6, None, 1e-5)

PER_RUN = dict(
    a_x=16, a_g=16, a_st=1, a_ve=1, a_rs=1, a_xn=2, a_xT=2, a_xf=3, a_xh=1, a_xl=1, a_qkv=6, a_qkvd=6,
    a_sq=1, a_nrm=1, a_qs=1, a_qh=1, a_kh=2, a_kl=1, a_T=8, a_qT=4, a_kA=4, a_kB=4, a_S=16, a_mx=8,
    a_nm=1, a_T2=4, a_q2a=2, a_q2d=2, a_ex=8, a_pv=8, a_o=2, a_oT=2, a_on=2, a_nT=2, a_oh=2, a_ol=2,
    a_pr=2, a_prd=2, a_gb=1, a_xa=1, a_x1=2, a_warm=2,
    m_g=16, m_bn=2, m_st=1, m_ve=1, m_rs=1, m_xn=2, m_gb=1, m_xb=1, m_xT=2, m_xf=3, m_xh=3, m_xl=1, m_h=5,
    m_hf=5, m_hh=5, m_hl=5, m_y=2, m_x2=2, m_out=16, m_mod=1, a_mod=1,
    r_e=16, r_T=2, r_x=2, r_z=1, r_zs=1, r_y=1, r_ys=1, r_o=2, r_x3=2,
)


def upto(name, run, k):
    return run * PER_RUN[name] + k


def build(nc, t):
    with ExitStack() as ctx:
        def sb(name, shape, dt=F32, at=ctx):
            return at.enter_context(nc.sbuf_tensor(name, shape, dt))

        def ps(name, shape):
            return ctx.enter_context(nc.psum_tensor(name, shape, F32))

        def sem(name):
            return ctx.enter_context(nc.semaphore(name))

        s = {name: sem(name) for name in PER_RUN}

        def wait(eng, name, run, k):
            value = upto(name, run, k)
            if not (isinstance(value, int) and value <= 0):
                eng.wait_ge(s[name], value)

        S = ps("S", [P, 4, 512])
        ABANK = [ps("A0", [P, 512]), ps("A1", [P, 512])]
        MBANK = [ps("M0", [P, 512]), ps("M1", [P, 512])]

        ident = sb("ident", [P, P])
        modT = sb("modT", [KP, LAYERS, 12, B])
        U = sb("U", [KP, KC, ROT])
        UT = sb("UT", [ROT, D])
        mhalf = sb("mhalf", [P, 2])

        gates = nc.dram_tensor("gates", (LAYERS, B, 2 * D), F32, kind="Internal").ap()
        expm = nc.dram_tensor("expm", (B, ROT, ROT), F32, kind="Internal").ap()
        mid = [nc.dram_tensor(f"mid{i}", (B, T, D), F32, kind="Internal").ap() for i in range(2)]

        preamble(nc, t, sem, S, ABANK, MBANK, ident, modT, U, UT, mhalf, gates, expm)

        wqkv = [sb(f"wqkv_{h}", [KP, KC, 3 * D], F32R) for h in ("hi", "lo")]
        wo = [sb(f"wo_{h}", [KP, KC, D], F32R) for h in ("hi", "lo")]
        w1 = [sb(f"w1_{h}", [KP, KC, F], F32R) for h in ("hi", "lo")]
        w2 = [sb(f"w2_{h}", [P, FM, D], F32R) for h in ("hi", "lo")]
        bqkv = sb("bqkv", [P, 3 * D])
        gam = sb("gam", [P, 2 * HD])
        bet = sb("bet", [P, 2 * HD])
        bo = sb("bo", [P, D])
        b2 = sb("b2", [P, D])
        b1T = sb("b1T", [P, FM])
        xld = sb("xld", [P, NT, D])
        xa = sb("xa", [P, NT, D])
        xn = sb("xn", [P, NT, D])
        gA = sb("gA", [P, D])
        gbA = sb("gbA", [P, D])
        amod = sb("amod", [KP, 6])
        oraw = sb("oraw", [P, 4, T])
        xf = oraw[0:KP, 0:3, :]
        xh = sb("xh", [KP, KC, T], F32R)
        xl = sb("xl", [KP, KC, T], F32R)
        qs = sb("qs", [P, NT, H, SLOT], F32R)
        ks = sb("ks", [P, NT, H, SLOT], F32R)
        V = sb("V", [P, NT, H, 32])
        qT = sb("qT", [P, PAIRS, T], F32R)
        oh, ol = (qT[0:KP, KC * i:KC * i + KC, :] for i in range(2))
        kz = [sb(f"kz{a}", [P, PAIRS, T], F32R) for a in range(2)]
        pT = sb("pT", [P, 3, 2, 512])
        flat = pT[:, :, :, :].rearrange("p s a c -> p (s a c)")
        qk = flat[:, 0:NT * 2 * D].rearrange("p (t c) -> p t c", t=NT)
        sq = flat[:, NT * 2 * D:2 * NT * 2 * D]
        on = flat[:, 4 * NT * D:5 * NT * D].rearrange("p (t d) -> p t d", t=NT)
        arrive = ([flat[0:KP, 3 * D * k:3 * D * (k + 1)] for k in range(KC)]
                  + [flat[0:KP, 9 * D:10 * D], xa[0:KP, 0, :], xa[0:KP, 1, :]])
        mx = sb("mx", [P, PAIRS, 2, NT])
        nmx = sb("nmx", [P, PAIRS, 2, NT])
        stA = sb("stA", [P, NT, 6])
        mvA = sb("mvA", [P, NT, 2])
        rsA = sb("rsA", [P, NT])
        veA = sb("veA", [P, NT])
        sm = sb("sm", [P, 64])
        nv = sb("nv", [P, 64])
        na = sb("na", [P, 64])
        ny = sb("ny", [P, 64])
        rden = sb("rden", [P, NT, H])
        warm = sb("warm", [P, 2])
        x1 = sb("x1", [P, NT, D])
        xbo = sb("xbo", [P, 2, NT, D])
        xb = xbo[:, 0, :, :]
        xo = xbo[:, 1, :, :]
        gM = sb("gM", [P, D])
        gbM = sb("gbM", [P, D])
        mmod = sb("mmod", [KP, 6])
        hf = sb("hf", [P, 2, F // 2])
        xf2 = hf[0:KP, :, :].rearrange("p r c -> p (r c)")[:, 0:KC * T].rearrange("p (c n) -> p c n", c=KC)
        xh2 = sb("xh2", [KP, KC, T], F32R)
        xl2 = sb("xl2", [KP, KC, T], F32R)
        hh = sb("hh", [P, FM, T], F32R)
        hl = sb("hl", [P, FM, T], F32R)
        stM = sb("stM", [P, NT, 6])
        mvM = sb("mvM", [P, NT, 2])
        rsM = sb("rsM", [P, NT])
        veM = sb("veM", [P, NT])
        eb = sb("eb", [ROT, ROT])
        zT = sb("zT", [ROT, T])
        yT = sb("yT", [ROT, T])

        w_in = sem("w_in")
        w_hi = sem("w_hi")
        w_lo = sem("w_lo")
        v_in = [sem("v_in0"), sem("v_in1")]
        v_hi = sem("v_hi")
        v_lo = sem("v_lo")
        p_in = sem("p_in")
        w_mean = sem("w_mean")
        w_step = sem("w_step")
        set_done = sem("set_done")
        dve_step = sem("dve_step")

        def a_chunks(layer):
            w = t[layer]
            return ([(w["wqkv"].rearrange("(k p) n -> p k n", p=KP)[:, k, :],
                      [x[:, k, :] for x in wqkv]) for k in range(KC)]
                    + [(w["wo"].rearrange("(k p) n -> p k n", p=KP)[:, k, :],
                        [x[:, k, :] for x in wo]) for k in range(KC)])

        def m_chunks(layer):
            w = t[layer]
            return ([(w["w1"].rearrange("(k p) n -> p k n", p=KP)[:, k, :], KP, F,
                      [x[:, k, :] for x in w1]) for k in range(KC)]
                    + [(w["w2"].rearrange("(k p) n -> p k n", p=P)[:, 3 * k:3 * k + 3, :], P, 3 * D,
                        [x[:, 3 * k:3 * k + 3, :].rearrange("p k n -> p (k n)") for x in w2]) for k in range(FM // 3)])

        NCH = 2 * KC
        V_RING = 2
        vst = [xbo[:, :, :, :].rearrange("p x t d -> p (x t d)"), hf[:, :, :].rearrange("p r c -> p (r c)")]

        def load_a(sp, layer):
            for c, (ap, _) in enumerate(a_chunks(layer)):
                sp.dma_start(arrive[c], ap).then_inc(w_in, 16)

        def load_m(sp, layer, cs):
            for c in cs:
                ap, rows, cols, _ = m_chunks(layer)[c]
                if c >= V_RING:
                    sp.wait_ge(v_lo, layer * NCH + c - V_RING + 1)
                to = vst[c % V_RING][0:rows, 0:cols]
                if len(ap.shape) == 3:
                    to = to.rearrange("p (k n) -> p k n", k=ap.shape[1])
                sp.dma_start(to, ap).then_inc(v_in[c % V_RING], 16)

        def high_a(act, layer):
            act.wait_ge(w_in, 16 * NCH * (layer + 1))
            for c, (_, to) in enumerate(a_chunks(layer)):
                if c < KC and QK_EPS[layer] is not None:
                    act.wait_ge(w_mean, (layer // 2) * KC + c + 1)
                act.activation(to[0], arrive[c], ACT.Identity).then_inc(w_hi, 1)

        def high_m(act, layer, cs):
            for c in cs:
                _, rows, cols, to = m_chunks(layer)[c]
                act.wait_ge(v_in[c % V_RING], 16 * (layer * NCH // V_RING + c // V_RING + 1))
                act.activation(to[0], vst[c % V_RING][0:rows, 0:cols], ACT.Identity).then_inc(v_hi, 1)

        def low_m(pool, layer, cs):
            for c in cs:
                _, rows, cols, to = m_chunks(layer)[c]
                pool.wait_ge(v_hi, layer * NCH + c + 1)
                pool.tensor_tensor(to[1], vst[c % V_RING][0:rows, 0:cols], to[0].bitcast(F32), ALU.subtract).then_inc(v_lo, 1)
                pool.wait_ge(v_lo, layer * NCH + c + 1)

        w_steps = [0]

        def weight_step(dve, op):
            op.then_inc(w_step, 1)
            w_steps[0] += 1
            dve.wait_ge(w_step, w_steps[0])

        def center(dve, columns, rows):
            by_head = columns.rearrange("p (h d) -> p h d", d=HD)
            mean = sm[0:rows, 0:2 * H]
            weight_step(dve, dve.tensor_reduce(mean, by_head, AX.X, ALU.add))
            weight_step(dve, dve.tensor_scalar(mean, mean, -1.0 / HD, None, ALU.mult))
            weight_step(dve, dve.tensor_tensor(by_head, by_head, mean.unsqueeze(2).broadcast_to([rows, 2 * H, HD]), ALU.add))

        def low_a(dve, layer):
            dve.wait_ge(w_in, 16 * NCH * (layer + 1))
            if QK_EPS[layer] is not None:
                for c in range(KC):
                    center(dve, arrive[c][:, 0:2 * D], KP)
                    dve.sem_inc(w_mean, 1)
            for c, (_, to) in enumerate(a_chunks(layer)):
                dve.wait_ge(w_hi, layer * NCH + c + 1)
                dve.tensor_tensor(to[1], arrive[c], to[0].bitcast(F32), ALU.subtract).then_inc(w_lo, 1)

        def constant_wait(eng):
            eng.nop(nofuse=True)

        steps = [0]
        par = 0

        for layer in range(LAYERS):
            first, last = layer * B, layer * B + B
            src = t["x"] if layer == 0 else mid[layer - 1]
            dst = t["out"] if layer == LAYERS - 1 else mid[layer]
            start = first + 2
            rot = layer == LAYERS - 1
            eps = QK_EPS[layer]
            early = (0,) if eps is None else (0, 1)
            w = t[layer]

            def qk_run(n):
                return n - B if layer == 2 else n

            def wait_normed(eng, n):
                if eps is None:
                    wait(eng, "a_qkvd", n, 6)
                else:
                    wait(eng, "a_nrm", qk_run(n), 1)

            def slots(eng, slot):
                slot(None, None, first)
                slot(first, None, first + 1)
                slot(first + 1, first, first + 2)
                with eng.Fori(start, last - 1) as n:
                    slot(n, n - 1, n + 1)
                slot(last - 1, last - 2, None)
                slot(None, last - 1, None)

            parameter_loads = [(bqkv[:, :], w["bqkv"].partition_broadcast(P)), (bo[:, :], w["bo"].partition_broadcast(P)),
                               (b2[:, :], w["b2"].partition_broadcast(P)), (b1T[:, :], w["b1T"])]
            if eps is not None:
                parameter_loads += [(gam[:, 0:HD], w["gq"].partition_broadcast(P)), (gam[:, HD:2 * HD], w["gk"].partition_broadcast(P))]
            if rot:
                parameter_loads += [(bet[:, 0:HD], w["bq"].partition_broadcast(P)), (bet[:, HD:2 * HD], w["bk"].partition_broadcast(P))]
            par += len(parameter_loads)

            with ExitStack() as lc:
                block = lc.enter_context(nc.Block())

                @block.sync
                def _(sp):
                    def load_x(n):
                        wait(sp, "a_xn", n, 0)
                        wait(sp, "a_xa", n, 0)
                        sp.dma_start(xld[:, :, :], src[n - first].rearrange("(t p) d -> p t d", p=P)).then_inc(s["a_x"], 16)

                    def load_gA(n):
                        wait(sp, "a_x1", n, 0)
                        sp.dma_start(gA[:, :], gates[layer, n - first, 0:D].partition_broadcast(P)).then_inc(s["a_g"], 16)

                    def load_gM(n):
                        wait(sp, "m_x2", n, 0)
                        sp.dma_start(gM[:, :], gates[layer, n - first, D:2 * D].partition_broadcast(P)).then_inc(s["m_g"], 16)
                        if rot:
                            wait(sp, "r_y", n - first, 0)
                            sp.dma_start(eb[:, :], expm[n - first]).then_inc(s["r_e"], 16)

                    def store(n):
                        if rot:
                            wait(sp, "r_x3", n - first, 2)
                        else:
                            wait(sp, "m_x2", n, 2)
                        sp.dma_start(dst[n - first].rearrange("(t p) d -> p t d", p=P), xo[:, :, :]).then_inc(s["m_out"], 16)

                    def slot(a, m, p):
                        if a is None and m is not None and layer < LAYERS - 1:
                            wait(sp, "a_x1", last, 0)
                            load_a(sp, layer + 1)
                            wait(sp, "a_xn", last, 0)
                            wait(sp, "a_xa", last, 0)
                            sp.dma_start(xld[:, :, :], dst[0].rearrange("(t p) d -> p t d", p=P)).then_inc(s["a_x"], 16)
                        if a is not None:
                            load_gA(a)
                        if m is not None:
                            load_gM(m)
                        if p is not None and (a is not None or m is not None):
                            load_x(p)
                        if a is not None and m is None:
                            load_m(sp, layer, range(V_RING, NCH))
                        if m is not None:
                            store(m)

                    if layer == 0:
                        load_x(first)
                        load_a(sp, layer)
                    for to, ap in parameter_loads:
                        sp.dma_start(to, ap).then_inc(p_in, 16)
                    load_m(sp, layer, range(V_RING))
                    slots(sp, slot)
                    sp.wait_ge(s["m_out"], upto("m_out", last, 0))

                @block.gpsimd
                def _(pool):
                    def constants():
                        pool.memset(qs[:, :, :, :].bitcast(F32), 0.0).then_inc(set_done, 1)
                        pool.memset(ks[:, :, :, :].bitcast(F32), 0.0).then_inc(set_done, 1)
                        pool.memset(V[:, :, :, :], 0.0).then_inc(set_done, 1)
                        for a in range(2):
                            pool.memset(kz[a][:, :, :].bitcast(F32), 0.0).then_inc(set_done, 1)
                        pool.wait_ge(set_done, 5)
                        pool.memset(ks[:, :, :, 0:2].bitcast(F32), 1.0).then_inc(set_done, 1)
                        pool.memset(V[:, :, :, 0:1], 1.0).then_inc(set_done, 1)

                    def A_mod(n, layer, first):
                        wait(pool, "a_xf", n, 0)
                        pool.tensor_copy(amod[:, :], modT[:, layer, 0:6, bass.ds(n - first, 1)].rearrange("p c b -> p (c b)")).then_inc(s["a_mod"], 1)

                    def M_mod(n):
                        wait(pool, "m_xf", n, 0)
                        pool.tensor_copy(mmod[:, :], modT[:, layer, 6:12, bass.ds(n - first, 1)].rearrange("p c b -> p (c b)")).then_inc(s["m_mod"], 1)

                    def A_rstd(n):
                        wait(pool, "a_xn", n, 0)
                        wait(pool, "a_st", n, 1)
                        constant_wait(pool)
                        pool.tensor_scalar(veA[:, :], mvA[:, :, 1], 1.0, 1e-6, ALU.mult, ALU.add).then_inc(s["a_ve"], 1)
                        wait(pool, "a_ve", n, 1)
                        pool.tensor_tensor(rsA[:, :], veA[:, :], mhalf[:, :], ALU.pow).then_inc(s["a_rs"], 1)

                    def M_rstd(n):
                        wait(pool, "m_xn", n, 0)
                        wait(pool, "m_st", n, 1)
                        constant_wait(pool)
                        pool.tensor_scalar(veM[:, :], mvM[:, :, 1], 1.0, 1e-6, ALU.mult, ALU.add).then_inc(s["m_ve"], 1)
                        wait(pool, "m_ve", n, 1)
                        pool.tensor_tensor(rsM[:, :], veM[:, :], mhalf[:, :], ALU.pow).then_inc(s["m_rs"], 1)

                    def A_xh(n):
                        wait(pool, "a_qkv", n, 0)
                        wait(pool, "a_xf", n, 3)
                        constant_wait(pool)
                        pool.tensor_scalar(xh[:, :, :], xf, 1.0, 0.0, ALU.mult, ALU.add).then_inc(s["a_xh"], 1)

                    def M_xh(n):
                        wait(pool, "m_h", n, 0)
                        for c in range(KC):
                            wait(pool, "m_xf", n, c + 1)
                            constant_wait(pool)
                            pool.tensor_scalar(xh2[:, c, :], xf2[:, c, :], 1.0, 0.0, ALU.mult, ALU.add).then_inc(s["m_xh"], 1)

                    def A_residual(n):
                        wait(pool, "a_g", n, 16)
                        wait(pool, "a_x", n, 16)
                        wait(pool, "a_x1", n, 0)
                        pool.tensor_tensor(gbA[:, :], gA[:, :], bo[:, :], ALU.mult).then_inc(s["a_gb"], 1)
                        wait(pool, "a_gb", n, 1)
                        pool.tensor_tensor(xa[:, :, :], xld[:, :, :], gbA[:, :].unsqueeze(1).broadcast_to([P, NT, D]), ALU.add).then_inc(s["a_xa"], 1)

                    def M_residual(n):
                        wait(pool, "m_g", n, 16)
                        wait(pool, "m_x2", n, 0)
                        wait(pool, "a_x1", n, 2)
                        pool.tensor_tensor(gbM[:, :], gM[:, :], b2[:, :], ALU.mult).then_inc(s["m_gb"], 1)
                        wait(pool, "m_gb", n, 1)
                        pool.tensor_tensor(xb[:, :, :], x1[:, :, :], gbM[:, :].unsqueeze(1).broadcast_to([P, NT, D]), ALU.add).then_inc(s["m_xb"], 1)

                    def M_hh(n, f):
                        wait(pool, "m_y", n, 0)
                        wait(pool, "m_hf", n, f + 1)
                        m = min(2, FM - 2 * f)
                        constant_wait(pool)
                        pool.tensor_scalar(hh[:, 2 * f:2 * f + m, :].rearrange("p m c -> p (m c)"), hf[:, f % 2, 0:m * T],
                                           1.0, 0.0, ALU.mult, ALU.add).then_inc(s["m_hh"], 1)

                    def slot(a, m, p):
                        if m is not None:
                            M_mod(m)
                            M_rstd(m)
                        if a is not None:
                            if m is None:
                                pool.wait_ge(p_in, 16 * par)
                                pool.wait_ge(w_lo, NCH * (layer + 1))
                            A_residual(a)
                            if m is None:
                                wait(pool, "a_xa", a, 1)
                                low_m(pool, layer, range(NCH - 1))
                        if m is not None:
                            M_xh(m)
                            M_residual(m)
                        if p is not None and (a is not None or layer == 0):
                            A_mod(p, layer, first)
                        if m is not None:
                            for f in range(5):
                                M_hh(m, f)
                        if p is not None and (a is not None or layer == 0):
                            A_rstd(p)
                        if a is None and m is not None and layer < LAYERS - 1:
                            A_mod(last, layer + 1, last)
                            A_rstd(last)
                        if p is not None:
                            A_xh(p)
                            if a is None and layer == 0:
                                constants()
                        if a is not None and m is None:
                            wait(pool, "a_xh", p, 1)
                            low_m(pool, layer, (NCH - 1,))

                    slots(pool, slot)

                @block.scalar
                def _(act):
                    if layer == 0:
                        high_a(act, layer)
                    act.wait_ge(p_in, 16 * par)

                    def M_xf(n):
                        wait(act, "m_mod", n, 1)
                        wait(act, "m_hl", n, 0)
                        for c in range(KC):
                            if c != 1:
                                wait(act, "m_xT", n, c // 2 + 1)
                            act.activation(xf2[:, c, :], MBANK[c // 2][0:KP, (c % 2) * T:(c % 2 + 1) * T], ACT.Identity,
                                           bias=mmod[:, c:c + 1], scale=mmod[:, 3 + c:4 + c]).then_inc(s["m_xf"], 1)

                    def M_gelu(n, f):
                        wait(act, "m_h", n, f + 1)
                        if f == 0:
                            wait(act, "m_xl", n, 1)
                        if f >= 2:
                            wait(act, "m_hl", n, f - 1)
                        for i in range(min(2, FM - 2 * f)):
                            op = act.activation(hf[:, f % 2, i * T:(i + 1) * T], MBANK[f % 2][:, i * T:(i + 1) * T],
                                                ACT.Gelu if rot else ACT.Gelu_apprx_tanh, bias=b1T[:, 2 * f + i:2 * f + i + 1])
                        op.then_inc(s["m_hf"], 1)

                    def A_square(n):
                        wait(act, "a_qkvd", n, 4)
                        act.activation(sq, qk.rearrange("p t c -> p (t c)"), ACT.Square).then_inc(s["a_sq"], 1)

                    def A_hi(n):
                        wait(act, "a_T", n, 0)
                        wait_normed(act, n)
                        for i in range(NT):
                            kv = qk[:, i, D:2 * D].rearrange("p (h d) -> p h d", h=H)
                            op = act.activation(ks[:, i, :, 2:2 + HD], kv, ACT.Identity)
                        op.then_inc(s["a_kh"], 1)
                        wait(act, "a_T2", n, 0)
                        for i in range(NT):
                            qv = qk[:, i, 0:D].rearrange("p (h d) -> p h d", h=H)
                            op = act.activation(qs[:, i, :, 2 + HD:2 + 2 * HD], qv, ACT.Identity)
                        op.then_inc(s["a_qh"], 1)
                        for i in range(NT):
                            kv = qk[:, i, D:2 * D].rearrange("p (h d) -> p h d", h=H)
                            op = act.activation(ks[:, i, :, 2 + 2 * HD:2 + 3 * HD], kv, ACT.Identity)
                        op.then_inc(s["a_kh"], 1)

                    def A_turned(n, f):
                        if f == 0:
                            wait(act, "a_S", n, 0)
                            wait(act, "a_pr", n, 0)
                        wait(act, "a_T", n, 2 * f + 1)
                        act.activation(qT[:, 2 * f:2 * f + 2, :].rearrange("p m c -> p (m c)"), ABANK[0][:, :], ACT.Identity).then_inc(s["a_qT"], 1)
                        wait(act, "a_T", n, 2 * f + 2)
                        act.activation(kz[0][0:SLOT, 2 * f:2 * f + 2, :].rearrange("p m c -> p (m c)"), ABANK[1][0:SLOT, :],
                                       ACT.Identity).then_inc(s["a_kA"], 1)
                        act.activation(kz[1][SLOT:P, 2 * f:2 * f + 2, :].rearrange("p m c -> p (m c)"), ABANK[1][SLOT:P, :],
                                       ACT.Identity).then_inc(s["a_kB"], 1)

                    def A_turned2(n, f):
                        wait(act, "a_T2", n, f + 1)
                        act.activation(qT[:, 2 * f:2 * f + 2, :].rearrange("p m c -> p (m c)"), ABANK[f % 2][:, :], ACT.Identity).then_inc(s["a_q2a"], 1)

                    def load_table(n, i, function):
                        wait(act, "a_warm", n, i)
                        act.activation(warm[:, i:i + 1], mhalf[:, 0:1], function).then_inc(s["a_warm"], 1)

                    def A_exp(n, p):
                        if p >= 3:
                            wait(act, "a_pv", n, p - 2)
                        wait(act, "a_S", n, PAIRS + p + 1)
                        r = 2 * (p % 2)
                        act.activation(pT[:, p % 3, :, :], S[:, r:r + 2, :], ACT.Exp, scale=float(HD) ** -0.5).then_inc(s["a_ex"], 1)

                    def A_ohi(n):
                        wait(act, "a_nT", n, 1)
                        act.activation(oh[:, 0:2, :].rearrange("p m c -> p (m c)"), ABANK[0][0:KP, :], ACT.Identity).then_inc(s["a_oh"], 1)
                        wait(act, "a_nT", n, 2)
                        act.activation(oh[:, 2, :], ABANK[1][0:KP, 0:T], ACT.Identity).then_inc(s["a_oh"], 1)

                    def R_x(n):
                        b = n - first
                        wait(act, "r_T", b, 1)
                        act.activation(xf2[:, 0:2, :].rearrange("p m c -> p (m c)"), MBANK[1][0:KP, :], ACT.Identity).then_inc(s["r_x"], 1)
                        wait(act, "r_T", b, 2)
                        act.activation(xf2[:, 2, :], MBANK[0][0:KP, 0:T], ACT.Identity).then_inc(s["r_x"], 1)

                    def R_z(n):
                        wait(act, "r_z", n - first, 1)
                        act.activation(zT[:, :], MBANK[1][0:ROT, 0:T], ACT.Identity).then_inc(s["r_zs"], 1)

                    def R_y(n):
                        wait(act, "r_y", n - first, 1)
                        act.activation(yT[:, :], MBANK[0][0:ROT, 0:T], ACT.Identity).then_inc(s["r_ys"], 1)

                    def slot(a, m, p):
                        if a is not None and m is None:
                            high_m(act, layer, range(KC))
                        if a is not None and eps is not None:
                            A_square(a)
                        if a is not None and m is None:
                            high_m(act, layer, range(KC, NCH - 1))
                        if m is not None:
                            M_xf(m)
                        if a is None and m is not None and layer < LAYERS - 1:
                            wait(act, "a_pr", last, 0)
                            high_a(act, layer + 1)
                        if a is not None and eps is None:
                            A_hi(a)
                        late = a is not None and eps is None
                        if m is not None:
                            for f in range(2 if late else 5 if rot else 4):
                                M_gelu(m, f)
                        if a is not None and eps is not None:
                            A_hi(a)
                        if m is not None and not late and not rot:
                            M_gelu(m, 4)
                        if a is not None:
                            for f in range(4):
                                if m is not None and late and f in (1, 3):
                                    M_gelu(m, 2 + f // 2)
                                A_turned(a, f)
                            if m is not None and late:
                                M_gelu(m, 4)
                            load_table(a, 0, ACT.Exp)
                            A_turned2(a, 0)
                            A_turned2(a, 2)
                            for i in range(PAIRS):
                                A_exp(a, i)
                                if m is not None and rot:
                                    if i == 4:
                                        R_x(m)
                                    if i == 6:
                                        R_z(m)
                                    if i == 7:
                                        R_y(m)
                        elif rot and m is not None:
                            R_x(m)
                            R_z(m)
                            R_y(m)
                        if a is not None and m is None:
                            high_m(act, layer, (NCH - 1,))
                        if a is not None:
                            load_table(a, 1, ACT.Gelu if rot else ACT.Gelu_apprx_tanh)
                            A_ohi(a)

                    slots(act, slot)

                @block.vector
                def _(dve):
                    STEPS_P = 1
                    STEPS_A = 4 + (14 if eps is not None else 0) + (1 if rot else 0)
                    STEPS_M = 2
                    base = steps[0]
                    state = {}

                    def own(op):
                        op.then_inc(dve_step, 1)
                        state["k"] += 1
                        dve.wait_ge(dve_step, state["from"] + state["k"])

                    def parameters():
                        dve.wait_ge(p_in, 16 * par)
                        if eps is not None:
                            center(dve, bqkv[:, 0:2 * D], P)
                            if not rot:
                                weight_step(dve, dve.tensor_tensor(gam[:, 0:HD], gam[:, 0:HD], gam[:, HD:2 * HD], ALU.mult))

                    def A_stats(n):
                        wait(dve, "a_x", n, 16)
                        wait(dve, "a_rs", n, 0)
                        for i in range(NT):
                            op = dve.bn_stats(stA[:, i, :], xld[:, i, :])
                        own(op)
                        constant_wait(dve)
                        for i in range(NT):
                            op = dve.bn_aggr(mvA[:, i, :], stA[:, i, :])
                        op.then_inc(s["a_st"], 1)

                    def M_stats(n):
                        wait(dve, "m_bn", n, 2)
                        wait(dve, "m_rs", n, 0)
                        constant_wait(dve)
                        for i in range(NT):
                            op = dve.bn_aggr(mvM[:, i, :], stM[:, i, :])
                        op.then_inc(s["m_st"], 1)

                    def A_norm(n):
                        wait(dve, "a_st", n, 1)
                        wait(dve, "a_xT", n, 0)
                        wait(dve, "a_rs", n, 1)
                        for i in range(NT):
                            dve.tensor_scalar(xn[:, i, :], xld[:, i, :], mvA[:, i, 0:1], rsA[:, i:i + 1],
                                              ALU.subtract, ALU.mult).then_inc(s["a_xn"], 1)

                    def M_norm(n):
                        wait(dve, "m_st", n, 1)
                        wait(dve, "m_out", n, 0)
                        wait(dve, "m_rs", n, 1)
                        for i in range(NT):
                            dve.tensor_scalar(xo[:, i, :], x1[:, i, :], mvM[:, i, 0:1], rsM[:, i:i + 1],
                                              ALU.subtract, ALU.mult).then_inc(s["m_xn"], 1)

                    def A_xf(n, c):
                        if c == 0:
                            wait(dve, "a_mod", n, 1)
                            wait(dve, "a_oT", n - 1, 0)
                        if c != 1:
                            wait(dve, "a_xT", n, c // 2 + 1)
                        dve.tensor_scalar(xf[:, c, :], MBANK[1][0:KP, (c % 2) * T:(c % 2 + 1) * T], amod[:, 3 + c:4 + c],
                                          amod[:, c:c + 1], ALU.mult, ALU.add).then_inc(s["a_xf"], 1)

                    def A_xl(n):
                        wait(dve, "a_qkv", n, 0)
                        wait(dve, "a_xh", n, 1)
                        dve.tensor_tensor(xl[:, :, :], xf, xh[:, :, :].bitcast(F32), ALU.subtract).then_inc(s["a_xl"], 1)

                    def M_xl(n):
                        wait(dve, "m_h", n, 0)
                        wait(dve, "m_xh", n, 3)
                        dve.tensor_tensor(xl2[:, :, :], xf2, xh2[:, :, :].bitcast(F32), ALU.subtract).then_inc(s["m_xl"], 1)

                    def A_qkv(n, fills):
                        if fills[0] == 0:
                            wait(dve, "a_pv", n, 0)
                        for f in fills:
                            wait(dve, "a_qkv", n, f + 1)
                            i, part = (f // 2, f % 2) if f < 4 else (f - 4, 2)
                            to = qk[:, i, part * D:(part + 1) * D] if part < 2 else V[:, i, :, 1:1 + HD]
                            a, b = S[:, f % 4, 0:D], bqkv[:, part * D:(part + 1) * D]
                            if part == 2:
                                a, b = (z.rearrange("p (h d) -> p h d", h=H) for z in (a, b))
                            dve.tensor_tensor(to, a, b, ALU.add).then_inc(s["a_qkvd"], 1)

                    heads = qk.rearrange("p t c -> p (t c)").rearrange("p (g d) -> p g d", d=HD)

                    def A_heads_sum(n):
                        wait(dve, "a_sq", qk_run(n), 1)
                        own(dve.tensor_reduce(nv[:, :], sq.rearrange("p (g d) -> p g d", d=HD), AX.X, ALU.add))

                    def A_heads_rstd(n):
                        own(dve.tensor_scalar(nv[:, :], nv[:, :], 1.0 / HD, eps, ALU.mult, ALU.add))
                        own(dve.tensor_scalar(ny[:, :].bitcast(I32), nv[:, :].bitcast(I32), 1, None, ALU.logical_shift_right))
                        own(dve.tensor_scalar(ny[:, :].bitcast(I32), ny[:, :].bitcast(I32), -1.0, float(NEWTON_MAGIC), ALU.mult, ALU.add))
                        for _ in range(3):
                            own(dve.scalar_tensor_tensor(out=na[:, :], in0=ny[:, :], scalar=-0.5, in1=ny[:, :], op0=ALU.mult, op1=ALU.mult))
                            own(dve.tensor_tensor(na[:, :], na[:, :], nv[:, :], ALU.mult))
                            own(dve.scalar_tensor_tensor(out=ny[:, :], in0=na[:, :], scalar=1.5, in1=ny[:, :], op0=ALU.add, op1=ALU.mult))

                    def A_heads_norm(n, m):
                        own(dve.tensor_tensor(heads, heads, ny[:, :].unsqueeze(2).broadcast_to([P, 64, HD]), ALU.mult))
                        if m is not None:
                            M_hl(m, 1)
                        for table, op in ((gam, ALU.mult),) + (((bet, ALU.add),) if rot else ()):
                            parts = 2 if rot else 1
                            for j in range(NT):
                                part = qk[:, j, 0:parts * D].rearrange("p (x h d) -> p x h d", h=H, d=HD)
                                step = dve.tensor_tensor(part, part, table[:, 0:parts * HD].rearrange("p (x d) -> p x d", d=HD)
                                                         .unsqueeze(2).broadcast_to([P, parts, H, HD]), op)
                            if table is (bet if rot else gam):
                                step.then_inc(s["a_nrm"], 1)
                                wait(dve, "a_nrm", qk_run(n), 1)
                            else:
                                own(step)
                                if m is not None:
                                    M_hl(m, 2)

                    def A_halves(n):
                        wait(dve, "a_T2", n, 0)
                        wait(dve, "a_qkvd", n, 6)
                        dve.memset(qs[:, :, :, 0:2].bitcast(F32), 0.0)
                        for i in range(NT):
                            qv = qk[:, i, 0:D].rearrange("p (h d) -> p h d", h=H)
                            op = dve.tensor_copy(qs[:, i, :, 2:2 + HD], qv)
                        own(op)
                        for i in range(NT):
                            qv = qk[:, i, 0:D].rearrange("p (h d) -> p h d", h=H)
                            op = dve.tensor_tensor(qs[:, i, :, 2 + 2 * HD:2 + 3 * HD], qv, qs[:, i, :, 2:2 + HD].bitcast(F32), ALU.subtract)
                        op.then_inc(s["a_qs"], 1)
                        wait(dve, "a_kh", n, 1)
                        wait(dve, "a_T", n, 0)
                        for i in range(NT):
                            op = dve.tensor_tensor(
                                ks[:, i, :, 2 + HD:2 + 2 * HD], qk[:, i, D:2 * D].rearrange("p (h d) -> p h d", h=H),
                                ks[:, i, :, 2:2 + HD].bitcast(F32), ALU.subtract)
                        op.then_inc(s["a_kl"], 1)

                    def M_hl(n, f):
                        wait(dve, "m_hh", n, f + 1)
                        m = min(2, FM - 2 * f)
                        dve.tensor_tensor(hl[:, 2 * f:2 * f + m, :].rearrange("p m c -> p (m c)"), hf[:, f % 2, 0:m * T],
                                          hh[:, 2 * f:2 * f + m, :].rearrange("p m c -> p (m c)").bitcast(F32),
                                          ALU.subtract).then_inc(s["m_hl"], 1)

                    def A_max(n, p):
                        wait(dve, "a_S", n, p + 1)
                        if p == 0:
                            wait(dve, "a_nm", n, 0)
                        r = 2 * (p % 2)
                        dve.tensor_reduce(mx[:, p, :, :], S[:, r:r + 2, :].rearrange("p a (t k) -> p a t k", t=NT),
                                          AX.X, ALU.max).then_inc(s["a_mx"], 1)

                    def A_negmax(n):
                        wait(dve, "a_T", n, 8)
                        wait(dve, "a_mx", n, PAIRS)
                        own(dve.tensor_scalar(nmx[:, :, :, :], mx[:, :, :, :], -1.0, None, ALU.mult))
                        view = nmx[:, :, :, :].rearrange("p q a t -> p t (q a)")
                        own(dve.tensor_copy(qs[:, :, :, 0], view))
                        dve.tensor_tensor(qs[:, :, :, 1], view, qs[:, :, :, 0].bitcast(F32), ALU.subtract).then_inc(s["a_nm"], 1)

                    def A_turned2(n, f):
                        wait(dve, "a_T2", n, f + 1)
                        dve.tensor_copy(qT[:, 2 * f:2 * f + 2, :].rearrange("p m c -> p (m c)"), ABANK[f % 2][:, :]).then_inc(s["a_q2d"], 1)

                    def A_oraw(n, p, i):
                        if i == 0 and p is not None:
                            wait(dve, "a_xl", p, 1)
                        wait(dve, "a_pv", n, 4 * i + 4)
                        dve.tensor_copy(oraw[:, 2 * i:2 * i + 2, :].rearrange("p m c -> p (m c)"), ABANK[i][:, :]).then_inc(s["a_o"], 1)

                    def A_out(n):
                        for i in range(NT):
                            wait(dve, "a_oT", n, i + 1)
                            op = dve.reciprocal(rden[:, i, :], ABANK[i][:, :].rearrange("p (h d) -> p h d", h=H)[:, :, 0])
                        own(op)
                        for i in range(NT):
                            v = ABANK[i][:, :].rearrange("p (h d) -> p h d", h=H)
                            dve.tensor_tensor(on[:, i, :].rearrange("p (h d) -> p h d", h=H), v[:, :, 1:1 + HD],
                                              rden[:, i, :].unsqueeze(2).broadcast_to([P, H, HD]), ALU.mult).then_inc(s["a_on"], 1)

                    def A_olo(n):
                        wait(dve, "a_oh", n, 1)
                        dve.tensor_tensor(ol[:, 0:2, :].rearrange("p m c -> p (m c)"), ABANK[0][0:KP, :],
                                          oh[:, 0:2, :].rearrange("p m c -> p (m c)").bitcast(F32), ALU.subtract).then_inc(s["a_ol"], 1)
                        wait(dve, "a_oh", n, 2)
                        dve.tensor_tensor(ol[:, 2, :], ABANK[1][0:KP, 0:T], oh[:, 2, :].bitcast(F32), ALU.subtract).then_inc(s["a_ol"], 1)

                    def A_x1(n):
                        wait(dve, "a_xa", n, 1)
                        wait(dve, "m_xb", n, 0)
                        wait(dve, "m_xn", n, 0)
                        wait(dve, "m_st", n, 0)
                        for i in range(NT):
                            wait(dve, "a_pr", n, i + 1)
                            dve.tensor_tensor(x1[:, i, :], ABANK[i][:, 0:D], gA[:, :], ALU.mult).then_inc(s["a_prd"], 1)
                            wait(dve, "a_prd", n, i + 1)
                            dve.tensor_tensor(x1[:, i, :], x1[:, i, :], xa[:, i, :], ALU.add).then_inc(s["a_x1"], 1)
                            wait(dve, "a_x1", n, i + 1)
                            constant_wait(dve)
                            dve.bn_stats(stM[:, i, :], x1[:, i, :]).then_inc(s["m_bn"], 1)

                    def M_x2(n, i):
                        if i == 0:
                            wait(dve, "m_xb", n, 1)
                            wait(dve, "m_xT", n, 2)
                        wait(dve, "m_y", n, i + 1)
                        own(dve.tensor_tensor(xo[:, i, :], MBANK[1 - i][:, 0:D], gM[:, :], ALU.mult))
                        dve.tensor_tensor(xo[:, i, :], xo[:, i, :], xb[:, i, :], ALU.add).then_inc(s["m_x2"], 1)

                    def R_x3(n):
                        wait(dve, "m_x2", n, 2)
                        wait(dve, "r_T", n - first, 2)
                        for i in range(NT):
                            wait(dve, "r_o", n - first, i + 1)
                            dve.tensor_tensor(xo[:, i, :], MBANK[1 - i][:, 0:D], xo[:, i, :], ALU.add).then_inc(s["r_x3"], 1)

                    def slot(a, m, p):
                        if a is not None:
                            opened, run_a, run_m = a - first + 1, a - first, (a - first - 1 if m is not None else 0)
                        elif m is not None:
                            opened, run_a, run_m = B, B, B - 1
                        else:
                            opened, run_a, run_m = 0, 0, 0
                        state["from"] = base + opened * STEPS_P + run_a * STEPS_A + run_m * STEPS_M
                        if a is None and m is None and layer > 0:
                            state["from"] += STEPS_P
                        state["k"] = 0
                        if m is not None:
                            M_stats(m)
                        if a is not None:
                            if m is None and layer == 0:
                                dve.wait_ge(set_done, 7)
                            A_qkv(a, (1, 2) if eps is None else (2,))
                        if m is not None:
                            if isinstance(m, int) and m == first:
                                dve.wait_ge(v_lo, NCH * (layer + 1))
                            M_norm(m)
                        if a is not None:
                            A_qkv(a, (3, 4))
                            if eps is not None:
                                A_heads_sum(a)
                            A_qkv(a, (5,))
                        if m is not None:
                            M_xl(m)
                        if a is not None and eps is None:
                            A_halves(a)
                        if a is not None and eps is not None:
                            A_heads_rstd(a)
                        if a is None and m is not None and layer < LAYERS - 1:
                            wait(dve, "a_pr", last, 0)
                            low_a(dve, layer + 1)
                        if m is not None:
                            M_hl(m, 0)
                        if a is not None and eps is not None:
                            A_heads_norm(a, m)
                        if a is not None and eps is not None:
                            A_halves(a)
                        if m is not None:
                            for f in range(1 if a is None or eps is None else 3 if rot else 2,
                                           5 if a is None or eps is not None else 2):
                                M_hl(m, f)
                        if a is not None:
                            for i in range(PAIRS):
                                A_max(a, i)
                                if m is not None and eps is None and i in (0, 2, 4):
                                    M_hl(m, 2 + i // 2)
                            A_negmax(a)
                        if m is not None:
                            M_x2(m, 0)
                        if a is not None:
                            A_turned2(a, 1)
                        if p is not None and (a is not None or layer == 0):
                            A_stats(p)
                        if a is None and m is not None and layer < LAYERS - 1:
                            A_stats(last)
                            A_norm(last)
                        if a is not None:
                            A_turned2(a, 3)
                        if p is not None and (a is not None or layer == 0):
                            A_norm(p)
                        if a is None and m is None and layer == 0:
                            low_a(dve, layer)
                        if m is not None and rot:
                            M_x2(m, 1)
                        if p is not None:
                            A_xf(p, 0)
                            A_xf(p, 1)
                            A_xf(p, 2)
                            A_xl(p)
                        if a is not None:
                            A_oraw(a, p, 0)
                            A_oraw(a, p, 1)
                        if m is not None and rot:
                            R_x3(m)
                        if a is not None:
                            A_out(a)
                        if p is not None:
                            if a is None:
                                parameters()
                            A_qkv(p, (0,))
                        if a is not None:
                            A_olo(a)
                        if m is not None and not rot:
                            M_x2(m, 1)
                        if p is not None and eps is not None:
                            A_qkv(p, (1,))
                        if a is not None:
                            A_x1(a)
                        opens = (p is not None and (a is not None or layer == 0)) or (a is None and m is not None and layer < LAYERS - 1)
                        assert state["k"] == STEPS_P * opens + STEPS_A * (a is not None) + STEPS_M * (m is not None)

                    slots(dve, slot)
                    steps[0] = base + B * (STEPS_P + STEPS_A + STEPS_M)

                @block.tensor
                def _(pe):

                    def three(out, xs, ws, n_k, lhs, rhs):
                        terms = [(xs[0], ws[0]), (xs[0], ws[1]), (xs[1], ws[0])]
                        for j, (x, wt) in enumerate(terms):
                            for k in range(n_k):
                                op = pe.matmul(out, lhs(x, k), rhs(wt, k), start=(j == 0 and k == 0), stop=(j == 2 and k == n_k - 1))
                        return op

                    def turn3(x, banks, done, run):
                        for c in range(KC):
                            for i in range(NT):
                                op = pe.transpose(banks[c // 2][0:KP, (c % 2) * T + i * P:(c % 2) * T + (i + 1) * P],
                                                  x[:, i, c * KP:(c + 1) * KP], ident[:, :])
                            if c:
                                op.then_inc(s[done], 1)

                    def A_turn(n, m, part):
                        if part == 0:
                            wait(pe, "a_xn", n, 2)
                            if m is not None:
                                wait(pe, "m_x2", m, 1)
                        else:
                            wait(pe, "a_xf", n, 2)
                        for c in ((0, 1), (2,))[part]:
                            for i in range(NT):
                                op = pe.transpose(MBANK[1][0:KP, (c % 2) * T + i * P:(c % 2) * T + (i + 1) * P],
                                                  xn[:, i, c * KP:(c + 1) * KP], ident[:, :])
                        op.then_inc(s["a_xT"], 1)

                    def A_qkv(n, fills):
                        if fills[0] == 0:
                            wait(pe, "a_xl", n, 1)
                        for f in fills:
                            i, part = (f // 2, f % 2) if f < 4 else (f - 4, 2)
                            if f == 0:
                                wait(pe, "a_ex", n, -1)
                            elif f == 2:
                                wait(pe, "a_ex", n, 0)
                            elif f >= 4:
                                wait(pe, "a_qkvd", n, f - 3)
                            three(S[:, f % 4, 0:D], (xh, xl), wqkv, KC,
                                  lambda x, k: x[:, k, i * P:(i + 1) * P],
                                  lambda wt, k: wt[:, k, part * D:(part + 1) * D]).then_inc(s["a_qkv"], 1)

                    def A_turn_pairs(bank, x, f):
                        for p in range(2):
                            for i in range(NT):
                                op = pe.transpose(bank[:, p * T + i * P:p * T + (i + 1) * P],
                                                  x[:, i, 4 * f + 2 * p:4 * f + 2 * p + 2, :].rearrange("p h d -> p (h d)").bitcast(F32), ident[:, :])
                        return op

                    def A_turn_q(n, f):
                        if f == 0:
                            wait(pe, "a_prd", n, 0)
                            wait(pe, "a_qh", n, 1)
                            wait(pe, "a_qs", n, 1)
                        else:
                            wait(pe, "a_qT", n, f)
                        A_turn_pairs(ABANK[0], qs, f).then_inc(s["a_T"], 1)

                    def A_turn_k(n, f):
                        if f == 0:
                            wait(pe, "a_kh", n, 2)
                            wait(pe, "a_kl", n, 1)
                        else:
                            wait(pe, "a_kA", n, f)
                            wait(pe, "a_kB", n, f)
                        A_turn_pairs(ABANK[1], ks, f).then_inc(s["a_T"], 1)

                    def A_scores(n, p):
                        if p % 2 == 0:
                            wait(pe, "a_qT", n, p // 2 + 1)
                            wait(pe, "a_kA", n, p // 2 + 1)
                            wait(pe, "a_kB", n, p // 2 + 1)
                        if p < 2:
                            wait(pe, "a_qkvd", n, 6)
                        else:
                            wait(pe, "a_mx", n, p - 1)
                        for a in range(2):
                            for i in range(NT):
                                op = pe.matmul(S[:, 2 * (p % 2) + a, i * T:(i + 1) * T], qT[:, p, i * P:(i + 1) * P], kz[a][:, p, :],
                                               start=True, stop=True)
                        op.then_inc(s["a_S"], 1)

                    def A_turn_q2(n, f):
                        if f == 0:
                            wait(pe, "a_qT", n, 4)
                            wait(pe, "a_nm", n, 1)
                        if f == 1:
                            wait(pe, "a_kA", n, 4)
                            wait(pe, "a_kB", n, 4)
                        if f == 2:
                            wait(pe, "a_q2a", n, 1)
                        if f == 3:
                            wait(pe, "a_q2d", n, 1)
                        A_turn_pairs(ABANK[f % 2], qs, f).then_inc(s["a_T2"], 1)

                    def A_scoresT(n, p):
                        if p % 2 == 0:
                            wait(pe, "a_q2a" if p % 4 == 0 else "a_q2d", n, p // 4 + 1)
                        if p < 2:
                            wait(pe, "a_mx", n, PAIRS - 1 + p)
                        else:
                            wait(pe, "a_ex", n, p - 1)
                        for a in range(2):
                            for i in range(NT):
                                op = pe.matmul(S[:, 2 * (p % 2) + a, i * T:(i + 1) * T], kz[a][:, p, i * P:(i + 1) * P], qT[:, p, :],
                                               start=True, stop=True)
                        op.then_inc(s["a_S"], 1)

                    def A_pv(n, p):
                        if p == 0:
                            wait(pe, "a_q2a", n, 2)
                            wait(pe, "a_q2d", n, 2)
                        wait(pe, "a_ex", n, p + 1)
                        j = p // 2
                        for i in range(NT):
                            for a in range(2):
                                g = 2 * (p % 2) + a
                                op = pe.matmul(ABANK[j // 2][32 * g:32 * g + 32, (j % 2) * T:(j % 2 + 1) * T], V[:, i, 2 * p + a, :],
                                               pT[:, p % 3, a, i * T:(i + 1) * T], start=(i == 0), stop=(i == NT - 1),
                                               tile_position=(0, 32 * g))
                        op.then_inc(s["a_pv"], 1)

                    def A_turn_o(n):
                        for i in range(NT):
                            if i == 0:
                                wait(pe, "a_o", n, 2)
                            for j in range(4):
                                op = pe.transpose(ABANK[i][:, j * P:(j + 1) * P], oraw[:, j, i * P:(i + 1) * P], ident[:, :])
                            op.then_inc(s["a_oT"], 1)

                    def A_turn_n(n):
                        wait(pe, "a_on", n, 2)
                        turn3(on, ABANK, "a_nT", n)

                    def A_proj(n):
                        wait(pe, "a_ol", n, 2)
                        for i in range(NT):
                            three(ABANK[i][:, 0:D], (oh, ol), wo, KC, lambda x, k: x[:, k, i * P:(i + 1) * P],
                                  lambda wt, k: wt[:, k, :]).then_inc(s["a_pr"], 1)

                    def M_turn(n, a):
                        wait(pe, "a_xf", last if a is None else a + 1, 0)
                        if rot:
                            wait(pe, "r_x3", n - first, 0)
                            if isinstance(n, int) and n == first:
                                wait(pe, "m_x2", n, 0)
                        else:
                            wait(pe, "m_x2", n, 0)
                        wait(pe, "m_xn", n, 2)
                        turn3(xo, MBANK, "m_xT", n)

                    def M_up_part(n, m, terms):
                        f, i = divmod(m, 2)
                        for j in terms:
                            wt, x = ((w1[0], xh2), (w1[1], xh2), (w1[0], xl2))[j]
                            if m == 0 and j == 2:
                                wait(pe, "m_xl", n, 1)
                            for k in range(KC):
                                if m == 0 and j == 0:
                                    wait(pe, "m_xh", n, k + 1)
                                op = pe.matmul(MBANK[f % 2][:, i * T:(i + 1) * T], wt[:, k, m * P:(m + 1) * P], x[:, k, :],
                                               start=(j == 0 and k == 0), stop=(j == 2 and k == KC - 1))
                        if j == 2 and (i == 1 or m == FM - 1):
                            op.then_inc(s["m_h"], 1)

                    def M_up_first(n):
                        wait(pe, "m_xf", n, 2)
                        M_up_part(n, 0, (0, 1))
                        wait(pe, "m_xf", n, 3)
                        M_up_part(n, 2, (0, 1))
                        M_up_part(n, 0, (2,))
                        M_up_part(n, 1, (0, 1, 2))
                        M_up_part(n, 2, (2,))
                        M_up_part(n, 3, (0, 1, 2))

                    def M_up(n, f):
                        wait(pe, "m_hf", n, f - 1)
                        for m in range(2 * f, min(2 * f + 2, FM)):
                            M_up_part(n, m, (0, 1, 2))

                    DOWN = [(j, k) for ks_ in (range(6), range(6, FM)) for j in range(2) for k in ks_] + [(2, k) for k in range(FM)]

                    def M_down(n, i, lo, hi):
                        if lo == 0 and i == 0:
                            wait(pe, "m_hf", n, 4)
                        if lo == 0 and i == 1:
                            wait(pe, "m_hf", n, 5)
                        for z in range(lo, hi):
                            j, k = DOWN[z]
                            x, wt = ((hh, w2[0]), (hh, w2[1]), (hl, w2[0]))[j]
                            if i == 0 and j == 0 and k % 2 == 0:
                                wait(pe, "m_hh", n, k // 2 + 1)
                            if i == 0 and z == 2 * FM:
                                wait(pe, "m_hl", n, 5)
                            op = pe.matmul(MBANK[1 - i][:, 0:D], x[:, k, i * P:(i + 1) * P], wt[:, k, :],
                                           start=(z == 0), stop=(z == 3 * FM - 1))
                        if hi == 3 * FM:
                            op.then_inc(s["m_y"], 1)

                    def R_turn(n, p=None):
                        wait(pe, "m_x2", n, 2)
                        if p is not None:
                            wait(pe, "a_xf", p, 3)
                        turn3(xo, MBANK[::-1], "r_T", n)

                    def R_z(n):
                        wait(pe, "r_x", n - first, 2)
                        for k in range(KC):
                            op = pe.matmul(MBANK[1][0:ROT, 0:T], U[:, k, :], xf2[:, k, :], start=(k == 0), stop=(k == KC - 1))
                        op.then_inc(s["r_z"], 1)

                    def R_y(n):
                        wait(pe, "r_zs", n - first, 1)
                        wait(pe, "r_e", n - first, 16)
                        constant_wait(pe)
                        pe.matmul(MBANK[0][0:ROT, 0:T], eb[:, :], zT[:, :], start=True, stop=True).then_inc(s["r_y"], 1)

                    def R_out(n):
                        wait(pe, "r_ys", n - first, 1)
                        for i in range(NT):
                            pe.matmul(MBANK[1 - i][:, 0:D], yT[:, i * P:(i + 1) * P], UT[:, :], start=True, stop=True).then_inc(s["r_o"], 1)

                    def slot(a, m, p):
                        def down(i, lo, hi):
                            if m is not None and hi > lo:
                                M_down(m, i, lo, hi)

                        if a is not None:
                            A_qkv(a, (1, 2, 3, 4) if eps is None else (2, 3, 4))
                        if m is not None:
                            M_turn(m, a)
                            if isinstance(m, int) and m == first:
                                pe.wait_ge(v_lo, NCH * (layer + 1))
                        if a is not None:
                            A_qkv(a, (5,))
                        if m is not None:
                            M_up_first(m)
                            if a is None or eps is not None:
                                for f in range(2, 5):
                                    M_up(m, f)
                        if a is None:
                            down(0, 0, 27)
                            down(1, 0, 27)
                            if p is not None:
                                A_turn(p, m, 0)
                                A_turn(p, m, 1)
                                pe.wait_ge(w_lo, NCH * (layer + 1))
                                A_qkv(p, early)
                            if rot and m is not None:
                                R_turn(m)
                                R_z(m)
                                R_y(m)
                                R_out(m)
                            return
                        if eps is not None:
                            here = 18 if rot else 12
                            down(0, 0, here)
                            fills = [lambda f=f: down(0, here + (27 - here) * f // 5, here + (27 - here) * (f + 1) // 5) for f in range(5)]
                            if rot:
                                down(1, 0, 9)
                        elif m is not None:
                            fills = [lambda f=f: M_up(m, f) for f in range(2, 5)] + [lambda: down(0, 0, 12), lambda: down(0, 12, 27)]
                        else:
                            fills = [lambda: None] * 5
                        if m is None and layer == 0:
                            pe.wait_ge(set_done, 7)
                        A_turn_q(a, 0)
                        A_turn_k(a, 0)
                        if eps is None:
                            fills[0]()
                        A_turn_q(a, 1)
                        if eps is not None:
                            fills[0]()
                        A_turn_k(a, 1)
                        for f in range(4):
                            A_scores(a, 2 * f)
                            A_scores(a, 2 * f + 1)
                            if f < 2:
                                A_turn_q(a, f + 2)
                                A_turn_k(a, f + 2)
                            fills[f + 1]()
                        places = ((9, 12, 16, 16, 21, 24, 27), (0, 3, 7, 7, 12, 15, 27), (17, 20, 24, 27, 27, 27, 27))[layer]
                        down(1, 9 if rot else 0, places[0])
                        A_turn_q2(a, 0)
                        A_turn_q2(a, 1)
                        down(1, places[0], places[1])
                        A_turn_q2(a, 2)
                        A_turn_q2(a, 3)
                        A_scoresT(a, 0)
                        A_scoresT(a, 1)
                        down(1, places[1], places[2])
                        for i in range(2, PAIRS):
                            A_scoresT(a, i)
                            A_pv(a, i - 2)
                            if i == 2:
                                down(1, places[2], places[3])
                            if p is not None and i == 3:
                                A_turn(p, m, 0)
                            if p is not None and i == 4:
                                A_turn(p, m, 1)
                            if m is not None and rot:
                                if i == 5:
                                    R_turn(m, p)
                                if i == 6:
                                    R_z(m)
                                if i == 7:
                                    R_y(m)
                        A_pv(a, PAIRS - 2)
                        A_pv(a, PAIRS - 1)
                        down(1, places[3], places[4])
                        if rot and m is not None:
                            R_out(m)
                        A_turn_o(a)
                        if p is not None:
                            A_qkv(p, (0,))
                        down(1, places[4], places[5])
                        A_turn_n(a)
                        if p is not None and eps is not None:
                            A_qkv(p, (1,))
                        down(1, places[5], places[6])
                        A_proj(a)

                    slots(pe, slot)


def preamble(nc, t, sem, S, ABANK, MBANK, ident, modT, U, UT, mhalf, gates, expm):
    HB = B // 2
    with ExitStack() as ctx:
        def sb(name, shape, dt=F32):
            return ctx.enter_context(nc.sbuf_tensor(name, shape, dt))

        cT = sb("cT", [KP, KC, B])
        sT = sb("sT", [KP, KC, B])
        wmod = sb("wmod", [KP, 2, KC, 6 * D])
        bmodT = sb("bmodT", [KP, LAYERS, 12])
        bgate = sb("bgate", [B, LAYERS, 2 * D])
        grow = sb("grow", [B, 2 * D])
        WJ = 16
        wr = sb("wr", [KP, KC, 2, WJ, ROT])
        bfull = sb("bfull", [P, ROT])
        sign = sb("sign", [P, ROT])
        Bm = sb("Bm", [P, HB, ROT])
        Nm = sb("Nm", [P, HB, ROT])
        Em = sb("Em", [P, HB, ROT])
        Fm = sb("Fm", [P, HB, ROT])
        Bk = sb("Bk", [P, HB, ROT])
        Nk = sb("Nk", [P, HB, ROT])
        blockones = sb("blockones", [P, P])
        house_row = sb("house_row", [P, P])
        eye2 = sb("eye2", [P, ROT])
        after = sb("after", [P, ROT])
        mask = sb("mask", [P, ROT + D])
        house = sb("house", [P, 1])
        G = sb("G", [P, D])
        mk = sb("mk", [P, D])
        vs = sb("vs", [P, D])
        junk = sb("junk", [P, D])
        junk2 = sb("junk2", [P, D])
        dot = sb("dot", [P, 1])
        n2 = sb("n2", [P, 1])
        rt = sb("rt", [P, 1])
        sg = sb("sg", [P, ROT])
        q = [sb(f"q{i}", [P, 1]) for i in range(7)]

        load = sem("load")
        wm_in = [sem("wm_in0"), sem("wm_in1")]
        wr_in = [sem("wr_in0"), sem("wr_in1")]
        silu = sem("silu")
        const = sem("const")
        mod_mm = sem("mod_mm")
        mod_out = sem("mod_out")
        gate_out = sem("gate_out")
        a_mm = sem("a_mm")
        a_done = sem("a_done")
        e_mm = sem("e_mm")
        e_up = sem("e_up")
        e_k = sem("e_k")
        e_out = sem("e_out")
        g_mk = sem("g_mk")
        g_vb = sem("g_vb")
        g_n2 = sem("g_n2")
        g_rt = sem("g_rt")
        g_step = sem("g_step")
        u_mm = sem("u_mm")
        u_n2 = sem("u_n2")
        u_rt = sem("u_rt")

        CONSTS = 23
        Q_FIRST, Q_MOD, Q_A, Q_TAYLOR, Q_SQUARE = 2, 6, 4, (2, 2, 2, 2, 2), 2
        A_FROM = Q_FIRST + LAYERS * Q_MOD
        TAYLOR_FROM = A_FROM + ROT // 16 * Q_A
        SQUARE_FROM = TAYLOR_FROM + sum(Q_TAYLOR)
        assert len(Q_TAYLOR) == TAYLOR - 1 and SQUARE_FROM + SQUARINGS * Q_SQUARE == ROT

        def steps_between(start, count):
            return range(start, start + count)

        GS = 12
        A4 = [S[:, i, :] for i in range(4)]
        NJ = ROT // WJ

        block = ctx.enter_context(nc.Block())

        @block.sync
        def _(sp):
            for to, ap in ((cT[:, :, :], t["cT"]), (bmodT[:, :, :], t["bmodT"]), (bfull[0:ROT, :], t["bfull"]),
                           (bfull[ROT:P, :], t["bfull"]), (G[0:ROT, :], t["PT"]), (G[ROT:P, :], t["PT"])):
                sp.dma_start(to, ap).then_inc(load, 16)
            for i in range(LAYERS):
                sp.dma_start(bgate[:, i, :], t["bgate"][i].partition_broadcast(B)).then_inc(load, 16)
            for i in range(LAYERS):
                if i >= 2:
                    sp.wait_ge(mod_mm, 2 * (i - 1))
                sp.dma_start(wmod[:, i % 2, :, :], t[i]["wmod"].rearrange("(k p) n -> p k n", p=KP)).then_inc(wm_in[i % 2], 16)
            for c in range(NJ):
                if c >= 2:
                    sp.wait_ge(a_mm, c - 1)
                sp.dma_start(wr[:, :, c % 2, :, :], t["wrot"].rearrange("(k p) j i -> p k j i", p=KP)[:, :, c * WJ:(c + 1) * WJ, :]).then_inc(wr_in[c % 2], 16)
            sp.wait_ge(e_up, 2 * (TAYLOR + SQUARINGS))
            for h in range(2):
                sp.dma_start(expm[h * HB:(h + 1) * HB].rearrange("b d e -> d b e"), Em[h * ROT:(h + 1) * ROT, :, :]).then_inc(e_out, 16)
            sp.wait_ge(gate_out, 16 * LAYERS)
            sp.wait_ge(e_out, 32)

        @block.gpsimd
        def _(pool):
            made = [0]

            def own(op):
                op.then_inc(const, 1)
                made[0] += 1
                pool.wait_ge(const, made[0])

            def keep(tile, rows, op, value, step=1, tilestep=-1):
                view = tile[rows[0]:rows[1], :]
                own(pool.affine_select(out=view, in_=view, compare_op=op, fill=value, base=0,
                                       pattern=[[tilestep, view.shape[1]]], channel_multiplier=step))

            for tile, value in ((ident, 0.0), (blockones, 0.0), (house_row, 0.0), (eye2, 0.0), (after, -1.0), (mask, 1.0),
                                (mhalf, -0.5), (house, 0.0), (sign, 1.0)):
                own(pool.memset(tile[:, :], value))
            keep(ident, (0, P), ALU.not_equal, 1.0)
            own(pool.memset(blockones[0:ROT, 0:ROT], 1.0))
            own(pool.memset(blockones[ROT:P, ROT:P], 1.0))
            own(pool.memset(house_row[ROT:ROT + 1, :], 1.0))
            own(pool.memset(mask[ROT:P, 0:ROT], 0.0))
            own(pool.memset(house[ROT:P, :], 1.0))
            for rows in ((0, ROT), (ROT, P)):
                keep(eye2, rows, ALU.not_equal, 1.0)
                keep(after, rows, ALU.is_gt, 0.0)
                keep(sign, rows, ALU.is_gt, -1.0, step=-1, tilestep=1)
                keep(sign, rows, ALU.not_equal, 0.0)
            assert made[0] == CONSTS
            with pool.Fori(0, ROT) as j:
                pool.wait_ge(g_n2, j + 1)
                pool.tensor_tensor(rt[:, :], n2[:, :], mhalf[:, 0:1], ALU.pow).then_inc(g_rt, 1)
            pool.wait_ge(u_n2, 1)
            pool.tensor_tensor(rt[:, :], n2[:, :], mhalf[:, 0:1], ALU.pow).then_inc(u_rt, 1)

        @block.scalar
        def _(act):
            act.wait_ge(load, 16 * 9)
            act.activation(sT[:, :, :], cT[:, :, :], ACT.Silu).then_inc(silu, 1)

            def length2(j):
                act.wait_ge(g_step, j * GS + 2)
                act.activation(junk2[:, :], vs[:, :], ACT.Square, accum_out=n2[:, :]).then_inc(g_n2, 1)

            for j in steps_between(0, Q_FIRST):
                length2(j)
            for i in range(LAYERS):
                for j in steps_between(Q_FIRST + i * Q_MOD, Q_MOD):
                    length2(j)
                act.wait_ge(mod_out, 3 * i + 3)
                act.dma_start(gates[i], grow[:, :]).then_inc(gate_out, 16)
            for j in steps_between(A_FROM, NJ * Q_A):
                length2(j)
            for k in range(TAYLOR, 0, -1):
                i = TAYLOR - k
                if i == 0:
                    act.wait_ge(a_done, 3 * NJ)
                else:
                    act.wait_ge(e_up, 2 * i)
                act.mul(Bk[:, :, :], Bm[:, :, :], 1.0 / k).then_inc(e_k, 1)
                act.mul(Nk[:, :, :], Bm[:, :, :], -1.0 / k).then_inc(e_k, 1)
                if i < len(Q_TAYLOR):
                    for j in steps_between(TAYLOR_FROM + sum(Q_TAYLOR[:i]), Q_TAYLOR[i]):
                        length2(j)
            with act.Fori(0, SQUARINGS * Q_SQUARE) as j:
                length2(j + SQUARE_FROM)
            act.wait_ge(g_step, GS * ROT)
            act.activation(junk2[:, :], G[:, :], ACT.Square, accum_out=n2[:, :]).then_inc(u_n2, 1)

        @block.vector
        def _(dve):
            dve.wait_ge(const, CONSTS)
            dve.wait_ge(load, 16 * 9)

            vb = MBANK[1]

            def basis_step(j):
                count = [0]

                def own(op):
                    op.then_inc(g_step, 1)
                    count[0] += 1
                    dve.wait_ge(g_step, j * GS + count[0])

                def col(tile):
                    return tile[:, bass.ds(j, 1)]

                own(dve.scalar_tensor_tensor(out=mk[:, :], in0=G[:, :], scalar=col(eye2), in1=mask[:, bass.ds(ROT - j, D)],
                                             op0=ALU.mult, op1=ALU.mult))
                dve.wait_ge(g_vb, j + 1)
                own(dve.tensor_copy(vs[:, :], vb[:, 0:D]))
                own(dve.scalar_tensor_tensor(out=junk[:, :], in0=vs[:, :], scalar=1.0, in1=G[:, :],
                                             op0=ALU.mult, op1=ALU.mult, accum_out=dot[:, :]))
                own(dve.tensor_scalar(q[1][:, :], col(vs), 0.0, 2.0, ALU.is_ge, ALU.mult))
                own(dve.tensor_scalar(col(sg), q[1][:, :], -1.0, house[:, :], ALU.add, ALU.mult))
                dve.wait_ge(g_rt, j + 1)
                own(dve.scalar_tensor_tensor(out=q[2][:, :], in0=n2[:, :], scalar=rt[:, :], in1=col(sg), op0=ALU.mult, op1=ALU.mult))
                own(dve.scalar_tensor_tensor(out=q[3][:, :], in0=col(vs), scalar=q[2][:, :], in1=n2[:, :], op0=ALU.mult, op1=ALU.add))
                own(dve.reciprocal(q[4][:, :], q[3][:, :]))
                own(dve.scalar_tensor_tensor(out=q[5][:, :], in0=col(G), scalar=q[2][:, :], in1=dot[:, :], op0=ALU.mult, op1=ALU.add))
                own(dve.tensor_scalar(q[6][:, :], q[5][:, :], q[4][:, :], col(after), ALU.mult, ALU.mult))
                own(dve.tensor_tensor(col(vs), col(vs), q[2][:, :], ALU.add))
                own(dve.scalar_tensor_tensor(out=G[:, :], in0=vs[:, :], scalar=q[6][:, :], in1=G[:, :], op0=ALU.mult, op1=ALU.add))
                assert count[0] == GS

            for j in steps_between(0, Q_FIRST):
                basis_step(j)
            for i in range(LAYERS):
                for j in steps_between(Q_FIRST + i * Q_MOD, Q_MOD):
                    basis_step(j)
                dve.wait_ge(mod_mm, 2 * i + 1)
                v = modT[:, i, :, :]
                dve.tensor_tensor(v, MBANK[0][0:KP, 0:12 * B].rearrange("p (c b) -> p c b", b=B),
                                  bmodT[:, i, :].unsqueeze(2).broadcast_to([KP, 12, B]), ALU.add).then_inc(mod_out, 1)
                dve.wait_ge(mod_out, 3 * i + 1)
                for c in (3, 9):
                    op = dve.tensor_scalar(v[:, c:c + 3, :], v[:, c:c + 3, :], 1.0, None, ALU.add)
                op.then_inc(mod_out, 1)
                dve.wait_ge(mod_mm, 2 * i + 2)
                if i:
                    dve.wait_ge(gate_out, 16 * i)
                for g in range(2):
                    op = dve.tensor_tensor(grow[:, g * D:(g + 1) * D], ABANK[g][0:B, 0:D], bgate[:, i, g * D:(g + 1) * D], ALU.add)
                op.then_inc(mod_out, 1)
            for c in range(NJ):
                for j in steps_between(A_FROM + c * Q_A, Q_A):
                    basis_step(j)
                dve.wait_ge(a_mm, c + 1)
                for h in range(2):
                    to = Bm[h * ROT:(h + 1) * ROT, :, c * WJ:(c + 1) * WJ]
                    at = A4[c % 4][h * ROT:(h + 1) * ROT, :].rearrange("p (j b) -> p b j", b=B)[:, h * HB:(h + 1) * HB, :]
                    op = dve.tensor_tensor(to, at, bfull[h * ROT:(h + 1) * ROT, c * WJ:(c + 1) * WJ].unsqueeze(1).broadcast_to([ROT, HB, WJ]), ALU.add)
                op.then_inc(a_done, 1)
                dve.wait_ge(a_done, 3 * c + 1)
                part = Bm[:, :, c * WJ:(c + 1) * WJ]
                dve.tensor_tensor(part, part, sign[:, c * WJ:(c + 1) * WJ].unsqueeze(1).broadcast_to([P, HB, WJ]), ALU.mult).then_inc(a_done, 1)
                dve.wait_ge(a_done, 3 * c + 2)
                dve.tensor_scalar(part, part, 2.0 ** -SQUARINGS, None, ALU.mult).then_inc(a_done, 1)
            dve.wait_ge(a_done, 3 * NJ)
            dve.tensor_scalar(Nm[:, :, :], Bm[:, :, :], -1.0, None, ALU.mult).then_inc(a_done, 1)
            dve.wait_ge(e_k, 2)
            dve.tensor_copy(Em[:, :, :], Bk[:, :, :]).then_inc(e_up, 1)
            dve.tensor_copy(Fm[:, :, :], Nk[:, :, :]).then_inc(e_up, 1)
            S2 = S[:, :, :].rearrange("p (x y) c -> p x (y c)", x=2)

            def flat(x):
                return x[:, :, :].rearrange("p b e -> p (b e)")

            for k in range(TAYLOR - 1, 0, -1):
                i = TAYLOR - k
                for j in steps_between(TAYLOR_FROM + sum(Q_TAYLOR[:i - 1]), Q_TAYLOR[i - 1]):
                    basis_step(j)
                dve.wait_ge(e_k, 2 * i + 2)
                dve.wait_ge(e_mm, i)
                for x, part, m in ((Em, 0, Bk), (Fm, 1, Nk)):
                    dve.scalar_tensor_tensor(out=flat(x), in0=S2[:, part, :], scalar=1.0 / k, in1=flat(m),
                                             op0=ALU.mult, op1=ALU.add).then_inc(e_up, 1)
            with dve.Fori(0, SQUARINGS) as i:
                for j in range(Q_SQUARE):
                    basis_step(i * Q_SQUARE + (SQUARE_FROM + j))
                dve.wait_ge(e_mm, i + TAYLOR)
                dve.wait_ge(e_up, 2 * i + 2 * TAYLOR)
                for x, part in ((Em, 0), (Fm, 1)):
                    dve.scalar_tensor_tensor(out=flat(x), in0=flat(x), scalar=2.0, in1=S2[:, part, :],
                                             op0=ALU.mult, op1=ALU.add).then_inc(e_up, 1)

            dve.wait_ge(u_mm, 1)
            end = GS * ROT
            dve.tensor_tensor(junk[0:ROT, 0:ROT], ABANK[1][0:ROT, 0:ROT], eye2[0:ROT, :], ALU.mult).then_inc(g_step, 1)
            dve.wait_ge(g_step, end + 1)
            dve.tensor_reduce(dot[0:ROT, :], junk[0:ROT, 0:ROT], AX.X, ALU.add).then_inc(g_step, 1)
            dve.wait_ge(u_rt, 1)
            dve.wait_ge(g_step, end + 2)
            dve.scalar_tensor_tensor(out=q[0][0:ROT, :], in0=dot[0:ROT, :], scalar=-1.0, in1=rt[0:ROT, :], op0=ALU.mult, op1=ALU.mult).then_inc(g_step, 1)
            dve.wait_ge(g_step, end + 3)
            dve.tensor_scalar(UT[:, :], G[0:ROT, :], q[0][0:ROT, :], None, ALU.mult).then_inc(g_step, 1)
            dve.wait_ge(u_mm, 2)
            dve.tensor_copy(U[:, :, :], ABANK[0][0:KP, 0:KC * ROT].rearrange("p (k e) -> p k e", k=KC)).then_inc(g_step, 1)

        @block.tensor
        def _(pe):
            def spread(j):
                pe.wait_ge(g_step, j * GS + 1)
                pe.matmul(MBANK[1][:, 0:D], blockones[:, :], mk[:, :], start=True, stop=True).then_inc(g_vb, 1)

            pe.wait_ge(silu, 1)
            for j in steps_between(0, Q_FIRST):
                spread(j)
            for i in range(LAYERS):
                pe.wait_ge(wm_in[i % 2], 16 * (i // 2 + 1))
                if i:
                    pe.wait_ge(mod_out, 3 * i)
                for c, part in enumerate((0, 1, 3, 4)):
                    spread(Q_FIRST + i * Q_MOD + c)
                    for e in range(KC):
                        for k in range(KC):
                            op = pe.matmul(MBANK[0][0:KP, (3 * c + e) * B:(3 * c + e + 1) * B],
                                           wmod[:, i % 2, k, part * D + e * KP:part * D + (e + 1) * KP], sT[:, k, :],
                                           start=(k == 0), stop=(k == KC - 1))
                op.then_inc(mod_mm, 1)
                for g, part in enumerate((2, 5)):
                    spread(Q_FIRST + i * Q_MOD + 4 + g)
                    for k in range(KC):
                        op = pe.matmul(ABANK[g][0:B, 0:D], sT[:, k, :], wmod[:, i % 2, k, part * D:(part + 1) * D], start=(k == 0), stop=(k == KC - 1))
                op.then_inc(mod_mm, 1)
            for c in range(NJ):
                pe.wait_ge(wr_in[c % 2], 16 * (c // 2 + 1))
                for j in range(WJ):
                    if j % (WJ // Q_A) == 0:
                        spread(A_FROM + c * Q_A + j // (WJ // Q_A))
                    for h in range(2):
                        for k in range(KC):
                            op = pe.matmul(A4[c % 4][h * ROT:(h + 1) * ROT, j * B:(j + 1) * B], wr[:, k, c % 2, j, :], sT[:, k, :],
                                           start=(k == 0), stop=(k == KC - 1))
                op.then_inc(a_mm, 1)
            pe.wait_ge(a_done, 3 * NJ + 1)

            def products(left_e, left_f, columns):
                work = [(x, part, lhs, b) for x, part, lhs in ((Em, 0, left_e), (Fm, 2, left_f)) for b in range(HB)]
                for at, (x, part, lhs, b) in enumerate(work):
                    for c, j in enumerate(columns):
                        if at == 3 + c * len(work) // len(columns):
                            spread(j)
                    for h in range(2):
                        rows = slice(h * ROT, (h + 1) * ROT)
                        bank = part + b * ROT // 512
                        to = b * ROT % 512
                        op = pe.matmul(S[rows, bank, to:to + ROT], lhs[rows, b, :], x[rows, b, :], start=True, stop=True)
                return op

            for k in range(TAYLOR - 1, 0, -1):
                i = TAYLOR - k
                pe.wait_ge(e_up, 2 * i)
                products(Nm, Bm, steps_between(TAYLOR_FROM + sum(Q_TAYLOR[:i - 1]), Q_TAYLOR[i - 1])).then_inc(e_mm, 1)
            with pe.Fori(0, SQUARINGS) as i:
                pe.wait_ge(e_up, 2 * i + 2 * TAYLOR)
                pe.nop(nofuse=True)
                products(Fm, Em, [i * Q_SQUARE + (SQUARE_FROM + j) for j in range(Q_SQUARE)]).then_inc(e_mm, 1)
            pe.wait_ge(g_step, GS * ROT)
            pe.matmul(ABANK[1][:, 0:ROT], house_row[:, :], sg[:, :], start=True, stop=True).then_inc(u_mm, 1)
            pe.wait_ge(g_step, GS * ROT + 4)
            for k in range(KC):
                op = pe.transpose(ABANK[0][0:KP, k * ROT:(k + 1) * ROT], UT[:, k * KP:(k + 1) * KP], ident[0:ROT, 0:ROT])
            op.then_inc(u_mm, 1)


_LAYER = [
    dict(wmod="w_mod", bmod="b_mod", wqkv="w_qkv", bqkv="b_qkv", gq="g_q", gk="g_k", wo="w_proj", bo="b_proj", w1="w1", b1="b1", w2="w2", b2="b2"),
    dict(wmod="ada_w", bmod="ada_b", wqkv="qkv_w", bqkv="qkv_b", wo="out_w", bo="out_b", w1="w1", b1="b1", w2="w2", b2="b2"),
    dict(wmod="w_ada", bmod="b_ada", wqkv="w_qkv", bqkv="b_qkv", gq="qn_g", bq="qn_b", gk="kn_g", bk="kn_b", wo="w_proj", bo="b_proj", w1="w1", b1="b1", w2="w2", b2="b2"),
]


def kernel(**inputs):
    import concourse.bacc as _bacc
    from concourse.bass_utils import run_bass_kernel_spmd as _run

    nc = _bacc.Bacc("TRN2", target_bir_lowering=False, num_devices=1)
    arrays = {}

    def give(name, a):
        a = np.ascontiguousarray(a)
        name = f"in_{name}_dram"
        arrays[name] = a
        return nc.dram_tensor(name, a.shape, mybir.dt.from_np(a.dtype), kind="ExternalInput").ap()

    t = {"x": give("x", inputs["x"])}
    c = np.asarray(inputs["cond_1152"])
    t["cT"] = give("cT", c.T.reshape(KC, KP, B).transpose(1, 0, 2))
    bm, bg = [], []
    for i, names in enumerate(_LAYER):
        p = f"L{i}_cond_"
        t[i] = {}
        for k, name in names.items():
            a = np.asarray(inputs[p + name])
            if k == "b1":
                t[i]["b1T"] = give(f"L{i}_b1T", a.reshape(FM, P).T)
            elif k == "bmod":
                parts = a.reshape(6, KC, KP)
                bm.append(parts[[0, 1, 3, 4]].reshape(12, KP).T)
                bg.append(parts[[2, 5]].reshape(2 * D))
            else:
                t[i][k] = give(f"L{i}_{k}", a)
    t["bmodT"] = give("bmodT", np.stack(bm, 1))
    t["bgate"] = give("bgate", np.stack(bg))
    t["PT"] = give("PT", np.asarray(inputs["L3_cond_P"]).T)
    iu, ju = np.triu_indices(ROT, k=1)
    at = np.zeros((ROT, ROT), np.int64)
    at[iu, ju] = at[ju, iu] = np.arange(iu.size)
    W = np.asarray(inputs["L3_cond_W"])
    t["wrot"] = give("wrot", W[at.T.ravel()].reshape(ROT, ROT, D).transpose(2, 0, 1))
    t["bfull"] = give("bfull", np.asarray(inputs["L3_cond_b"])[at])
    t["out"] = nc.dram_tensor("out_0_dram", (B, T, D), F32, kind="ExternalOutput").ap()
    build(nc, t)
    r = _run(nc, [arrays], core_ids=[0])
    return r.results[0]["out_0_dram"]
```
